# Optimizing a Trainium2 kernel written in Bass

```python
import numpy as np
import jax
import jax.numpy as jnp

def _softmax(x, axis=-1):
    return jax.nn.softmax(x, axis=axis)

def _gelu(x):
    return jax.nn.gelu(x, approximate=True)

def _silu(x):
    return jax.nn.silu(x)

def _sigmoid(x):
    return jax.nn.sigmoid(x)

def _layernorm(x, axis=-1, eps=1e-05):
    m = jnp.mean(x, axis=axis, keepdims=True)
    v = jnp.var(x, axis=axis, keepdims=True)
    return (x - m) / jnp.sqrt(v + eps)

def _scatter_add(tgt, idx, src, axis=0):
    return tgt.at[idx].add(src)

def _segment_sum(src, seg, n):
    return jax.ops.segment_sum(src, seg, n)
kernel_name = 'mk_gnn_ffn_d1_gnn_r8_6e23d5'

def setup_inputs(seed: int=0):
    np.random.seed(seed)
    _w = jnp.asarray

    def _rec_inputs():
        import jax
        import jax.numpy as jnp
        _gk = jax.random.key(seed)
        x = -0.0002117 + 1 * jax.random.normal(jax.random.fold_in(_gk, 1), (6250, 256), jnp.float32)
        src = jax.random.randint(jax.random.fold_in(_gk, 2), (100000,), 0, 6250, jnp.int32)
        dst = jnp.minimum((6250 * jax.random.uniform(jax.random.fold_in(_gk, 3), (100000,)) ** 2.0).astype(jnp.int32), 49999)
        _o = jnp.argsort(dst, stable=True)
        src = src[_o]
        dst = dst[_o]
        edge_attr_256 = -6.47781e-05 + 0.999943 * jax.random.normal(jax.random.fold_in(_gk, 11), (100000, 256), jnp.float32)
        return (x, src, dst, edge_attr_256)
    x, src, dst, edge_attr_256 = _rec_inputs()

    def _L0_gnn_setup():
        import jax, jax.numpy as jnp
        import numpy as np
        N_VERTEX = 12500
        N_EDGE = 100000
        HIDDEN = 256
        key = jax.random.key(seed)
        ks = jax.random.split(key, 10)
        d = HIDDEN
        vertex_features = jax.random.normal(ks[0], (N_VERTEX, d), dtype=jnp.float32)
        edge_features = jax.random.normal(ks[1], (N_EDGE, d), dtype=jnp.float32)
        edge_index = jax.random.randint(ks[2], (2, N_EDGE), 0, N_VERTEX, dtype=jnp.int64)

        def lin(k, fan_in, fan_out):
            lim = 1.0 / np.sqrt(fan_in)
            kw, kb = jax.random.split(k)
            W = jax.random.uniform(kw, (fan_in, fan_out), minval=-lim, maxval=lim, dtype=jnp.float32)
            b = jax.random.uniform(kb, (fan_out,), minval=-lim, maxval=lim, dtype=jnp.float32)
            return (W, b)
        W1, b1 = lin(ks[3], 2 * d, d)
        W2, b2 = lin(ks[4], d, d)
        W3, b3 = lin(ks[5], d, d)
        return {'vertex_features': vertex_features, 'edge_features': edge_features, 'edge_index': edge_index, 'W1': W1, 'b1': b1, 'W2': W2, 'b2': b2, 'W3': W3, 'b3': b3}
    _L0_gnn_all = _L0_gnn_setup()
    _L0_gnn_in = {k: v for k, v in _L0_gnn_all.items() if k in ('W1', 'b1', 'W2', 'b2', 'W3', 'b3')}
    del _L0_gnn_all

    def _L0_ffn_setup():
        import jax, jax.numpy as jnp
        import numpy as np
        DIM = 256
        H = 8
        D = 64
        G = 64
        INNER = H * D
        SCALE = D ** (-0.5)
        key = jax.random.key(seed)
        ks = jax.random.split(key, 12)
        B, N = (4, 2048)
        x = jax.random.normal(ks[0], (B, N, DIM), dtype=jnp.float32)
        s = lambda fan_in: 1.0 / np.sqrt(fan_in)
        W_fx = jax.random.normal(ks[1], (DIM, INNER), dtype=jnp.float32) * s(DIM)
        b_fx = jnp.zeros((INNER,), dtype=jnp.float32)
        W_x = jax.random.normal(ks[2], (DIM, INNER), dtype=jnp.float32) * s(DIM)
        b_x = jnp.zeros((INNER,), dtype=jnp.float32)
        A = jax.random.normal(ks[3], (G, D), dtype=jnp.float32)
        Q, _ = jnp.linalg.qr(A.T)
        W_slice = Q[:, :G].astype(jnp.float32)
        b_slice = jnp.zeros((G,), dtype=jnp.float32)
        W_q = jax.random.normal(ks[4], (D, D), dtype=jnp.float32) * s(D)
        W_k = jax.random.normal(ks[5], (D, D), dtype=jnp.float32) * s(D)
        W_v = jax.random.normal(ks[6], (D, D), dtype=jnp.float32) * s(D)
        W_out = jax.random.normal(ks[7], (INNER, DIM), dtype=jnp.float32) * s(INNER)
        b_out = jnp.zeros((DIM,), dtype=jnp.float32)
        temperature = jnp.ones((1, H, 1, 1), dtype=jnp.float32) * 0.5
        return {'x': x, 'W_fx': W_fx, 'b_fx': b_fx, 'W_x': W_x, 'b_x': b_x, 'W_slice': W_slice, 'b_slice': b_slice, 'W_q': W_q, 'W_k': W_k, 'W_v': W_v, 'W_out': W_out, 'b_out': b_out, 'temperature': temperature}
    _L0_ffn_all = _L0_ffn_setup()
    _L0_ffn_in = {k: v for k, v in _L0_ffn_all.items() if k in ('W_fx', 'b_fx', 'W_x', 'b_x', 'W_slice', 'b_slice', 'W_q', 'W_k', 'W_v', 'W_out', 'b_out', 'temperature')}
    del _L0_ffn_all
    return {'x': x, 'src': src, 'dst': dst, 'edge_attr_256': edge_attr_256, 'L0_gnn_W1': _L0_gnn_in['W1'], 'L0_gnn_b1': _L0_gnn_in['b1'], 'L0_gnn_W2': _L0_gnn_in['W2'], 'L0_gnn_b2': _L0_gnn_in['b2'], 'L0_gnn_W3': _L0_gnn_in['W3'], 'L0_gnn_b3': _L0_gnn_in['b3'], 'L0_ffn_W_fx': _L0_ffn_in['W_fx'], 'L0_ffn_b_fx': _L0_ffn_in['b_fx'], 'L0_ffn_W_x': _L0_ffn_in['W_x'], 'L0_ffn_b_x': _L0_ffn_in['b_x'], 'L0_ffn_W_slice': _L0_ffn_in['W_slice'], 'L0_ffn_b_slice': _L0_ffn_in['b_slice'], 'L0_ffn_W_q': _L0_ffn_in['W_q'], 'L0_ffn_W_k': _L0_ffn_in['W_k'], 'L0_ffn_W_v': _L0_ffn_in['W_v'], 'L0_ffn_W_out': _L0_ffn_in['W_out'], 'L0_ffn_b_out': _L0_ffn_in['b_out'], 'L0_ffn_temperature': _L0_ffn_in['temperature']}

def reference(x, src, dst, edge_attr_256, L0_gnn_W1, L0_gnn_b1, L0_gnn_W2, L0_gnn_b2, L0_gnn_W3, L0_gnn_b3, L0_ffn_W_fx, L0_ffn_b_fx, L0_ffn_W_x, L0_ffn_b_x, L0_ffn_W_slice, L0_ffn_b_slice, L0_ffn_W_q, L0_ffn_W_k, L0_ffn_W_v, L0_ffn_W_out, L0_ffn_b_out, L0_ffn_temperature):
    import jax
    import jax.numpy as jnp

    def _L0_gnn_ref(vertex_features, edge_features, edge_index, W1, b1, W2, b2, W3, b3):
        import jax, jax.numpy as jnp
        import numpy as np
        N_VERTEX = 12500
        N_EDGE = 100000
        HIDDEN = 256
        num_vertex = vertex_features.shape[0]
        receivers_idx = edge_index[1]
        aggr = jax.ops.segment_sum(edge_features, receivers_idx, num_segments=num_vertex)
        collected = jnp.concatenate([vertex_features, aggr], axis=-1)
        h = jax.nn.relu(collected @ W1 + b1)
        h = jax.nn.relu(h @ W2 + b2)
        return h @ W3 + b3

    def _L0_ffn_ref(x, W_fx, b_fx, W_x, b_x, W_slice, b_slice, W_q, W_k, W_v, W_out, b_out, temperature):
        import jax, jax.numpy as jnp
        import numpy as np
        DIM = 256
        H = 8
        D = 64
        G = 64
        INNER = H * D
        SCALE = D ** (-0.5)
        B, N, _ = x.shape
        fx_mid = (x @ W_fx + b_fx).reshape(B, N, H, D).transpose(0, 2, 1, 3)
        x_mid = (x @ W_x + b_x).reshape(B, N, H, D).transpose(0, 2, 1, 3)
        temp = jnp.clip(temperature, 0.1, 5.0)
        slice_weights = jax.nn.softmax((x_mid @ W_slice + b_slice) / temp, axis=-1)
        slice_norm = slice_weights.sum(axis=2)
        slice_token = jnp.einsum('bhnc,bhng->bhgc', fx_mid, slice_weights)
        slice_token = slice_token / (slice_norm[..., None] + 1e-05)
        q = slice_token @ W_q
        k = slice_token @ W_k
        v = slice_token @ W_v
        attn = jax.nn.softmax(jnp.einsum('bhgc,bhkc->bhgk', q, k) * SCALE, axis=-1)
        out_slice = jnp.einsum('bhgk,bhkc->bhgc', attn, v)
        out_x = jnp.einsum('bhgc,bhng->bhnc', out_slice, slice_weights)
        out_x = out_x.transpose(0, 2, 1, 3).reshape(B, N, INNER)
        return out_x @ W_out + b_out
    edge_index = jnp.stack([src, dst])
    x = x + _L0_gnn_ref(_layernorm(x, axis=-1), edge_attr_256, edge_index, L0_gnn_W1, L0_gnn_b1, L0_gnn_W2, L0_gnn_b2, L0_gnn_W3, L0_gnn_b3)
    x = x + _L0_ffn_ref(_layernorm(x, axis=-1)[None], L0_ffn_W_fx, L0_ffn_b_fx, L0_ffn_W_x, L0_ffn_b_x, L0_ffn_W_slice, L0_ffn_b_slice, L0_ffn_W_q, L0_ffn_W_k, L0_ffn_W_v, L0_ffn_W_out, L0_ffn_b_out, L0_ffn_temperature)[0]
    return x

_drawn_inputs = setup_inputs


def setup_inputs(seed=0):
    import zlib

    import numpy as np

    out = dict(_drawn_inputs(seed))
    spreads = {'L0_ffn_b_fx': (0.0, 0.1),
     'L0_ffn_b_x': (0.0, 0.8),
     'L0_ffn_b_slice': (0.0, 2.0),
     'L0_ffn_b_out': (0.0, 0.1),
     'L0_ffn_temperature': (0.5, 0.6)}
    factors = {'L0_gnn_b1': 8.0,
     'L0_gnn_b2': 3.196,
     'L0_ffn_W_x': 8.0,
     'L0_ffn_W_slice': 8.0,
     'L0_ffn_W_q': 8.0,
     'L0_ffn_W_k': 8.0}
    for name, (base, spread) in spreads.items():
        noise = np.random.default_rng([zlib.crc32(name.encode()), seed]).standard_normal(out[name].shape)
        drawn = base * np.exp(spread * noise) if base else spread * noise
        out[name] = jnp.asarray(drawn.astype(out[name].dtype))
    for name, factor in factors.items():
        out[name] = (out[name] * factor).astype(out[name].dtype)
    return out
```

```python
from contextlib import ExitStack

import concourse.bass as bass
from concourse import mybir

F32 = mybir.dt.float32
I32 = mybir.dt.int32
ALU = mybir.AluOpType
ACT = mybir.ActivationFunctionType
AX = mybir.AxisListType

P = 128
UNROLL = 4
WINDOW = 64
ROWS_PER_PART = 2
GROUP = P * ROWS_PER_PART
CHUNK_GROUPS = 4
EPS_LN = 1e-5
EPS_NORM = 1e-5
CREDIT = 16


def past(t, n):
    return not isinstance(t, int) or t >= n


def before(t, n):
    return not isinstance(t, int) or t < n


def run_steps(eng, step, total, peel_front, loop_trips):
    first = peel_front * UNROLL
    for t in range(first):
        step(t, t % UNROLL, t // UNROLL)
    with eng.Fori(peel_front, peel_front + loop_trips) as i:
        for s in range(UNROLL):
            step(i * UNROLL + s, s, i)
    for t in range((peel_front + loop_trips) * UNROLL, total):
        step(t, t % UNROLL, t // UNROLL)


def build(nc, x, dst, edges, w1, b1, w2, b2, w3, b3, w_fx, b_fx, w_x, b_x, w_slice, b_slice,
          w_q, w_k, w_v, w_out, b_out, temperature, out):
    N, F = x.shape
    E = edges.shape[0]
    KF = F // P
    H = temperature.shape[1]
    D, G = w_slice.shape
    S = H * G
    PAIRS = S // P
    TILES = -(-N // P)
    NPAD = TILES * P
    LAST_ROWS = N - (TILES - 1) * P

    GROUPS = -(-E // GROUP)
    LAST_EDGES = E - (GROUPS - 1) * GROUP
    LAST_PARTS = LAST_EDGES // ROWS_PER_PART
    CHUNKS = -(-GROUPS // CHUNK_GROUPS)
    CHUNK_EDGES = CHUNK_GROUPS * GROUP
    FULL_CHUNKS = E // CHUNK_EDGES
    TAIL_GROUPS = GROUPS - FULL_CHUNKS * CHUNK_GROUPS
    EDGE_TRIPS = FULL_CHUNKS // UNROLL
    GTILES = -(-GROUPS // P)
    FULL_GTILES = GROUPS // P
    WIDE = 488
    WIDES = -(-(N + WINDOW) // WIDE)
    AGG = WIDE * WIDES
    SCALE = float(D) ** -0.5
    assert F == KF * P and P == 2 * G and D == G and S == 512 and AGG >= N + WINDOW
    assert LAST_EDGES % ROWS_PER_PART == 0 and 2 * EDGE_TRIPS == TILES - 1
    MLP_CHUNKS = (TILES - 1) // 4

    with ExitStack() as ctx:
        def sb(name, shape, dt=F32):
            return ctx.enter_context(nc.sbuf_tensor(name, shape, dt))

        def sem(name):
            return ctx.enter_context(nc.semaphore(name))

        x_sb = sb("x_sb", [P, TILES, F])
        big = sb("big", [P, KF * AGG + KF * NPAD])
        agg = big[:, 0:KF * AGG].rearrange("p (h n) -> p h n", h=KF)
        h1x = big[:, KF * AGG:].rearrange("p (h n) -> p h n", h=KF)
        sw_t = big[:, 0:PAIRS * NPAD].rearrange("p (j n) -> p j n", j=PAIRS)
        tmp = big[:, KF * AGG:]
        dst_f = tmp[:, 0:1024].rearrange("p (t e) -> p t e", t=GTILES)
        rel_g = tmp[:, 1024:2048].rearrange("p (t e) -> p t e", t=GTILES)
        wx = tmp[:, 2048:3072].rearrange("p (k n) -> p k n", k=KF)
        wx_t = tmp[:, 3072:4096].rearrange("p (k j n) -> p k j n", k=KF, j=PAIRS)
        bx_rep = tmp[:, 4096:4608].rearrange("p (j n) -> p j n", j=PAIRS)
        blk_s = tmp[:, 4608:4736]
        bx_col = tmp[:, 4736:4740]
        bsl_bc = tmp[:, 4740:4804]
        temp_bc = tmp[:, 4804:4812]
        inv_temp = tmp[:, 4812:4820]
        dst_i = tmp[:, 5000:6024].bitcast(I32).rearrange("p (t e) -> p t e", t=GTILES)

        ring_mem = sb("ring_mem", [P, UNROLL * CHUNK_GROUPS * ROWS_PER_PART * F])
        ring = ring_mem[:, :].rearrange("p (s g k f) -> p s g k f", s=UNROLL, g=CHUNK_GROUPS, k=ROWS_PER_PART)

        def part(start, size):
            return ring_mem[:, start:start + size]

        h1_t = part(0, 1024).rearrange("p (m n) -> p m n", m=KF)
        h2_t = part(1024, 1024).rearrange("p (m n) -> p m n", m=KF)
        wfx_sb = part(2048, 1024).rearrange("p (k n) -> p k n", k=KF)
        wout_sb = part(3072, 1024).rearrange("p (j n) -> p j n", j=PAIRS)
        bout_bc = part(4096, 256)
        bfx_bc = part(4352, 256).rearrange("p (j c) -> p j c", j=PAIRS)
        wq_sb = part(4608, 64)
        wk_sb = part(4672, 64)
        wv2_sb = part(4736, 128)
        sw_sum = part(4864, 512)
        soft = part(5376, 2048).rearrange("p (b n) -> p b n", b=UNROLL)
        xn_t = part(7424, 512).rearrange("p (b k n) -> p b k n", b=2, k=KF)
        s_t = part(0, 1024).rearrange("p (k n) -> p k n", k=KF)
        tok = part(1024, 256).rearrange("p (j c) -> p j c", j=PAIRS)
        nb = part(1280, 256).rearrange("p (j c) -> p j c", j=PAIRS)
        norm = part(7936, 4)
        rnorm = part(7940, 4)
        att_mx = part(7944, 8)
        att_sm = part(7952, 8)
        att_rc = part(7960, 8)
        tok_t = part(1536, 512)
        q_t = part(5376, 512)
        k_t = part(5888, 512)
        v_blk = part(6400, 512).rearrange("p (j n) -> p j n", j=PAIRS)
        att = part(6912, 512)
        a_blk = part(7424, 512).rearrange("p (j n) -> p j n", j=PAIRS)
        stage = soft
        o_sb = h1_t.rearrange("p m n -> p (m n)").rearrange("p (b f) -> p b f", b=UNROLL)

        onehot = sb("onehot", [P, 2, CHUNK_GROUPS * ROWS_PER_PART, WINDOW])
        vw = onehot[:, :, :, :].rearrange("p b g w -> p (b g w)").rearrange("p (j n) -> p j n", j=PAIRS)
        xn = sb("xn", [P, UNROLL, F])
        xo = xn
        ln_t = sb("ln_t", [P, KF, 2 * P])
        m_blk = sb("m_blk", [P, PAIRS, F])
        w1_sb = m_blk[:, :, :]
        w2_sb = part(5376, 512).rearrange("p (k n) -> p k n", k=KF)
        w3_sb = part(5888, 512).rearrange("p (k n) -> p k n", k=KF)
        wc = sb("wc", [P, KF, S])
        c_bc = sb("c_bc", [P, S])
        b3_bc = sb("b3_bc", [P, F])
        ident = sb("ident", [P, P])
        ones = sb("ones", [P, 1])
        iota_w = sb("iota_w", [P, WINDOW])
        rel = sb("rel", [P, CHUNKS * CHUNK_GROUPS, ROWS_PER_PART])
        base_i = xn[:, 2:4, :].rearrange("p b f -> p (b f)").bitcast(I32)
        base_col = sb("base_col", [P, GTILES])
        far_col = sb("far_col", [P, GTILES])
        far_one = sb("far_one", [P, 1])
        far_i = sb("far_i", [1, 2], I32)
        b1_sb = sb("b1_sb", [P, KF])
        b2_sb = sb("b2_sb", [P, KF])
        half = sb("half", [P, UNROLL])
        row_no = sb("row_no", [P, 1])
        row_ok = sb("row_ok", [P, 1])
        bn6 = sb("bn6", [P, UNROLL, 6])
        mv1 = sb("mv1", [P, 2, 2])
        var_e = sb("var_e", [P, UNROLL])
        rstd1 = sb("rstd1", [P, 2])
        mv4 = sb("mv4", [P, UNROLL, 2])
        eps = sb("eps", [P, UNROLL])
        mean2 = sb("mean2", [P, TILES])
        rstd2 = sb("rstd2", [P, TILES])
        carrier = sb("carrier", [P, 1])
        mx = sb("mx", [P, UNROLL, H])
        sm = sb("sm", [P, UNROLL, H])
        rc = sb("rc", [P, UNROLL, H])
        g_iota = part(2048, 512)
        g_hot = part(2560, 1024).rearrange("p (k n) -> p k n", k=ROWS_PER_PART)
        g_dst = part(3600, 2).bitcast(I32)
        g_abs = part(3604, 2)
        g_cov = part(3608, 2)
        g_win = part(3612, 2)

        ps = ctx.enter_context(nc.psum_tensor("ps", [P, 8, 512], F32))

        dst_in = sem("dst_in")
        edge_in = [sem(f"edge_in{s}") for s in range(UNROLL)]
        x_in = sem("x_in")
        x_tail_in = sem("x_tail_in")
        prep_in = sem("prep_in")
        mlp_in = sem("mlp_in")
        w23_in = sem("w23_in")
        late_in = sem("late_in")
        dst_clear = sem("dst_clear")
        consts = sem("consts")
        x_clear = sem("x_clear")
        blk_clear = sem("blk_clear")
        agg_clear = sem("agg_clear")
        prep_v = sem("prep_v")
        prep_t = sem("prep_t")
        hot_ready = sem("hot_ready")
        sums_ready = sem("sums_ready")
        groups_added = sem("groups_added")
        bn_done = sem("bn_done")
        mv1_ready = sem("mv1_ready")
        var1_ready = sem("var1_ready")
        rstd1_ready = sem("rstd1_ready")
        xn1_ready = sem("xn1_ready")
        ln_tp = sem("ln_tp")
        ln_t_ready = sem("ln_t_ready")
        h1x_psum = sem("h1x_psum")
        h1x_ready = sem("h1x_ready")
        xb3_ready = sem("xb3_ready")
        edges_done = sem("edges_done")
        gen_e_in = sem("gen_e_in")
        gen_d_in = sem("gen_d_in")
        gen_v = sem("gen_v")
        gen_hot = sem("gen_hot")
        gen_sums = sem("gen_sums")
        gen_group = sem("gen_group")
        l1_psum = sem("l1_psum")
        h1_sum = sem("h1_sum")
        h1_ready = sem("h1_ready")
        l2_psum = sem("l2_psum")
        h2_ready = sem("h2_ready")
        l3_psum = sem("l3_psum")
        x2_ready = sem("x2_ready")
        bn2_done = sem("bn2_done")
        mv2_ready = sem("mv2_ready")
        mean2_ready = sem("mean2_ready")
        var2_ready = sem("var2_ready")
        rstd2_ready = sem("rstd2_ready")
        xn2_ready = sem("xn2_ready")
        tp_ready = sem("tp_ready")
        xn_t_ready = sem("xn_t_ready")
        logits_ready = sem("logits_ready")
        biased = sem("biased")
        max_ready = sem("max_ready")
        shifted = sem("shifted")
        exp_ready = sem("exp_ready")
        total_ready = sem("total_ready")
        recip_ready = sem("recip_ready")
        sw_ready = sem("sw_ready")
        sw_tp = sem("sw_tp")
        sw_t_ready = sem("sw_t_ready")
        sw_summed = sem("sw_summed")
        sw_sum_clear = sem("sw_sum_clear")
        att_v = sem("att_v")
        att_t = sem("att_t")
        att_a = sem("att_a")
        att_clear = sem("att_clear")
        staged = sem("staged")
        xo_ready = sem("xo_ready")
        y_psum = sem("y_psum")
        y_ready = sem("y_ready")
        y_out = [sem(f"y_out{q}") for q in range(2)]

        block = ctx.enter_context(nc.Block())
        HOT = CHUNK_GROUPS * ROWS_PER_PART

        def tiles_of(t0, n):
            return x_sb[:, bass.ds(t0, n), :]

        @block.sync
        def _(sp):
            full = FULL_GTILES * P * GROUP
            sp.dma_start(dst_i[:, 0:FULL_GTILES, :],
                         dst[0:full].rearrange("(t p e) -> p t e", p=P, e=GROUP)).then_inc(dst_in, 16)
            sp.wait_ge(dst_clear, 1)
            whole = GROUPS - 1 - FULL_GTILES * P
            sp.dma_start(dst_i[0:whole, FULL_GTILES, :],
                         dst[full:full + whole * GROUP].rearrange("(p e) -> p e", e=GROUP)).then_inc(dst_in, 16)
            row = dst.rearrange("(a e) -> a e", a=1)
            sp.dma_start(dst_i[whole:whole + 1, FULL_GTILES, 0:LAST_EDGES],
                         row[:, E - LAST_EDGES:E]).then_inc(dst_in, 16)
            sp.dma_start(dst_i[whole:whole + 1, FULL_GTILES, LAST_EDGES:GROUP],
                         row[:, E - (GROUP - LAST_EDGES):E]).then_inc(dst_in, 16)

            def chunk(c, s, i):
                if past(c, UNROLL):
                    sp.wait_ge(sums_ready, c - UNROLL + 1)
                if before(c, FULL_CHUNKS):
                    sp.dma_start(ring[:, s].rearrange("p g k f -> p g (k f)"),
                                 edges[bass.ds(c * CHUNK_EDGES, CHUNK_EDGES), :].rearrange(
                                     "(g p k) f -> p g (k f)", p=P, k=ROWS_PER_PART)).then_inc(edge_in[s], 16)
                else:
                    e0 = FULL_CHUNKS * CHUNK_EDGES
                    e1 = (GROUPS - 1) * GROUP
                    sp.dma_start(ring[:, s, 0:TAIL_GROUPS - 1].rearrange("p g k f -> p g (k f)"),
                                 edges[e0:e1, :].rearrange("(g p k) f -> p g (k f)", p=P,
                                                           k=ROWS_PER_PART)).then_inc(edge_in[s], 16)
                    sp.dma_start(ring[0:LAST_PARTS, s, TAIL_GROUPS - 1].rearrange("p k f -> p (k f)"),
                                 edges[e1:E, :].rearrange("(p k) f -> p (k f)",
                                                          k=ROWS_PER_PART)).then_inc(edge_in[s], 16)
                if s == 0 and before(c, FULL_CHUNKS - 1):
                    if past(c, UNROLL):
                        sp.wait_ge(x_in, i * 16)
                    sp.dma_start(tiles_of(i * 2, 2),
                                 x[bass.ds(i * (2 * P), 2 * P), :].rearrange("(t p) f -> p t f", p=P)
                                 ).then_inc(x_in, 16)

            run_steps(sp, chunk, CHUNKS, 1, EDGE_TRIPS - 1)
            sp.wait_ge(x_clear, 1)
            sp.dma_start(x_sb[0:LAST_ROWS, TILES - 1, :], x[(TILES - 1) * P:N, :]).then_inc(x_tail_in, 16)

            sp.wait_ge(edges_done, 1)
            far = sp.value_load(far_i[0:1, 0:1], min_val=0, max_val=1)

            def reload(g, parts):
                sp.wait_ge(gen_group, g + 1)
                rows = bass.ds(g * GROUP, parts * ROWS_PER_PART)
                sp.dma_start(ring[0:parts, 0, 0].rearrange("p k f -> p (k f)"),
                             edges[rows, :].rearrange("(p k) f -> p (k f)", k=ROWS_PER_PART)).then_inc(gen_e_in, 16)
                sp.dma_start(g_dst[0:parts, :],
                             dst[rows].rearrange("(p k) -> p k", k=ROWS_PER_PART)).then_inc(gen_d_in, 16)

            with sp.If(far > 0):
                with sp.Fori(0, GROUPS - 1) as g:
                    reload(g, P)
                reload(GROUPS - 1, LAST_PARTS)

            sp.wait_ge(edges_done, 2)
            sp.dma_start(w2_sb, w2.rearrange("(k p) n -> p k n", p=P)).then_inc(w23_in, 16)
            sp.dma_start(w3_sb, w3.rearrange("(k p) n -> p k n", p=P)).then_inc(w23_in, 16)
            sp.dma_start(wfx_sb, w_fx.rearrange("(k p) n -> p k n", p=P)).then_inc(late_in, 16)
            sp.dma_start(wout_sb, w_out.rearrange("(j p) n -> p j n", p=P)).then_inc(late_in, 16)
            sp.dma_start(bout_bc, b_out.rearrange("(a n) -> a n", a=1).broadcast_to([P, F])).then_inc(late_in, 16)
            bfx = b_fx.rearrange("(j h c) -> h j c", h=2, c=D)
            for hh in range(2):
                sp.dma_start(bfx_bc[hh * G:(hh + 1) * G], bfx[hh:hh + 1].broadcast_to([G, PAIRS, D])
                             ).then_inc(late_in, 16)
                sp.dma_start(wv2_sb[0:D, hh * D:(hh + 1) * D], w_v).then_inc(late_in, 16)
            sp.dma_start(wq_sb[0:D, :], w_q).then_inc(late_in, 16)
            sp.dma_start(wk_sb[0:D, :], w_k).then_inc(late_in, 16)

            def store(t, s, i):
                if s % 2 == 1:
                    sp.wait_ge(y_ready, t + 1)
                    sp.dma_start(out[bass.ds((t - 1) * P, 2 * P), :].rearrange("(t p) f -> p t f", p=P),
                                 o_sb[:, s - 1:s + 1, :]).then_inc(y_out[s // 2], 16)
                elif isinstance(t, int) and t == TILES - 1:
                    sp.wait_ge(y_ready, TILES)
                    sp.dma_start(out[t * P:N, :], o_sb[0:LAST_ROWS, s, :]).then_inc(y_out[0], 16)

            run_steps(sp, store, TILES, 0, MLP_CHUNKS)
            sp.wait_ge(y_out[0], 16 * (MLP_CHUNKS + 1))
            sp.wait_ge(y_out[1], 16 * MLP_CHUNKS)

        @block.gpsimd
        def _(pool):
            pool.memset(dst_i[:, FULL_GTILES, :], 0).then_inc(dst_clear, 1)
            pool.memset(ident[:, :], 0.0).then_inc(consts, 1)
            pool.wait_ge(consts, 1)
            pool.affine_select(out=ident[:, :], in_=ident[:, :], compare_op=ALU.not_equal, fill=1.0, base=0,
                               pattern=[[-1, P]], channel_multiplier=1).then_inc(consts, 1)
            pool.iota(iota_w[:, :], [[1, WINDOW]], base=0, channel_multiplier=0,
                      allow_small_or_imprecise_dtypes=True).then_inc(consts, 1)
            pool.memset(blk_s, 0.0).then_inc(blk_clear, 1)
            pool.memset(half[:, :], -0.5).then_inc(consts, 1)
            pool.memset(eps[:, :], EPS_LN).then_inc(consts, 1)
            pool.memset(ones[:, :], 1.0).then_inc(consts, 1)
            pool.iota(row_no[:, :], [[0, 1]], base=0, channel_multiplier=1,
                      allow_small_or_imprecise_dtypes=True).then_inc(consts, 1)
            pool.memset(agg[:, 1, :], 0.0).then_inc(agg_clear, 1)
            pool.memset(x_sb[:, TILES - 1, :], 0.0).then_inc(x_clear, 1)
            pool.wait_ge(consts, 7)

            def rstd(mv, dest, n, ready, tiles_ready, step_sem, done, count):
                pool.wait_ge(ready, tiles_ready)
                pool.tensor_tensor(var_e[:, 0:n], mv, eps[:, 0:n], ALU.add).then_inc(step_sem, 1)
                pool.wait_ge(step_sem, count)
                pool.tensor_tensor(dest, var_e[:, 0:n], half[:, 0:n], ALU.pow).then_inc(done, 1)

            pool.wait_ge(mlp_in, 16 * 4)

            def ln_pair(i, n):
                rstd(mv1[:, 0:n, 1], rstd1[:, 0:n], n, mv1_ready, i * 2 + n, var1_ready, rstd1_ready, i + 1)
                pool.wait_ge(xn1_ready, i * 2 + n)
                pool.tensor_tensor(tiles_of(i * 2, n), tiles_of(i * 2, n),
                                   b3_bc[:, :].unsqueeze(1).broadcast_to([P, n, F]), ALU.add).then_inc(xb3_ready, 1)

            with pool.Fori(0, EDGE_TRIPS) as i:
                ln_pair(i, 2)
            ln_pair(EDGE_TRIPS, 1)

            def rstd_chunk(i, n):
                rstd(mv4[:, 0:n, 1], rstd2[:, bass.ds(i * 4, n)], n, mv2_ready, i * 4 + n, var2_ready,
                     rstd2_ready, i + 1)

            rstd_chunk(0, 4)
            with pool.Fori(1, MLP_CHUNKS) as i:
                pool.wait_ge(rstd2_ready, i)
                rstd_chunk(i, 4)
            pool.wait_ge(rstd2_ready, MLP_CHUNKS)
            rstd_chunk(MLP_CHUNKS, 1)

            pool.wait_ge(edges_done, 2)
            pool.memset(sw_sum, 0.0).then_inc(sw_summed, 1)

            def soft_step(t, s, i):
                if before(t, TILES):
                    pool.wait_ge(max_ready, t + 1)
                    v = soft[:, s, :].rearrange("p (h g) -> p h g", h=H)
                    pool.tensor_tensor(v, v, mx[:, s, :].unsqueeze(2).broadcast_to([P, H, G]),
                                       ALU.subtract).then_inc(shifted, 1)
                if past(t, 1):
                    pool.wait_ge(sw_ready, t)
                    pool.wait_ge(sw_summed, t)
                    pool.tensor_tensor(sw_sum, sw_sum, soft[:, (s - 1) % UNROLL, :], ALU.add).then_inc(sw_summed, 1)

            run_steps(pool, soft_step, TILES + 1, 1, (TILES - 1) // UNROLL - 1)

            pool.wait_ge(sw_tp, TILES)
            pool.wait_ge(sw_summed, TILES + 1)
            pool.memset(v_blk, 0.0).then_inc(att_clear, 1)
            pool.memset(a_blk, 0.0).then_inc(att_clear, 1)

            pool.wait_ge(late_in, 16 * 9)

            def residual(t, s, i):
                if past(t, UNROLL):
                    pool.wait_ge(y_ready, t - UNROLL + 1)
                pool.tensor_tensor(xo[:, s, :], x_sb[:, bass.ds(t, 1), :].rearrange("p a f -> p (a f)"),
                                   bout_bc, ALU.add).then_inc(xo_ready, 1)

            run_steps(pool, residual, TILES, 1, MLP_CHUNKS - 1)

        @block.scalar
        def _(act):
            act.dma_start(wx, w_x.rearrange("(k p) n -> p k n", p=P)).then_inc(prep_in, 16)
            act.dma_start(bx_col, b_x.rearrange("(j p) -> p j", p=P), allow_slow_non_contiguous=True).then_inc(prep_in, 16)
            act.dma_start(bsl_bc, b_slice.rearrange("(a g) -> a g", a=1).broadcast_to([P, G])).then_inc(prep_in, 16)
            act.dma_start(temp_bc, temperature.rearrange("a h b c -> a (h b c)").broadcast_to([P, H])
                          ).then_inc(prep_in, 16)
            act.dma_start(w1_sb, w1.rearrange("(k p) n -> p k n", p=P)).then_inc(mlp_in, 16)
            act.dma_start(b1_sb[:, :], b1.rearrange("(m p) -> p m", p=P), allow_slow_non_contiguous=True).then_inc(mlp_in, 16)
            act.dma_start(b2_sb[:, :], b2.rearrange("(m p) -> p m", p=P), allow_slow_non_contiguous=True).then_inc(mlp_in, 16)
            act.dma_start(b3_bc[:, :], b3.rearrange("(a n) -> a n", a=1).broadcast_to([P, F])).then_inc(mlp_in, 16)
            act.wait_ge(blk_clear, 1)
            for hh in range(2):
                act.dma_start(blk_s[hh * D:(hh + 1) * D, hh * G:(hh + 1) * G], w_slice).then_inc(prep_in, 16)
            act.wait_ge(mlp_in, 16 * 4)

            def ln_pair(i, n):
                act.wait_ge(ln_tp, i + 1)
                act.activation(ln_t[:, :, 0:n * P], ps[:, 4, :].rearrange("p (k c) -> p k c", k=KF)[:, :, 0:n * P],
                               ACT.Copy).then_inc(ln_t_ready, 1)
                act.wait_ge(h1x_psum, i + 1)
                for m in range(KF):
                    act.activation(h1x[:, m, bass.ds(i * 2 * P, n * P)], ps[:, 5, m * 256:m * 256 + n * P],
                                   ACT.Identity, bias=b1_sb[:, m:m + 1]).then_inc(h1x_ready, 1)

            with act.Fori(0, EDGE_TRIPS) as i:
                ln_pair(i, 2)
            ln_pair(EDGE_TRIPS, 1)

            def relus(i, cols):
                act.wait_ge(h1_sum, i + 1)
                act.activation(h1_t[:, :, 0:cols], h1_t[:, :, 0:cols], ACT.Relu).then_inc(h1_ready, 1)
                act.wait_ge(l2_psum, i + 1)
                for m in range(KF):
                    act.activation(h2_t[:, m, 0:cols], ps[:, 2 + m, 0:cols], ACT.Relu,
                                   bias=b2_sb[:, m:m + 1]).then_inc(h2_ready, 1)

            with act.Fori(0, MLP_CHUNKS) as i:
                relus(i, 4 * P)
            relus(MLP_CHUNKS, P)

            def copy_xn_t(t, b):
                act.wait_ge(tp_ready, t + 1)
                act.activation(xn_t[:, b], ps[:, 2 + b, 0:2 * P].rearrange("p (k n) -> p k n", k=KF),
                               ACT.Copy).then_inc(xn_t_ready, 1)

            def soft_step(t, s, i):
                if before(t, TILES - 1):
                    if past(t, 1):
                        act.wait_ge(logits_ready, t)
                    copy_xn_t(t + 1, (s + 1) % 2)
                if past(t, 2):
                    act.wait_ge(sw_tp, t - 1)
                    act.activation(sw_t[:, :, bass.ds((t - 2) * P, P)],
                                   ps[:, 6 + s % 2, :].rearrange("p (j n) -> p j n", j=PAIRS),
                                   ACT.Copy).then_inc(sw_t_ready, 1)
                if before(t, TILES):
                    act.wait_ge(shifted, t + 1)
                    act.activation(soft[:, s, :], soft[:, s, :], ACT.Exp).then_inc(exp_ready, 1)

            copy_xn_t(0, 0)
            run_steps(act, soft_step, TILES + 2, 1, (TILES - 1) // UNROLL - 1)

            act.wait_ge(att_clear, 1)
            act.wait_ge(att_t, 4)
            act.activation(q_t[0:D, :], ps[0:D, 0, :], ACT.Copy, scale=SCALE).then_inc(att_a, 1)
            act.wait_ge(att_v, 13)
            act.activation(att[0:G, :], att[0:G, :], ACT.Exp).then_inc(att_a, 1)

            def stage_step(t, s, i):
                if past(t, UNROLL):
                    act.wait_ge(y_psum, t - UNROLL + 1)
                act.activation(stage[:, s, :].rearrange("p (j n) -> p j n", j=PAIRS),
                               sw_t[:, :, bass.ds(t * P, P)], ACT.Copy).then_inc(staged, 1)

            act.wait_ge(att_t, 8)
            run_steps(act, stage_step, TILES, 1, MLP_CHUNKS - 1)

        @block.vector
        def _(dve):
            done = [0]

            def then(ins):
                ins.then_inc(prep_v, 1)
                done[0] += 1
                return done[0]

            dve.memset(agg[:, 0, :], 0.0).then_inc(agg_clear, 1)
            dve.wait_ge(dst_in, 16 * 4)
            dve.wait_ge(prep_v, then(dve.tensor_copy(dst_f, dst_i)))
            dve.wait_ge(prep_v, then(dve.tensor_reduce(base_col[:, :], dst_f, AX.X, ALU.min)))
            dve.wait_ge(prep_v, then(dve.tensor_scalar(base_col[:, :], base_col[:, :], 0.0, float(N), ALU.max, ALU.min)))
            for t in range(GTILES):
                n = then(dve.tensor_scalar(rel_g[:, t, :], dst_f[:, t, :], base_col[:, t:t + 1], None, ALU.subtract))
            dve.wait_ge(prep_v, n)
            dve.wait_ge(prep_v, then(dve.tensor_reduce(far_col[:, :], rel_g, AX.X, ALU.max)))
            then(dve.tensor_reduce(far_one[:, :], far_col[:, :], AX.X, ALU.max))
            dve.wait_ge(prep_t, 1)
            for k in range(ROWS_PER_PART):
                for t in range(GTILES):
                    n = min(P, CHUNKS * CHUNK_GROUPS - t * P)
                    then(dve.tensor_copy(rel[:, t * P:t * P + n, k], ps[:, 6 + k, t * P:t * P + n]))
            dve.wait_ge(prep_t, 2)
            then(dve.tensor_copy(base_i[0:1, :], ps[0:1, 5, :]))
            dve.wait_ge(prep_v, then(dve.tensor_reduce(far_col[0:1, 0:1], ps[0:1, 4, 0:P], AX.X, ALU.max)))
            table = then(dve.tensor_scalar(far_i[0:1, 0:1], far_col[0:1, 0:1], float(WINDOW), None, ALU.is_ge))
            dve.wait_ge(prep_v, table)
            dve.wait_ge(agg_clear, 2)
            dve.wait_ge(consts, 7)
            dve.tensor_scalar(row_ok[:, :], row_no[:, :], float(LAST_ROWS), None, ALU.is_lt).then_inc(groups_added, CREDIT)

            base_regs = [dve.alloc_register(f"base{n}") for n in range(UNROLL * CHUNK_GROUPS)]
            base_of = [None] * len(base_regs)

            def build_hot(c, b):
                dve.tensor_tensor(onehot[:, b], iota_w[:, :].unsqueeze(1).broadcast_to([P, HOT, WINDOW]),
                                  rel[:, bass.ds(c * CHUNK_GROUPS, CHUNK_GROUPS), :].rearrange("p g k -> p (g k)")
                                  .unsqueeze(2).broadcast_to([P, HOT, WINDOW]), ALU.is_equal).then_inc(hot_ready, 1)

            def norm_stats(i, n):
                for a in range(n):
                    dve.bn_stats(bn6[:, a, :], x_sb[:, bass.ds(i * 2 + a, 1), :].rearrange("p a f -> p (a f)")
                                 ).then_inc(bn_done, 1)
                dve.wait_ge(bn_done, i * 2 + n)
                dve.tensor_copy(carrier[:, :], bn6[:, 0, 0:1])
                for a in range(n):
                    dve.bn_aggr(mv1[:, a, :], bn6[:, a, :]).then_inc(mv1_ready, 1)

            def norm_rows(i, n):
                dve.wait_ge(rstd1_ready, i + 1)
                for a in range(n):
                    dve.tensor_scalar(xn[:, a, :], x_sb[:, bass.ds(i * 2 + a, 1), :].rearrange("p a f -> p (a f)"),
                                      mv1[:, a, 0:1], rstd1[:, a:a + 1], ALU.subtract, ALU.mult).then_inc(xn1_ready, 1)

            def chunk(c, s, i):
                if s == 0:
                    dve.load(base_regs, base_i[0:1, bass.ds(i * (UNROLL * CHUNK_GROUPS), UNROLL * CHUNK_GROUPS)])
                    for n, r in enumerate(base_regs):
                        base_of[n] = dve.snap(r, min_val=0, max_val=N)
                if before(c, CHUNKS - 1):
                    build_hot(c + 1, (s + 1) % 2)
                dve.wait_ge(sums_ready, c + 1)
                for g in range(CHUNK_GROUPS if before(c, FULL_CHUNKS) else TAIL_GROUPS):
                    dve.wait_ge(groups_added, c * CHUNK_GROUPS + (CREDIT + g))
                    win = agg[:, :, bass.ds(base_of[s * CHUNK_GROUPS + g], WINDOW)]
                    dve.tensor_tensor(win, win, ps[:, s, g * P:(g + 1) * P].rearrange("p (h n) -> p h n", h=KF),
                                      ALU.add).then_inc(groups_added, 1)
                if before(c, FULL_CHUNKS - 1):
                    if s == 0:
                        dve.wait_ge(x_in, i * 16 + 16)
                        norm_stats(i, 2)
                    if s == 1:
                        norm_rows(i, 2)

            build_hot(0, 0)
            dve.wait_ge(prep_in, 16 * 6)
            dve.wait_ge(prep_v, then(dve.tensor_scalar(inv_temp, temp_bc, 0.1, 5.0, ALU.max, ALU.min)))
            then(dve.reciprocal(inv_temp, inv_temp))
            fold = then(dve.tensor_copy(bx_rep, bx_col.unsqueeze(2).broadcast_to([P, PAIRS, P])))
            dve.wait_ge(prep_t, 3)
            for k in range(KF):
                n = then(dve.tensor_copy(wx_t[:, k].rearrange("p j n -> p (j n)"), ps[:, 6 + k, :]))
            dve.wait_ge(prep_t, 4)
            dve.wait_ge(prep_v, n)
            inv_all = inv_temp.unsqueeze(2).broadcast_to([P, H, G])

            def heads(v):
                return v.rearrange("p (h g) -> p h g", h=H)

            for k in range(KF):
                then(dve.tensor_tensor(heads(wc[:, k, :]), heads(ps[:, 6 + k, :]), inv_all, ALU.mult))
            dve.wait_ge(prep_v, then(dve.tensor_tensor(heads(c_bc[:, :]), heads(ps[:, 5, :]),
                                                       bsl_bc.unsqueeze(1).broadcast_to([P, H, G]), ALU.add)))
            dve.wait_ge(prep_v, then(dve.tensor_tensor(heads(c_bc[:, :]), heads(c_bc[:, :]), inv_all, ALU.mult)))

            run_steps(dve, chunk, CHUNKS, 0, EDGE_TRIPS)
            dve.wait_ge(x_tail_in, 16)
            norm_stats(EDGE_TRIPS, 1)
            norm_rows(EDGE_TRIPS, 1)
            dve.wait_ge(groups_added, CREDIT + GROUPS)
            dve.drain().then_inc(edges_done, 1)

            far = dve.value_load(far_i[0:1, 0:1], min_val=0, max_val=1)
            with dve.If(far > 0):
                for n in range(512 // WINDOW):
                    dve.tensor_scalar(g_iota[:, n * WINDOW:(n + 1) * WINDOW], iota_w[:, :], float(n * WINDOW), None,
                                      ALU.add).then_inc(gen_v, 1)
                dve.wait_ge(gen_v, 8)
                dve.drain().then_inc(gen_group, 1)
                PER_GROUP = 3 + WIDES

                def far_group(g, parts):
                    step = g * PER_GROUP + 8
                    dve.wait_ge(gen_d_in, g * 16 + 16)
                    dve.tensor_copy(g_abs[0:parts, :], g_dst[0:parts, :]).then_inc(gen_v, 1)
                    dve.tensor_scalar(g_cov[0:parts, :], rel[0:parts, bass.ds(g, 1), :].rearrange("p g k -> p (g k)"),
                                      float(WINDOW), float(4 * AGG), ALU.is_lt, ALU.mult).then_inc(gen_v, 1)
                    dve.wait_ge(gen_v, step + 2)
                    dve.tensor_tensor(g_abs[0:parts, :], g_abs[0:parts, :], g_cov[0:parts, :], ALU.add).then_inc(gen_v, 1)
                    for w in range(WIDES):
                        dve.wait_ge(gen_v, step + (3 + w))
                        dve.tensor_scalar(g_win[0:parts, :], g_abs[0:parts, :], float(w * WIDE), None,
                                          ALU.subtract).then_inc(gen_v, 1)
                        dve.wait_ge(gen_v, step + (4 + w))
                        for k in range(ROWS_PER_PART):
                            dve.tensor_scalar(g_hot[0:parts, k, :], g_iota[0:parts, :], g_win[0:parts, k:k + 1], None,
                                              ALU.is_equal).then_inc(gen_hot, 1)
                        dve.wait_ge(gen_sums, g * WIDES + (w + 1))
                        view = agg[:, :, w * WIDE:(w + 1) * WIDE]
                        last = dve.tensor_tensor(view, view, ps[:, 0:2, 0:WIDE], ALU.add)
                        last.then_inc(groups_added, 1)
                        dve.wait_ge(groups_added, g * WIDES + (CREDIT + GROUPS + w + 1))
                    dve.memset(g_cov, 0.0).then_inc(gen_group, 1)

                with dve.Fori(0, GROUPS - 1) as g:
                    far_group(g, P)
                far_group(GROUPS - 1, LAST_PARTS)
            dve.drain().then_inc(edges_done, 1)

            def add_h1(i, cols):
                dve.wait_ge(l1_psum, i + 1)
                dve.tensor_tensor(h1_t[:, :, 0:cols], ps[:, 0:2, 0:cols], h1x[:, :, bass.ds(i * 4 * P, cols)],
                                  ALU.add).then_inc(h1_sum, 1)

            def residual(i, n):
                if past(i, 1):
                    dve.wait_ge(var2_ready, i)
                dve.wait_ge(l3_psum, i + 1)
                rows = tiles_of(i * 4, n)
                dve.tensor_tensor(rows, rows, ps[:, 4:6, :].rearrange("p b (t f) -> p (b t) f", f=F)[:, 0:n, :],
                                  ALU.add).then_inc(x2_ready, 1)
                dve.wait_ge(consts, 7)
                dve.wait_ge(x2_ready, i + 1)
                for a in range(n):
                    dve.bn_stats(bn6[:, a, :], x_sb[:, bass.ds(i * 4 + a, 1), :].rearrange("p a f -> p (a f)")
                                 ).then_inc(bn2_done, 1)
                dve.wait_ge(bn2_done, i * 4 + n)
                dve.tensor_copy(carrier[:, :], bn6[:, 0, 0:1])
                for a in range(n):
                    dve.bn_aggr(mv4[:, a, :], bn6[:, a, :]).then_inc(mv2_ready, 1)
                dve.wait_ge(mv2_ready, i * 4 + n)
                dve.tensor_copy(mean2[:, bass.ds(i * 4, n)], mv4[:, 0:n, 0]).then_inc(mean2_ready, 1)

            dve.wait_ge(h1x_ready, 2 * (EDGE_TRIPS + 1))
            dve.wait_ge(xb3_ready, EDGE_TRIPS + 1)
            add_h1(0, 4 * P)
            add_h1(1, 4 * P)
            residual(0, 4)
            with dve.Fori(1, MLP_CHUNKS - 1) as i:
                add_h1(i + 1, 4 * P)
                residual(i, 4)
            add_h1(MLP_CHUNKS, P)
            residual(MLP_CHUNKS - 1, 4)
            residual(MLP_CHUNKS, 1)

            dve.wait_ge(rstd2_ready, MLP_CHUNKS + 1)

            def normalise(t, s):
                if past(t, UNROLL):
                    dve.wait_ge(sw_tp, t - UNROLL + 1)
                dve.tensor_scalar(xn[:, s, :], x_sb[:, bass.ds(t, 1), :].rearrange("p a f -> p (a f)"),
                                  mean2[:, bass.ds(t, 1)], rstd2[:, bass.ds(t, 1)], ALU.subtract, ALU.mult
                                  ).then_inc(xn2_ready, 1)

            def soft_step(t, s, i):
                if before(t, TILES):
                    dve.wait_ge(logits_ready, t + 1)
                    if past(t, UNROLL):
                        dve.wait_ge(sw_tp, t - UNROLL + 1)
                        dve.wait_ge(sw_summed, t - UNROLL + 2)
                    dve.tensor_tensor(soft[:, s, :], ps[:, s % 2, :], c_bc[:, :], ALU.add).then_inc(biased, 1)
                    dve.wait_ge(biased, t + 1)
                    dve.tensor_reduce(mx[:, s, :], heads(soft[:, s, :]), AX.X, ALU.max).then_inc(max_ready, 1)
                if past(t, 1) and before(t, TILES + 1):
                    r = (s - 1) % UNROLL
                    dve.wait_ge(exp_ready, t)
                    dve.tensor_reduce(sm[:, r, :], heads(soft[:, r, :]), AX.X, ALU.add).then_inc(total_ready, 1)
                    dve.wait_ge(total_ready, t)
                    dve.reciprocal(rc[:, r, :], sm[:, r, :]).then_inc(recip_ready, 1)
                    dve.wait_ge(recip_ready, t)
                    if isinstance(t, int) and t == TILES:
                        dve.tensor_scalar(rc[:, r, :], rc[:, r, :], row_ok[:, 0:1], None, ALU.mult).then_inc(recip_ready, 1)
                        dve.wait_ge(recip_ready, t + 1)
                    dve.tensor_tensor(heads(soft[:, r, :]), heads(soft[:, r, :]),
                                      rc[:, r, :].unsqueeze(2).broadcast_to([P, H, G]), ALU.mult).then_inc(sw_ready, 1)
                if before(t, TILES - 2):
                    normalise(t + 2, (s + 2) % UNROLL)

            normalise(0, 0)
            normalise(1, 1)
            run_steps(dve, soft_step, TILES + 1, 1, (TILES - 1) // UNROLL - 2)

            n_att = [0]

            def att_step(ins):
                ins.then_inc(att_v, 1)
                n_att[0] += 1
                return n_att[0]

            dve.wait_ge(sw_tp, TILES)
            att_step(dve.tensor_copy(s_t, ps[:, 4:6, :]))
            dve.wait_ge(att_t, 1)
            dve.wait_ge(late_in, 16 * 9)
            n = att_step(dve.tensor_copy(norm, ps[:, 0, 0:PAIRS]))
            dve.wait_ge(att_v, n)
            att_step(dve.tensor_scalar(rnorm, norm, EPS_NORM, None, ALU.add))
            n = att_step(dve.tensor_tensor(nb, bfx_bc, norm.unsqueeze(2).broadcast_to([P, PAIRS, D]), ALU.mult))
            dve.wait_ge(att_v, n)
            n = att_step(dve.reciprocal(rnorm, rnorm))
            dve.wait_ge(att_t, 2)
            tp = ps[:, 1, :].rearrange("p (j c) -> p j c", j=PAIRS)
            for hh in range(2):
                rows = slice(hh * G, (hh + 1) * G)
                n = att_step(dve.tensor_tensor(tok[rows], tp[rows, :, hh * D:(hh + 1) * D], nb[rows], ALU.add))
            dve.wait_ge(att_v, n)
            att_step(dve.tensor_tensor(tok, tok, rnorm.unsqueeze(2).broadcast_to([P, PAIRS, D]), ALU.mult))
            dve.wait_ge(att_t, 3)
            att_step(dve.tensor_copy(tok_t[0:D, :], ps[0:D, 2, :]))
            dve.wait_ge(att_clear, 2)
            dve.wait_ge(att_t, 4)
            att_step(dve.tensor_copy(k_t[0:D, :], ps[0:D, 1, :]))
            vp = ps[:, 3, :].rearrange("p (j n) -> p j n", j=PAIRS)
            for hh in range(2):
                rows = slice(hh * D, (hh + 1) * D)
                n_v = att_step(dve.tensor_copy(v_blk[rows, :, hh * G:(hh + 1) * G], vp[rows, :, hh * G:(hh + 1) * G]))
            dve.wait_ge(att_t, 5)
            at3 = att[0:G, :].rearrange("p (h g) -> p h g", h=H)
            sp3 = ps[0:G, 2, :].rearrange("p (h g) -> p h g", h=H)
            dve.tensor_reduce(att_mx[0:G, :], sp3, AX.X, ALU.max).then_inc(biased, 1)
            dve.wait_ge(biased, TILES + 1)
            att_step(dve.tensor_tensor(at3, sp3, att_mx[0:G, :].unsqueeze(2).broadcast_to([G, H, G]), ALU.subtract))
            dve.wait_ge(att_t, 6)
            att_step(dve.tensor_copy(vw, ps[:, 4:6, :].rearrange("p b (j f) -> p (b j) f", f=F)))
            dve.wait_ge(att_a, 2)
            n = att_step(dve.tensor_reduce(att_sm[0:G, :], at3, AX.X, ALU.add))
            dve.wait_ge(att_v, n)
            n = att_step(dve.reciprocal(att_rc[0:G, :], att_sm[0:G, :]))
            dve.wait_ge(att_v, n)
            att_step(dve.tensor_tensor(at3, at3, att_rc[0:G, :].unsqueeze(2).broadcast_to([G, H, G]), ALU.mult))
            dve.wait_ge(att_t, 7)
            ap = ps[:, 6, 0:PAIRS * G].rearrange("p (j g) -> p j g", j=PAIRS)
            for hh in range(2):
                rows = slice(hh * G, (hh + 1) * G)
                att_step(dve.tensor_copy(a_blk[rows, :, hh * G:(hh + 1) * G], ap[rows]))
            dve.wait_ge(att_t, 8)
            att_step(dve.tensor_copy(m_blk[:, :, :], ps[:, 4:6, :].rearrange("p b (j f) -> p (b j) f", f=F)))

            def finish(t, s, i):
                dve.wait_ge(y_psum, t + 1)
                dve.wait_ge(xo_ready, t + 1)
                if past(t, UNROLL):
                    dve.wait_ge(y_out[s // 2], i * 16)
                dve.tensor_tensor(o_sb[:, s, :], ps[:, s, 0:F], xo[:, s, :], ALU.add).then_inc(y_ready, 1)

            run_steps(dve, finish, TILES, 1, MLP_CHUNKS - 1)

        @block.tensor
        def _(pe):
            mm = nc.tensor.matmul
            tr = nc.tensor.transpose
            pe.wait_ge(consts, 7)
            pe.wait_ge(prep_v, 7)
            for k in range(ROWS_PER_PART):
                for t in range(GTILES):
                    src = rel_g[:, t, :].rearrange("p (e k) -> p k e", k=ROWS_PER_PART)[:, k, :]
                    last = tr(ps[:, 6 + k, t * P:(t + 1) * P], src, ident[:, :])
            last.then_inc(prep_t, 1)
            pe.wait_ge(prep_v, 9)
            for t in range(GTILES):
                tr(ps[0:1, 5, t * P:(t + 1) * P], base_col[:, t:t + 1], ident[:, :])
            tr(ps[0:1, 4, 0:P], far_one[:, 0:1], ident[:, :]).then_inc(prep_t, 1)
            pe.wait_ge(prep_in, 16 * 6)
            pe.wait_ge(prep_v, 23)
            for k in range(KF):
                for j in range(PAIRS):
                    last = tr(ps[:, 6 + k, j * P:(j + 1) * P], wx[:, k, j * P:(j + 1) * P], ident[:, :])
            last.then_inc(prep_t, 1)
            pe.wait_ge(prep_v, 25)
            for j in range(PAIRS):
                for k in range(KF):
                    mm(ps[:, 6 + k, j * P:(j + 1) * P], lhsT=wx_t[:, k, j, :], rhs=blk_s, start=True, stop=True)
                last = mm(ps[:, 5, j * P:(j + 1) * P], lhsT=bx_rep[:, j, :], rhs=blk_s, start=True, stop=True)
            last.then_inc(prep_t, 1)
            pe.wait_ge(prep_v, 29)
            pe.wait_ge(mlp_in, 16 * 4)

            def chunk(c, s, i):
                pe.wait_ge(hot_ready, c + 1)
                if before(c, FULL_CHUNKS):
                    pe.wait_ge(edge_in[s], i * 16 + 16)
                else:
                    pe.wait_ge(edge_in[s], i * 16 + 32)
                pe.wait_ge(groups_added, c * CHUNK_GROUPS + (CREDIT - (UNROLL - 1) * CHUNK_GROUPS))
                groups = CHUNK_GROUPS if before(c, FULL_CHUNKS) else TAIL_GROUPS
                for g in range(groups):
                    parts = P if before(c, FULL_CHUNKS) or g < groups - 1 else LAST_PARTS
                    for h in range(KF):
                        for k in range(ROWS_PER_PART):
                            last = mm(ps[:, s, g * P + h * WINDOW:g * P + (h + 1) * WINDOW],
                                      lhsT=ring[0:parts, s, g, k, h * P:(h + 1) * P],
                                      rhs=onehot[0:parts, s % 2, g * ROWS_PER_PART + k, :],
                                      start=(k == 0), stop=(k == ROWS_PER_PART - 1))
                last.then_inc(sums_ready, 1)
                if before(c, FULL_CHUNKS - 1):
                    if s == 2:
                        ln_transposes(i, 2)
                    if s == 3:
                        first_layer_x(i, 2)

            def ln_transposes(i, n):
                pe.wait_ge(xn1_ready, i * 2 + n)
                for a in range(n):
                    for k in range(KF):
                        last = tr(ps[:, 4, k * 256 + a * P:k * 256 + (a + 1) * P], xn[:, a, k * P:(k + 1) * P],
                                  ident[:, :])
                last.then_inc(ln_tp, 1)

            def first_layer_x(i, n):
                pe.wait_ge(ln_t_ready, i + 1)
                for m in range(KF):
                    for k in range(KF):
                        last = mm(ps[:, 5, m * 256:m * 256 + n * P], lhsT=w1_sb[:, k, m * P:(m + 1) * P],
                                  rhs=ln_t[:, k, 0:n * P], start=(k == 0), stop=(k == KF - 1))
                last.then_inc(h1x_psum, 1)

            run_steps(pe, chunk, CHUNKS, 0, EDGE_TRIPS)
            ln_transposes(EDGE_TRIPS, 1)
            first_layer_x(EDGE_TRIPS, 1)

            pe.wait_ge(edges_done, 1)
            far = pe.value_load(far_i[0:1, 0:1], min_val=0, max_val=1)

            def far_group(g, parts):
                pe.wait_ge(gen_e_in, g * 16 + 16)
                for w in range(WIDES):
                    pe.wait_ge(gen_hot, g * (2 * WIDES) + (2 * w + 2))
                    for h in range(KF):
                        for k in range(ROWS_PER_PART):
                            last = mm(ps[:, h, 0:WIDE], lhsT=ring[0:parts, 0, 0, k, h * P:(h + 1) * P],
                                      rhs=g_hot[0:parts, k, 0:WIDE], start=(k == 0), stop=(k == ROWS_PER_PART - 1))
                    last.then_inc(gen_sums, 1)

            with pe.If(far > 0):
                with pe.Fori(0, GROUPS - 1) as g:
                    far_group(g, P)
                far_group(GROUPS - 1, LAST_PARTS)
            pe.wait_ge(edges_done, 2)

            def layer1(i, cols):
                for m in range(KF):
                    for k in range(KF):
                        last = mm(ps[:, m, 0:cols], lhsT=w1_sb[:, KF + k, m * P:(m + 1) * P],
                                  rhs=agg[:, k, bass.ds(i * 4 * P, cols)], start=(k == 0), stop=(k == KF - 1))
                last.then_inc(l1_psum, 1)

            def layer2(i, cols):
                pe.wait_ge(h1_ready, i + 1)
                for m in range(KF):
                    for k in range(KF):
                        last = mm(ps[:, 2 + m, 0:cols], lhsT=w2_sb[:, k, m * P:(m + 1) * P],
                                  rhs=h1_t[:, k, 0:cols], start=(k == 0), stop=(k == KF - 1))
                last.then_inc(l2_psum, 1)

            def layer3(i, n):
                pe.wait_ge(h2_ready, i * 2 + 2)
                if past(i, 1):
                    pe.wait_ge(x2_ready, i)
                for a in range(n):
                    for k in range(KF):
                        last = mm(ps[:, 4 + a // 2, (a % 2) * F:(a % 2 + 1) * F],
                                  lhsT=h2_t[:, k, a * P:(a + 1) * P], rhs=w3_sb[:, k, :],
                                  start=(k == 0), stop=(k == KF - 1))
                last.then_inc(l3_psum, 1)

            layer1(0, 4 * P)
            pe.wait_ge(w23_in, 32)
            layer2(0, 4 * P)
            layer1(1, 4 * P)
            layer3(0, 4)
            with pe.Fori(1, MLP_CHUNKS - 1) as i:
                layer2(i, 4 * P)
                layer1(i + 1, 4 * P)
                layer3(i, 4)
            layer2(MLP_CHUNKS - 1, 4 * P)
            layer1(MLP_CHUNKS, P)
            layer3(MLP_CHUNKS - 1, 4)
            layer2(MLP_CHUNKS, P)
            layer3(MLP_CHUNKS, 1)

            def tp_rows(t, s):
                pe.wait_ge(xn2_ready, t + 1)
                for k in range(KF):
                    last = tr(ps[:, 2 + s % 2, k * P:(k + 1) * P], xn[:, s, k * P:(k + 1) * P], ident[:, :])
                last.then_inc(tp_ready, 1)

            def soft_step(t, s, i):
                if before(t, TILES - 1):
                    tp_rows(t + 1, (s + 1) % UNROLL)
                if before(t, TILES):
                    pe.wait_ge(xn_t_ready, t + 1)
                    if past(t, 2):
                        pe.wait_ge(biased, t - 1)
                    for k in range(KF):
                        last = mm(ps[:, s % 2, :], lhsT=xn_t[:, s % 2, k, :], rhs=wc[:, k, :],
                                  start=(k == 0), stop=(k == KF - 1))
                    last.then_inc(logits_ready, 1)
                if past(t, 2):
                    r = (s - 2) % UNROLL
                    pe.wait_ge(sw_ready, t - 1)
                    for k in range(KF):
                        mm(ps[:, 4 + k, :], lhsT=xn[:, r, k * P:(k + 1) * P], rhs=soft[:, r, :],
                           start=isinstance(t, int) and t == 2, stop=isinstance(t, int) and t == TILES + 1)
                    if past(t, 4):
                        pe.wait_ge(sw_t_ready, t - 3)
                    for j in range(PAIRS):
                        last = tr(ps[:, 6 + s % 2, j * P:(j + 1) * P], soft[:, r, j * P:(j + 1) * P], ident[:, :])
                    last.then_inc(sw_tp, 1)

            tp_rows(0, 0)
            run_steps(pe, soft_step, TILES + 2, 1, (TILES - 1) // UNROLL - 1)

            pe.wait_ge(sw_summed, TILES + 1)
            for j in range(PAIRS):
                last = mm(ps[:, 0, j:j + 1], lhsT=sw_sum[:, j * P:(j + 1) * P], rhs=ones[:, 0:1], start=True, stop=True)
            last.then_inc(att_t, 1)
            pe.wait_ge(att_v, 1)
            pe.wait_ge(late_in, 16 * 9)
            for j in range(PAIRS):
                for k in range(KF):
                    last = mm(ps[:, 1, j * P:(j + 1) * P], lhsT=s_t[:, k, j * P:(j + 1) * P],
                              rhs=wfx_sb[:, k, j * P:(j + 1) * P], start=(k == 0), stop=(k == KF - 1))
            last.then_inc(att_t, 1)
            pe.wait_ge(att_v, 8)
            for j in range(PAIRS):
                last = tr(ps[0:D, 2, j * P:(j + 1) * P], tok[:, j, :], ident[:, :])
            last.then_inc(att_t, 1)
            pe.wait_ge(att_v, 9)
            mm(ps[0:D, 0, :], lhsT=wq_sb[0:D, :], rhs=tok_t[0:D, :], start=True, stop=True)
            mm(ps[0:D, 1, :], lhsT=wk_sb[0:D, :], rhs=tok_t[0:D, :], start=True, stop=True)
            mm(ps[:, 3, :], lhsT=wv2_sb[0:D, :], rhs=tok_t[0:D, :], start=True, stop=True).then_inc(att_t, 1)
            pe.wait_ge(att_a, 1)
            pe.wait_ge(att_v, 10)
            for h in range(H):
                last = mm(ps[0:G, 2, h * G:(h + 1) * G], lhsT=q_t[0:D, h * G:(h + 1) * G],
                          rhs=k_t[0:D, h * G:(h + 1) * G], start=True, stop=True)
            last.then_inc(att_t, 1)
            pe.wait_ge(att_v, 12)
            for j in range(PAIRS):
                last = mm(ps[:, 4 + j // 2, (j % 2) * F:(j % 2 + 1) * F], lhsT=v_blk[:, j, :], rhs=wout_sb[:, j, :],
                          start=True, stop=True)
            last.then_inc(att_t, 1)
            pe.wait_ge(att_v, 17)
            for j in range(PAIRS):
                last = tr(ps[:, 6, j * G:(j + 1) * G], att[0:G, j * P:(j + 1) * P], ident[0:G, 0:G])
            last.then_inc(att_t, 1)
            pe.wait_ge(att_v, 19)
            for j in range(PAIRS):
                last = mm(ps[:, 4 + j // 2, (j % 2) * F:(j % 2 + 1) * F], lhsT=a_blk[:, j, :], rhs=vw[:, j, :],
                          start=True, stop=True)
            last.then_inc(att_t, 1)
            pe.wait_ge(att_v, 20)

            def project(t, s, i):
                pe.wait_ge(staged, t + 1)
                if past(t, UNROLL):
                    pe.wait_ge(y_ready, t - UNROLL + 1)
                for j in range(PAIRS):
                    last = mm(ps[:, s, 0:F], lhsT=stage[:, s, j * P:(j + 1) * P], rhs=m_blk[:, j, :],
                              start=(j == 0), stop=(j == PAIRS - 1))
                last.then_inc(y_psum, 1)

            run_steps(pe, project, TILES, 1, MLP_CHUNKS - 1)


_INS = ['x', 'dst', 'edge_attr_256', 'L0_gnn_W1', 'L0_gnn_b1', 'L0_gnn_W2', 'L0_gnn_b2', 'L0_gnn_W3', 'L0_gnn_b3',
        'L0_ffn_W_fx', 'L0_ffn_b_fx', 'L0_ffn_W_x', 'L0_ffn_b_x', 'L0_ffn_W_slice', 'L0_ffn_b_slice',
        'L0_ffn_W_q', 'L0_ffn_W_k', 'L0_ffn_W_v', 'L0_ffn_W_out', 'L0_ffn_b_out', 'L0_ffn_temperature']


def kernel(**inputs):
    import numpy as np
    import concourse.bacc as bacc
    from concourse.bass_utils import run_bass_kernel_spmd as run

    nc = bacc.Bacc("TRN2", target_bir_lowering=False, num_devices=1)
    arrays = {f"{n}_in": np.ascontiguousarray(inputs[n]) for n in _INS}
    args = [nc.dram_tensor(n, a.shape, mybir.dt.from_np(a.dtype), kind="ExternalInput").ap()
            for n, a in arrays.items()]
    out = nc.dram_tensor("result", inputs['x'].shape, F32, kind="ExternalOutput").ap()
    build(nc, *args, out)
    return run(nc, [arrays], core_ids=[0]).results[0]["result"]
```

```python
from contextlib import ExitStack

import concourse.bass as bass
from concourse import mybir

F32 = mybir.dt.float32
BF16 = mybir.dt.bfloat16
I32 = mybir.dt.int32
ALU = mybir.AluOpType
ACT = mybir.ActivationFunctionType
AX = mybir.AxisListType

P = 128
UNROLL = 4
WINDOW = 64
ROWS_PER_PART = 2
GROUP = P * ROWS_PER_PART
CHUNK_GROUPS = 4
SPLIT = 2
WHOLE = CHUNK_GROUPS - SPLIT
EPS_LN = 1e-5
EPS_NORM = 1e-5
CREDIT = 16


def past(t, n):
    return not isinstance(t, int) or t >= n


def before(t, n):
    return not isinstance(t, int) or t < n


def run_steps(eng, step, total, peel_front, loop_trips):
    first = peel_front * UNROLL
    for t in range(first):
        step(t, t % UNROLL, t // UNROLL)
    with eng.Fori(peel_front, peel_front + loop_trips) as i:
        for s in range(UNROLL):
            step(i * UNROLL + s, s, i)
    for t in range((peel_front + loop_trips) * UNROLL, total):
        step(t, t % UNROLL, t // UNROLL)


def build(nc, x, dst, edges, w1, b1, w2, b2, w3, b3, w_fx, b_fx, w_x, b_x, w_slice, b_slice,
          w_q, w_k, w_v, w_out, b_out, temperature, out):
    N, F = x.shape
    E = edges.shape[0]
    KF = F // P
    H = temperature.shape[1]
    D, G = w_slice.shape
    S = H * G
    PAIRS = S // P
    TILES = -(-N // P)
    NPAD = TILES * P
    LAST_ROWS = N - (TILES - 1) * P

    GROUPS = -(-E // GROUP)
    LAST_EDGES = E - (GROUPS - 1) * GROUP
    LAST_PARTS = LAST_EDGES // ROWS_PER_PART
    CHUNKS = -(-GROUPS // CHUNK_GROUPS)
    CHUNK_EDGES = CHUNK_GROUPS * GROUP
    FULL_CHUNKS = E // CHUNK_EDGES
    TAIL_GROUPS = GROUPS - FULL_CHUNKS * CHUNK_GROUPS
    EDGE_TRIPS = FULL_CHUNKS // UNROLL
    GTILES = -(-GROUPS // P)
    FULL_GTILES = GROUPS // P
    WIDE = 488
    WIDES = -(-(N + WINDOW) // WIDE)
    AGG = WIDE * WIDES
    SCALE = float(D) ** -0.5
    assert F == KF * P and P == 2 * G and D == G and S == 512 and AGG >= N + WINDOW
    assert LAST_EDGES % ROWS_PER_PART == 0 and 2 * EDGE_TRIPS == TILES - 1
    MLP_CHUNKS = (TILES - 1) // 4

    with ExitStack() as ctx:
        def sb(name, shape, dt=F32):
            return ctx.enter_context(nc.sbuf_tensor(name, shape, dt))

        def sem(name):
            return ctx.enter_context(nc.semaphore(name))

        x_sb = sb("x_sb", [P, TILES, F])
        big = sb("big", [P, KF * AGG + KF * NPAD])
        agg = big[:, 0:KF * AGG].rearrange("p (h n) -> p h n", h=KF)
        h1x = big[:, KF * AGG:].rearrange("p (h n) -> p h n", h=KF)
        sw_t = big[:, 0:PAIRS * NPAD].rearrange("p (j n) -> p j n", j=PAIRS)
        tmp = big[:, KF * AGG:]
        dst_f = tmp[:, 0:1024].rearrange("p (t e) -> p t e", t=GTILES)
        rel_g = tmp[:, 1024:2048].rearrange("p (t e) -> p t e", t=GTILES)
        dst_i = tmp[:, 5000:6024].bitcast(I32).rearrange("p (t e) -> p t e", t=GTILES)

        ring_mem = sb("ring_mem", [P, UNROLL * CHUNK_GROUPS * ROWS_PER_PART * F])
        ring = ring_mem[:, :].rearrange("p (s g k f) -> p s g k f", s=UNROLL, g=CHUNK_GROUPS, k=ROWS_PER_PART)

        def part(start, size):
            return ring_mem[:, start:start + size]

        h1_t = part(0, 1024).rearrange("p (m n) -> p m n", m=KF)
        h2_t = part(1024, 1024).rearrange("p (m n) -> p m n", m=KF)
        wfx_sb = part(2048, 1024).rearrange("p (k n) -> p k n", k=KF)
        wout_sb = part(3072, 1024).rearrange("p (j n) -> p j n", j=PAIRS)
        bout_bc = part(4096, 256)
        bfx_bc = part(4352, 256).rearrange("p (j c) -> p j c", j=PAIRS)
        wq_sb = part(4608, 64)
        wk_sb = part(4672, 64)
        wv2_sb = part(4736, 128)
        sw_sum = part(4864, 512)
        soft = part(5376, 2048).rearrange("p (b n) -> p b n", b=UNROLL)
        xn_t = part(7424, 512).rearrange("p (b k n) -> p b k n", b=2, k=KF)
        b3_bc = sw_sum[:, 0:F]
        s_t = part(0, 1024).rearrange("p (k n) -> p k n", k=KF)
        tok = part(1024, 256).rearrange("p (j c) -> p j c", j=PAIRS)
        nb = part(1280, 256).rearrange("p (j c) -> p j c", j=PAIRS)
        norm = part(7936, 4)
        rnorm = part(7940, 4)
        att_mx = part(7944, 8)
        att_sm = part(7952, 8)
        att_rc = part(7960, 8)
        tok_t = part(1536, 512)
        q_t = part(5376, 512)
        k_t = part(5888, 512)
        v_blk = part(6400, 512).rearrange("p (j n) -> p j n", j=PAIRS)
        att = part(6912, 512)
        a_blk = part(7424, 512).rearrange("p (j n) -> p j n", j=PAIRS)
        stage = soft
        o_sb = h1_t.rearrange("p m n -> p (m n)").rearrange("p (b f) -> p b f", b=UNROLL)

        SPL = SPLIT * ROWS_PER_PART
        HOT = WHOLE * ROWS_PER_PART
        hot_f = sb("hot_f", [P, 2, HOT, WINDOW])
        hot_b = sb("hot_b", [P, 2, SPL, WINDOW], BF16)
        split_mem = sb("split_mem", [P, 3072])
        rest = split_mem[:, 0:2048].rearrange("p (b k f) -> p b k f", b=2, k=SPL)
        low = split_mem[:, 2048:3072].bitcast(BF16).rearrange("p (b k f) -> p b k f", b=2, k=SPL)
        wc = split_mem[:, 0:1024].rearrange("p (k n) -> p k n", k=KF)
        c_bc = split_mem[:, 1024:1536]
        w1b_sb = split_mem[:, 1536:2048].rearrange("p (k n) -> p k n", k=KF)
        m_blk = split_mem[:, 2048:3072].rearrange("p (j n) -> p j n", j=PAIRS)

        w2_sb = part(5376, 512).rearrange("p (k n) -> p k n", k=KF)
        w3_sb = part(5888, 512).rearrange("p (k n) -> p k n", k=KF)
        xn = sb("xn", [P, UNROLL, F])
        xo = xn
        vw = xn[:, :, :]
        ln_t = sb("ln_t", [P, KF, 2 * P])
        w1a_sb = sb("w1a_sb", [P, KF, F])
        wx = xn[:, :, :].rearrange("p b f -> p (b f)").rearrange("p (k n) -> p k n", k=KF)
        wx_t = part(6400, 1024).rearrange("p (k j n) -> p k j n", k=KF, j=PAIRS)
        bx_rep = part(7424, 512).rearrange("p (j n) -> p j n", j=PAIRS)
        tmp2 = ln_t[:, :, :].rearrange("p k n -> p (k n)")
        blk_s = tmp2[:, 0:128]
        bx_col = tmp2[:, 128:132]
        bsl_bc = tmp2[:, 132:196]
        temp_bc = tmp2[:, 196:204]
        inv_temp = tmp2[:, 204:212]
        ident = sb("ident", [P, P])
        ones = sb("ones", [P, 1])
        iota_w = sb("iota_w", [P, WINDOW])
        rel = sb("rel", [P, CHUNKS * CHUNK_GROUPS, ROWS_PER_PART])
        base_i = xn[:, 2:4, :].rearrange("p b f -> p (b f)").bitcast(I32)
        base_col = sb("base_col", [P, GTILES])
        far_col = sb("far_col", [P, GTILES])
        far_one = sb("far_one", [P, 1])
        far_i = sb("far_i", [1, 2], I32)
        b1_sb = sb("b1_sb", [P, KF])
        b2_sb = sb("b2_sb", [P, KF])
        half = sb("half", [P, UNROLL])
        row_no = sb("row_no", [P, 1])
        row_ok = sb("row_ok", [P, 1])
        bn6 = sb("bn6", [P, UNROLL, 6])
        mv1 = sb("mv1", [P, 2, 2])
        var_e = sb("var_e", [P, UNROLL])
        rstd1 = sb("rstd1", [P, 2])
        mv4 = sb("mv4", [P, UNROLL, 2])
        eps = sb("eps", [P, UNROLL])
        mean2 = sb("mean2", [P, TILES])
        rstd2 = sb("rstd2", [P, TILES])
        carrier = sb("carrier", [P, 1])
        mx = sb("mx", [P, UNROLL, H])
        sm = sb("sm", [P, UNROLL, H])
        rc = sb("rc", [P, UNROLL, H])
        g_iota = part(2048, 512)
        g_hot = part(2560, 1024).rearrange("p (k n) -> p k n", k=ROWS_PER_PART)
        g_dst = part(3600, 2).bitcast(I32)
        g_abs = part(3604, 2)
        g_cov = part(3608, 2)
        g_win = part(3612, 2)

        ps = ctx.enter_context(nc.psum_tensor("ps", [P, 8, 512], F32))

        dst_in = sem("dst_in")
        edge_in = [sem(f"edge_in{s}") for s in range(UNROLL)]
        x_in = sem("x_in")
        x_tail_in = sem("x_tail_in")
        fold_in = sem("fold_in")
        mlp_in = sem("mlp_in")
        w23_in = sem("w23_in")
        late_in = sem("late_in")
        dst_clear = sem("dst_clear")
        consts = sem("consts")
        x_clear = sem("x_clear")
        blk_clear = sem("blk_clear")
        agg_clear = sem("agg_clear")
        prep_v = sem("prep_v")
        prep_t = sem("prep_t")
        fold_v = sem("fold_v")
        fold_t = sem("fold_t")
        w1b_in = sem("w1b_in")
        rest_ready = sem("rest_ready")
        low_ready = sem("low_ready")
        hot_ready = sem("hot_ready")
        sums_ready = sem("sums_ready")
        groups_added = sem("groups_added")
        bn_done = sem("bn_done")
        mv1_ready = sem("mv1_ready")
        var1_ready = sem("var1_ready")
        rstd1_ready = sem("rstd1_ready")
        xn1_ready = sem("xn1_ready")
        ln_tp = sem("ln_tp")
        ln_t_ready = sem("ln_t_ready")
        h1x_psum = sem("h1x_psum")
        h1x_ready = sem("h1x_ready")
        xb3_ready = sem("xb3_ready")
        b3_in = sem("b3_in")
        edges_done = sem("edges_done")
        gen_e_in = sem("gen_e_in")
        gen_d_in = sem("gen_d_in")
        gen_v = sem("gen_v")
        gen_hot = sem("gen_hot")
        gen_sums = sem("gen_sums")
        gen_group = sem("gen_group")
        l1_psum = sem("l1_psum")
        h1_sum = sem("h1_sum")
        h1_ready = sem("h1_ready")
        l2_psum = sem("l2_psum")
        h2_ready = sem("h2_ready")
        l3_psum = sem("l3_psum")
        x2_ready = sem("x2_ready")
        bn2_done = sem("bn2_done")
        mv2_ready = sem("mv2_ready")
        mean2_ready = sem("mean2_ready")
        var2_ready = sem("var2_ready")
        rstd2_ready = sem("rstd2_ready")
        xn2_ready = sem("xn2_ready")
        tp_ready = sem("tp_ready")
        xn_t_ready = sem("xn_t_ready")
        logits_ready = sem("logits_ready")
        biased = sem("biased")
        max_ready = sem("max_ready")
        shifted = sem("shifted")
        exp_ready = sem("exp_ready")
        total_ready = sem("total_ready")
        recip_ready = sem("recip_ready")
        sw_ready = sem("sw_ready")
        xn_used = sem("xn_used")
        sw_tp = sem("sw_tp")
        sw_t_ready = sem("sw_t_ready")
        sw_summed = sem("sw_summed")
        sw_sum_clear = sem("sw_sum_clear")
        att_v = sem("att_v")
        att_t = sem("att_t")
        att_a = sem("att_a")
        att_clear = sem("att_clear")
        staged = sem("staged")
        xo_ready = sem("xo_ready")
        y_psum = sem("y_psum")
        y_ready = sem("y_ready")
        y_out = [sem(f"y_out{q}") for q in range(2)]

        block = ctx.enter_context(nc.Block())

        def upper(v):
            return v.bitcast(BF16)[:, 1::2]

        def tiles_of(t0, n):
            return x_sb[:, bass.ds(t0, n), :]

        @block.sync
        def _(sp):
            full = FULL_GTILES * P * GROUP
            sp.dma_start(dst_i[:, 0:FULL_GTILES, :],
                         dst[0:full].rearrange("(t p e) -> p t e", p=P, e=GROUP)).then_inc(dst_in, 16)
            sp.wait_ge(dst_clear, 1)
            whole = GROUPS - 1 - FULL_GTILES * P
            sp.dma_start(dst_i[0:whole, FULL_GTILES, :],
                         dst[full:full + whole * GROUP].rearrange("(p e) -> p e", e=GROUP)).then_inc(dst_in, 16)
            row = dst.rearrange("(a e) -> a e", a=1)
            sp.dma_start(dst_i[whole:whole + 1, FULL_GTILES, 0:LAST_EDGES],
                         row[:, E - LAST_EDGES:E]).then_inc(dst_in, 16)
            sp.dma_start(dst_i[whole:whole + 1, FULL_GTILES, LAST_EDGES:GROUP],
                         row[:, E - (GROUP - LAST_EDGES):E]).then_inc(dst_in, 16)

            def chunk(c, s, i):
                if past(c, UNROLL):
                    sp.wait_ge(sums_ready, c - UNROLL + 1)
                if before(c, FULL_CHUNKS):
                    sp.dma_start(ring[:, s].rearrange("p g k f -> p g (k f)"),
                                 edges[bass.ds(c * CHUNK_EDGES, CHUNK_EDGES), :].rearrange(
                                     "(g p k) f -> p g (k f)", p=P, k=ROWS_PER_PART)).then_inc(edge_in[s], 16)
                else:
                    e0 = FULL_CHUNKS * CHUNK_EDGES
                    e1 = (GROUPS - 1) * GROUP
                    sp.dma_start(ring[:, s, 0:TAIL_GROUPS - 1].rearrange("p g k f -> p g (k f)"),
                                 edges[e0:e1, :].rearrange("(g p k) f -> p g (k f)", p=P,
                                                           k=ROWS_PER_PART)).then_inc(edge_in[s], 16)
                    sp.dma_start(ring[0:LAST_PARTS, s, TAIL_GROUPS - 1].rearrange("p k f -> p (k f)"),
                                 edges[e1:E, :].rearrange("(p k) f -> p (k f)",
                                                          k=ROWS_PER_PART)).then_inc(edge_in[s], 16)
                if s == 0 and before(c, FULL_CHUNKS - 1):
                    if past(c, UNROLL):
                        sp.wait_ge(x_in, i * 16)
                    sp.dma_start(tiles_of(i * 2, 2),
                                 x[bass.ds(i * (2 * P), 2 * P), :].rearrange("(t p) f -> p t f", p=P)
                                 ).then_inc(x_in, 16)

            run_steps(sp, chunk, CHUNKS, 1, EDGE_TRIPS - 1)
            sp.wait_ge(x_clear, 1)
            sp.dma_start(x_sb[0:LAST_ROWS, TILES - 1, :], x[(TILES - 1) * P:N, :]).then_inc(x_tail_in, 16)

            sp.wait_ge(edges_done, 1)
            far = sp.value_load(far_i[0:1, 0:1], min_val=0, max_val=1)

            def reload(g, parts):
                sp.wait_ge(gen_group, g + 1)
                rows = bass.ds(g * GROUP, parts * ROWS_PER_PART)
                sp.dma_start(ring[0:parts, 0, 0].rearrange("p k f -> p (k f)"),
                             edges[rows, :].rearrange("(p k) f -> p (k f)", k=ROWS_PER_PART)).then_inc(gen_e_in, 16)
                sp.dma_start(g_dst[0:parts, :],
                             dst[rows].rearrange("(p k) -> p k", k=ROWS_PER_PART)).then_inc(gen_d_in, 16)

            with sp.If(far > 0):
                with sp.Fori(0, GROUPS - 1) as g:
                    reload(g, P)
                reload(GROUPS - 1, LAST_PARTS)

            sp.wait_ge(edges_done, 2)
            sp.dma_start(w1b_sb, w1[F:2 * F, :].rearrange("(k p) n -> p k n", p=P)).then_inc(w1b_in, 16)
            sp.dma_start(b3_bc, b3.rearrange("(a n) -> a n", a=1).broadcast_to([P, F])).then_inc(b3_in, 16)
            sp.dma_start(w2_sb, w2.rearrange("(k p) n -> p k n", p=P)).then_inc(w23_in, 16)
            sp.dma_start(w3_sb, w3.rearrange("(k p) n -> p k n", p=P)).then_inc(w23_in, 16)
            sp.wait_ge(h1x_ready, 2 * (EDGE_TRIPS + 1))
            sp.dma_start(wx, w_x.rearrange("(k p) n -> p k n", p=P)).then_inc(fold_in, 16)
            sp.dma_start(bx_col, b_x.rearrange("(j p) -> p j", p=P), allow_slow_non_contiguous=True).then_inc(fold_in, 16)
            sp.dma_start(bsl_bc, b_slice.rearrange("(a g) -> a g", a=1).broadcast_to([P, G])).then_inc(fold_in, 16)
            sp.dma_start(temp_bc, temperature.rearrange("a h b c -> a (h b c)").broadcast_to([P, H])
                         ).then_inc(fold_in, 16)
            sp.wait_ge(blk_clear, 1)
            for hh in range(2):
                sp.dma_start(blk_s[hh * D:(hh + 1) * D, hh * G:(hh + 1) * G], w_slice).then_inc(fold_in, 16)
            sp.dma_start(wfx_sb, w_fx.rearrange("(k p) n -> p k n", p=P)).then_inc(late_in, 16)
            sp.dma_start(wout_sb, w_out.rearrange("(j p) n -> p j n", p=P)).then_inc(late_in, 16)
            sp.dma_start(bout_bc, b_out.rearrange("(a n) -> a n", a=1).broadcast_to([P, F])).then_inc(late_in, 16)
            bfx = b_fx.rearrange("(j h c) -> h j c", h=2, c=D)
            for hh in range(2):
                sp.dma_start(bfx_bc[hh * G:(hh + 1) * G], bfx[hh:hh + 1].broadcast_to([G, PAIRS, D])
                             ).then_inc(late_in, 16)
                sp.dma_start(wv2_sb[0:D, hh * D:(hh + 1) * D], w_v).then_inc(late_in, 16)
            sp.dma_start(wq_sb[0:D, :], w_q).then_inc(late_in, 16)
            sp.dma_start(wk_sb[0:D, :], w_k).then_inc(late_in, 16)

            def store(t, s, i):
                if s % 2 == 1:
                    sp.wait_ge(y_ready, t + 1)
                    sp.dma_start(out[bass.ds((t - 1) * P, 2 * P), :].rearrange("(t p) f -> p t f", p=P),
                                 o_sb[:, s - 1:s + 1, :]).then_inc(y_out[s // 2], 16)
                elif isinstance(t, int) and t == TILES - 1:
                    sp.wait_ge(y_ready, TILES)
                    sp.dma_start(out[t * P:N, :], o_sb[0:LAST_ROWS, s, :]).then_inc(y_out[0], 16)

            run_steps(sp, store, TILES, 0, MLP_CHUNKS)
            sp.wait_ge(y_out[0], 16 * (MLP_CHUNKS + 1))
            sp.wait_ge(y_out[1], 16 * MLP_CHUNKS)

        @block.gpsimd
        def _(pool):
            pool.memset(dst_i[:, FULL_GTILES, :], 0).then_inc(dst_clear, 1)
            pool.memset(ident[:, :], 0.0).then_inc(consts, 1)
            pool.wait_ge(consts, 1)
            pool.affine_select(out=ident[:, :], in_=ident[:, :], compare_op=ALU.not_equal, fill=1.0, base=0,
                               pattern=[[-1, P]], channel_multiplier=1).then_inc(consts, 1)
            pool.iota(iota_w[:, :], [[1, WINDOW]], base=0, channel_multiplier=0,
                      allow_small_or_imprecise_dtypes=True).then_inc(consts, 1)
            pool.memset(half[:, :], -0.5).then_inc(consts, 1)
            pool.memset(eps[:, :], EPS_LN).then_inc(consts, 1)
            pool.memset(ones[:, :], 1.0).then_inc(consts, 1)
            pool.iota(row_no[:, :], [[0, 1]], base=0, channel_multiplier=1,
                      allow_small_or_imprecise_dtypes=True).then_inc(consts, 1)
            pool.memset(agg[:, 1, :], 0.0).then_inc(agg_clear, 1)
            pool.memset(x_sb[:, TILES - 1, :], 0.0).then_inc(x_clear, 1)
            pool.wait_ge(consts, 7)

            def rstd(mv, dest, n, ready, tiles_ready, step_sem, done, count):
                pool.wait_ge(ready, tiles_ready)
                pool.tensor_tensor(var_e[:, 0:n], mv, eps[:, 0:n], ALU.add).then_inc(step_sem, 1)
                pool.wait_ge(step_sem, count)
                pool.tensor_tensor(dest, var_e[:, 0:n], half[:, 0:n], ALU.pow).then_inc(done, 1)


            def ln_pair(i, n):
                rstd(mv1[:, 0:n, 1], rstd1[:, 0:n], n, mv1_ready, i * 2 + n, var1_ready, rstd1_ready, i + 1)

            def low_part(c, b, parts, rows):
                pool.wait_ge(rest_ready, c + 1)
                if past(c, 2):
                    pool.wait_ge(sums_ready, c - 1)
                v = rest[0:parts, b, 0:rows, :].rearrange("p k f -> p (k f)")
                pool.tensor_tensor(low[0:parts, b, 0:rows, :].rearrange("p k f -> p (k f)"), v, upper(v),
                                   ALU.subtract).then_inc(low_ready, 1)

            def chunk(c, s, i):
                if before(c, FULL_CHUNKS - 2):
                    low_part(c + 2, s % 2, P, SPL)
                elif c == FULL_CHUNKS - 2:
                    low_part(c + 2, s % 2, LAST_PARTS, (TAIL_GROUPS - WHOLE) * ROWS_PER_PART)
                if s == 1 and before(c, FULL_CHUNKS - 1):
                    ln_pair(i, 2)

            low_part(0, 0, P, SPL)
            low_part(1, 1, P, SPL)
            run_steps(pool, chunk, CHUNKS, 0, EDGE_TRIPS - 1)
            ln_pair(EDGE_TRIPS, 1)

            pool.wait_ge(h1x_ready, 2 * (EDGE_TRIPS + 1))
            pool.memset(blk_s, 0.0).then_inc(blk_clear, 1)
            pool.wait_ge(edges_done, 2)
            pool.wait_ge(b3_in, 16)

            def add_b3(i, n):
                pool.tensor_tensor(tiles_of(i * 4, n), tiles_of(i * 4, n),
                                   b3_bc.unsqueeze(1).broadcast_to([P, n, F]), ALU.add).then_inc(xb3_ready, 1)

            def rstd_chunk(i, n):
                rstd(mv4[:, 0:n, 1], rstd2[:, bass.ds(i * 4, n)], n, mv2_ready, i * 4 + n, var2_ready,
                     rstd2_ready, i + 1)

            add_b3(0, 4)
            add_b3(1, 4)
            rstd_chunk(0, 4)
            with pool.Fori(1, MLP_CHUNKS - 1) as i:
                add_b3(i + 1, 4)
                pool.wait_ge(rstd2_ready, i)
                rstd_chunk(i, 4)
            add_b3(MLP_CHUNKS, 1)
            pool.wait_ge(rstd2_ready, MLP_CHUNKS - 1)
            rstd_chunk(MLP_CHUNKS - 1, 4)
            pool.wait_ge(rstd2_ready, MLP_CHUNKS)
            rstd_chunk(MLP_CHUNKS, 1)

            pool.wait_ge(xb3_ready, MLP_CHUNKS + 1)
            pool.memset(sw_sum, 0.0).then_inc(sw_summed, 1)

            def soft_step(t, s, i):
                if before(t, TILES):
                    pool.wait_ge(max_ready, t + 1)
                    v = soft[:, s, :].rearrange("p (h g) -> p h g", h=H)
                    pool.tensor_tensor(v, v, mx[:, s, :].unsqueeze(2).broadcast_to([P, H, G]),
                                       ALU.subtract).then_inc(shifted, 1)
                if past(t, 1) and before(t, TILES + 1):
                    pool.wait_ge(sw_ready, t)
                    pool.wait_ge(sw_summed, t)
                    pool.tensor_tensor(sw_sum, sw_sum, soft[:, (s - 1) % UNROLL, :], ALU.add).then_inc(sw_summed, 1)

            run_steps(pool, soft_step, TILES + 1, 1, (TILES - 1) // UNROLL - 1)

            pool.wait_ge(sw_tp, TILES)
            pool.wait_ge(sw_summed, TILES + 1)
            pool.memset(v_blk, 0.0).then_inc(att_clear, 1)
            pool.memset(a_blk, 0.0).then_inc(att_clear, 1)

            pool.wait_ge(late_in, 16 * 9)
            pool.wait_ge(att_t, 8)

            def residual(t, s, i):
                if past(t, UNROLL):
                    pool.wait_ge(y_ready, t - UNROLL + 1)
                pool.tensor_tensor(xo[:, s, :], x_sb[:, bass.ds(t, 1), :].rearrange("p a f -> p (a f)"),
                                   bout_bc, ALU.add).then_inc(xo_ready, 1)

            run_steps(pool, residual, TILES, 1, MLP_CHUNKS - 1)

        @block.scalar
        def _(act):
            act.dma_start(w1a_sb[:, :, :], w1[0:F, :].rearrange("(k p) n -> p k n", p=P)).then_inc(mlp_in, 16)
            act.dma_start(b1_sb[:, :], b1.rearrange("(m p) -> p m", p=P), allow_slow_non_contiguous=True).then_inc(mlp_in, 16)
            act.dma_start(b2_sb[:, :], b2.rearrange("(m p) -> p m", p=P), allow_slow_non_contiguous=True).then_inc(mlp_in, 16)
            act.wait_ge(mlp_in, 16 * 3)

            def ln_pair(i, n):
                act.wait_ge(ln_tp, i + 1)
                act.activation(ln_t[:, :, 0:n * P], ps[:, 4, :].rearrange("p (k c) -> p k c", k=KF)[:, :, 0:n * P],
                               ACT.Copy).then_inc(ln_t_ready, 1)
                for m in range(KF):
                    act.wait_ge(h1x_psum, i * 2 + (m + 1))
                    act.activation(h1x[:, m, bass.ds(i * 2 * P, n * P)], ps[:, 5, m * 256:m * 256 + n * P],
                                   ACT.Identity, bias=b1_sb[:, m:m + 1]).then_inc(h1x_ready, 1)

            with act.Fori(0, EDGE_TRIPS) as i:
                ln_pair(i, 2)
            ln_pair(EDGE_TRIPS, 1)

            def relus(i, cols):
                act.wait_ge(h1_sum, i + 1)
                act.activation(h1_t[:, :, 0:cols], h1_t[:, :, 0:cols], ACT.Relu).then_inc(h1_ready, 1)
                act.wait_ge(l2_psum, i + 1)
                for m in range(KF):
                    act.activation(h2_t[:, m, 0:cols], ps[:, 2 + m, 0:cols], ACT.Relu,
                                   bias=b2_sb[:, m:m + 1]).then_inc(h2_ready, 1)

            with act.Fori(0, MLP_CHUNKS) as i:
                relus(i, 4 * P)
            relus(MLP_CHUNKS, P)

            def copy_xn_t(t, b):
                act.wait_ge(tp_ready, t + 1)
                act.activation(xn_t[:, b], ps[:, 2 + b, 0:2 * P].rearrange("p (k n) -> p k n", k=KF),
                               ACT.Copy).then_inc(xn_t_ready, 1)

            def soft_step(t, s, i):
                if past(t, 3):
                    act.wait_ge(sw_tp, t - 2)
                    act.activation(sw_t[:, :, bass.ds((t - 3) * P, P)],
                                   ps[:, 6 + (s - 3) % 2, :].rearrange("p (j n) -> p j n", j=PAIRS),
                                   ACT.Copy).then_inc(sw_t_ready, 1)
                if before(t, TILES - 1):
                    if past(t, 1):
                        act.wait_ge(logits_ready, t)
                    copy_xn_t(t + 1, (s + 1) % 2)
                if before(t, TILES):
                    act.wait_ge(shifted, t + 1)
                    act.activation(soft[:, s, :], soft[:, s, :], ACT.Exp).then_inc(exp_ready, 1)

            copy_xn_t(0, 0)
            run_steps(act, soft_step, TILES + 3, 2, (TILES - 1) // UNROLL - 2)

            act.wait_ge(att_clear, 1)
            act.wait_ge(att_t, 4)
            act.activation(q_t[0:D, :], ps[0:D, 0, :], ACT.Copy, scale=SCALE).then_inc(att_a, 1)
            act.wait_ge(att_v, 13)
            act.activation(att[0:G, :], att[0:G, :], ACT.Exp).then_inc(att_a, 1)

            def stage_step(t, s, i):
                if past(t, UNROLL):
                    act.wait_ge(y_psum, t - UNROLL + 1)
                act.activation(stage[:, s, :].rearrange("p (j n) -> p j n", j=PAIRS),
                               sw_t[:, :, bass.ds(t * P, P)], ACT.Copy).then_inc(staged, 1)

            act.wait_ge(att_t, 8)
            run_steps(act, stage_step, TILES, 1, MLP_CHUNKS - 1)

        @block.vector
        def _(dve):
            done = [0]

            def then(ins):
                ins.then_inc(prep_v, 1)
                done[0] += 1
                return done[0]

            dve.memset(agg[:, 0, :], 0.0).then_inc(agg_clear, 1)
            dve.wait_ge(dst_in, 16 * 4)
            dve.wait_ge(prep_v, then(dve.tensor_copy(dst_f, dst_i)))
            dve.wait_ge(prep_v, then(dve.tensor_reduce(base_col[:, :], dst_f, AX.X, ALU.min)))
            dve.wait_ge(prep_v, then(dve.tensor_scalar(base_col[:, :], base_col[:, :], 0.0, float(N), ALU.max, ALU.min)))
            for t in range(GTILES):
                n = then(dve.tensor_scalar(rel_g[:, t, :], dst_f[:, t, :], base_col[:, t:t + 1], None, ALU.subtract))
            dve.wait_ge(prep_v, n)
            dve.wait_ge(prep_v, then(dve.tensor_reduce(far_col[:, :], rel_g, AX.X, ALU.max)))
            then(dve.tensor_reduce(far_one[:, :], far_col[:, :], AX.X, ALU.max))
            dve.wait_ge(prep_t, 1)
            for k in range(ROWS_PER_PART):
                for t in range(GTILES):
                    n = min(P, CHUNKS * CHUNK_GROUPS - t * P)
                    then(dve.tensor_copy(rel[:, t * P:t * P + n, k], ps[:, 6 + k, t * P:t * P + n]))
            dve.wait_ge(prep_t, 2)
            then(dve.tensor_copy(base_i[0:1, :], ps[0:1, 5, :]))
            dve.wait_ge(prep_v, then(dve.tensor_reduce(far_col[0:1, 0:1], ps[0:1, 4, 0:P], AX.X, ALU.max)))
            table = then(dve.tensor_scalar(far_i[0:1, 0:1], far_col[0:1, 0:1], float(WINDOW), None, ALU.is_ge))
            dve.wait_ge(prep_v, table)
            dve.wait_ge(agg_clear, 2)
            dve.wait_ge(consts, 7)
            dve.tensor_scalar(row_ok[:, :], row_no[:, :], float(LAST_ROWS), None, ALU.is_lt).then_inc(groups_added, CREDIT)

            base_regs = [dve.alloc_register(f"base{n}") for n in range(UNROLL * CHUNK_GROUPS)]
            base_of = [None] * len(base_regs)

            def one_hot(dest, c, first, n, done):
                where = rel[:, bass.ds(c * CHUNK_GROUPS + first, n), :].rearrange("p g k -> p (g k)")
                shape = [P, n * ROWS_PER_PART, WINDOW]
                dve.tensor_tensor(dest, iota_w[:, :].unsqueeze(1).broadcast_to(shape),
                                  where.unsqueeze(2).broadcast_to(shape), ALU.is_equal).then_inc(done, 1)

            def hot_whole(c, b):
                one_hot(hot_f[:, b], c, 0, WHOLE, hot_ready)

            def hot_parts(c, b):
                one_hot(hot_b[:, b], c, WHOLE, SPLIT, hot_ready)

            def c_buf(s):
                return s % 2

            def split_rest(c, s, i, parts, rows, loads):
                dve.wait_ge(edge_in[s], i * 16 + loads * 16)
                v = ring[0:parts, s, WHOLE:, :, :].rearrange("p g k f -> p (g k f)")[:, 0:rows * F]
                dve.tensor_tensor(rest[0:parts, c_buf(s), 0:rows, :].rearrange("p k f -> p (k f)"), v, upper(v),
                                  ALU.subtract).then_inc(rest_ready, 1)

            def norm_stats(i, a):
                dve.bn_stats(bn6[:, a, :], x_sb[:, bass.ds(i * 2 + a, 1), :].rearrange("p a f -> p (a f)")
                             ).then_inc(bn_done, 1)

            def norm_sums(i, n):
                dve.wait_ge(bn_done, i * 2 + n)
                dve.tensor_copy(carrier[:, :], bn6[:, 0, 0:1])
                for a in range(n):
                    dve.bn_aggr(mv1[:, a, :], bn6[:, a, :]).then_inc(mv1_ready, 1)

            def norm_rows(i, a):
                dve.wait_ge(rstd1_ready, i + 1)
                dve.tensor_scalar(xn[:, a, :], x_sb[:, bass.ds(i * 2 + a, 1), :].rearrange("p a f -> p (a f)"),
                                  mv1[:, a, 0:1], rstd1[:, a:a + 1], ALU.subtract, ALU.mult).then_inc(xn1_ready, 1)

            def chunk(c, s, i):
                if s == 0:
                    dve.load(base_regs, base_i[0:1, bass.ds(i * (UNROLL * CHUNK_GROUPS), UNROLL * CHUNK_GROUPS)])
                    for n, r in enumerate(base_regs):
                        base_of[n] = dve.snap(r, min_val=0, max_val=N)
                dve.wait_ge(sums_ready, c + 1)
                ahead = []
                if before(c, FULL_CHUNKS - 2):
                    trip = i if s < 2 else i + 1
                    ahead.append(lambda: split_rest(c + 2, (s + 2) % UNROLL, trip, P, SPL, 1))
                elif c == FULL_CHUNKS - 2:
                    ahead.append(lambda: split_rest(c + 2, (s + 2) % UNROLL, (c + 2) // UNROLL, LAST_PARTS,
                                                    (TAIL_GROUPS - WHOLE) * ROWS_PER_PART, 2))
                if before(c, CHUNKS - 2):
                    ahead.append(lambda: hot_whole(c + 2, s % 2))
                    ahead.append(lambda: hot_parts(c + 2, s % 2))
                for g in range(CHUNK_GROUPS if before(c, FULL_CHUNKS) else TAIL_GROUPS):
                    dve.wait_ge(groups_added, c * CHUNK_GROUPS + (CREDIT + g))
                    win = agg[:, :, bass.ds(base_of[s * CHUNK_GROUPS + g], WINDOW)]
                    dve.tensor_tensor(win, win, ps[:, s, g * P:(g + 1) * P].rearrange("p (h n) -> p h n", h=KF),
                                      ALU.add).then_inc(groups_added, 1)
                    if ahead:
                        ahead.pop(0)()
                if before(c, FULL_CHUNKS - 1):
                    if s == 0:
                        dve.wait_ge(x_in, i * 16 + 16)
                    if s < 2:
                        norm_stats(i, s)
                    if s == 1:
                        norm_sums(i, 2)
                    if s >= 2:
                        norm_rows(i, s - 2)

            for c in range(2):
                hot_whole(c, c)
                split_rest(c, c, 0, P, SPL, 1)
                hot_parts(c, c)
            run_steps(dve, chunk, CHUNKS, 0, EDGE_TRIPS - 1)
            dve.wait_ge(x_tail_in, 16)
            norm_stats(EDGE_TRIPS, 0)
            norm_sums(EDGE_TRIPS, 1)
            dve.wait_ge(ln_tp, EDGE_TRIPS)
            norm_rows(EDGE_TRIPS, 0)
            dve.wait_ge(groups_added, CREDIT + GROUPS)
            dve.drain().then_inc(edges_done, 1)

            far = dve.value_load(far_i[0:1, 0:1], min_val=0, max_val=1)
            with dve.If(far > 0):
                for n in range(512 // WINDOW):
                    dve.tensor_scalar(g_iota[:, n * WINDOW:(n + 1) * WINDOW], iota_w[:, :], float(n * WINDOW), None,
                                      ALU.add).then_inc(gen_v, 1)
                dve.wait_ge(gen_v, 8)
                dve.drain().then_inc(gen_group, 1)
                PER_GROUP = 3 + WIDES

                def far_group(g, parts):
                    step = g * PER_GROUP + 8
                    dve.wait_ge(gen_d_in, g * 16 + 16)
                    dve.tensor_copy(g_abs[0:parts, :], g_dst[0:parts, :]).then_inc(gen_v, 1)
                    dve.tensor_scalar(g_cov[0:parts, :], rel[0:parts, bass.ds(g, 1), :].rearrange("p g k -> p (g k)"),
                                      float(WINDOW), float(4 * AGG), ALU.is_lt, ALU.mult).then_inc(gen_v, 1)
                    dve.wait_ge(gen_v, step + 2)
                    dve.tensor_tensor(g_abs[0:parts, :], g_abs[0:parts, :], g_cov[0:parts, :], ALU.add).then_inc(gen_v, 1)
                    for w in range(WIDES):
                        dve.wait_ge(gen_v, step + (3 + w))
                        dve.tensor_scalar(g_win[0:parts, :], g_abs[0:parts, :], float(w * WIDE), None,
                                          ALU.subtract).then_inc(gen_v, 1)
                        dve.wait_ge(gen_v, step + (4 + w))
                        for k in range(ROWS_PER_PART):
                            dve.tensor_scalar(g_hot[0:parts, k, :], g_iota[0:parts, :], g_win[0:parts, k:k + 1], None,
                                              ALU.is_equal).then_inc(gen_hot, 1)
                        dve.wait_ge(gen_sums, g * WIDES + (w + 1))
                        view = agg[:, :, w * WIDE:(w + 1) * WIDE]
                        last = dve.tensor_tensor(view, view, ps[:, 0:2, 0:WIDE], ALU.add)
                        last.then_inc(groups_added, 1)
                        dve.wait_ge(groups_added, g * WIDES + (CREDIT + GROUPS + w + 1))
                    dve.memset(g_cov, 0.0).then_inc(gen_group, 1)

                with dve.Fori(0, GROUPS - 1) as g:
                    far_group(g, P)
                far_group(GROUPS - 1, LAST_PARTS)
            dve.drain().then_inc(edges_done, 1)

            def add_h1(i, cols):
                dve.wait_ge(l1_psum, i + 1)
                dve.tensor_tensor(h1_t[:, :, 0:cols], ps[:, 0:2, 0:cols], h1x[:, :, bass.ds(i * 4 * P, cols)],
                                  ALU.add).then_inc(h1_sum, 1)

            def residual(i, n):
                if past(i, 1):
                    dve.wait_ge(var2_ready, i)
                dve.wait_ge(xb3_ready, i + 1)
                dve.wait_ge(l3_psum, i + 1)
                rows = tiles_of(i * 4, n)
                dve.tensor_tensor(rows, rows, ps[:, 4:6, :].rearrange("p b (t f) -> p (b t) f", f=F)[:, 0:n, :],
                                  ALU.add).then_inc(x2_ready, 1)
                dve.wait_ge(consts, 7)
                dve.wait_ge(x2_ready, i + 1)
                for a in range(n):
                    dve.bn_stats(bn6[:, a, :], x_sb[:, bass.ds(i * 4 + a, 1), :].rearrange("p a f -> p (a f)")
                                 ).then_inc(bn2_done, 1)
                dve.wait_ge(bn2_done, i * 4 + n)
                dve.tensor_copy(carrier[:, :], bn6[:, 0, 0:1])
                for a in range(n):
                    dve.bn_aggr(mv4[:, a, :], bn6[:, a, :]).then_inc(mv2_ready, 1)
                dve.wait_ge(mv2_ready, i * 4 + n)
                dve.tensor_copy(mean2[:, bass.ds(i * 4, n)], mv4[:, 0:n, 0]).then_inc(mean2_ready, 1)

            def heads(v):
                return v.rearrange("p (h g) -> p h g", h=H)

            folded = [0]

            def fold_step(ins):
                ins.then_inc(fold_v, 1)
                folded[0] += 1
                return folded[0]

            dve.wait_ge(h1x_ready, 2 * (EDGE_TRIPS + 1))
            add_h1(0, 4 * P)
            dve.wait_ge(fold_in, 16 * 6)
            dve.wait_ge(fold_v, fold_step(dve.tensor_scalar(inv_temp, temp_bc, 0.1, 5.0, ALU.max, ALU.min)))
            fold_step(dve.reciprocal(inv_temp, inv_temp))
            fold_step(dve.tensor_copy(bx_rep, bx_col.unsqueeze(2).broadcast_to([P, PAIRS, P])))
            add_h1(1, 4 * P)
            residual(0, 4)
            dve.wait_ge(fold_t, 1)
            for k in range(KF):
                fold_step(dve.tensor_copy(wx_t[:, k].rearrange("p j n -> p (j n)"), ps[:, 6 + k, :]))
            with dve.Fori(1, MLP_CHUNKS - 1) as i:
                add_h1(i + 1, 4 * P)
                residual(i, 4)
            inv_all = inv_temp.unsqueeze(2).broadcast_to([P, H, G])
            dve.wait_ge(fold_t, 2)
            for k in range(KF):
                fold_step(dve.tensor_tensor(heads(wc[:, k, :]), heads(ps[:, 6 + k, :]), inv_all, ALU.mult))
            add_h1(MLP_CHUNKS, P)
            residual(MLP_CHUNKS - 1, 4)
            dve.wait_ge(fold_t, 3)
            dve.wait_ge(fold_v, fold_step(dve.tensor_tensor(heads(c_bc), heads(ps[:, 6, :]),
                                                            bsl_bc.unsqueeze(1).broadcast_to([P, H, G]), ALU.add)))
            dve.wait_ge(fold_v, fold_step(dve.tensor_tensor(heads(c_bc), heads(c_bc), inv_all, ALU.mult)))
            residual(MLP_CHUNKS, 1)

            dve.wait_ge(rstd2_ready, MLP_CHUNKS + 1)

            def normalise(t, s):
                if past(t, UNROLL):
                    dve.wait_ge(xn_used, t - UNROLL + 1)
                dve.tensor_scalar(xn[:, s, :], x_sb[:, bass.ds(t, 1), :].rearrange("p a f -> p (a f)"),
                                  mean2[:, bass.ds(t, 1)], rstd2[:, bass.ds(t, 1)], ALU.subtract, ALU.mult
                                  ).then_inc(xn2_ready, 1)

            def soft_step(t, s, i):
                if before(t, TILES - 1):
                    normalise(t + 1, (s + 1) % UNROLL)
                if before(t, TILES):
                    dve.wait_ge(logits_ready, t + 1)
                    if past(t, UNROLL):
                        dve.wait_ge(sw_tp, t - UNROLL + 1)
                        dve.wait_ge(sw_summed, t - UNROLL + 2)
                    dve.tensor_tensor(soft[:, s, :], ps[:, s % 2, :], c_bc, ALU.add).then_inc(biased, 1)
                    dve.wait_ge(biased, t + 1)
                    dve.tensor_reduce(mx[:, s, :], heads(soft[:, s, :]), AX.X, ALU.max).then_inc(max_ready, 1)
                if past(t, 1):
                    r = (s - 1) % UNROLL
                    dve.wait_ge(exp_ready, t)
                    dve.tensor_reduce(sm[:, r, :], heads(soft[:, r, :]), AX.X, ALU.add).then_inc(total_ready, 1)
                    dve.wait_ge(total_ready, t)
                    dve.reciprocal(rc[:, r, :], sm[:, r, :]).then_inc(recip_ready, 1)
                    dve.wait_ge(recip_ready, t)
                    if isinstance(t, int) and t == TILES:
                        dve.tensor_scalar(rc[:, r, :], rc[:, r, :], row_ok[:, 0:1], None, ALU.mult).then_inc(recip_ready, 1)
                        dve.wait_ge(recip_ready, t + 1)
                    dve.tensor_tensor(heads(soft[:, r, :]), heads(soft[:, r, :]),
                                      rc[:, r, :].unsqueeze(2).broadcast_to([P, H, G]), ALU.mult).then_inc(sw_ready, 1)

            dve.wait_ge(fold_t, 3)
            normalise(0, 0)
            run_steps(dve, soft_step, TILES + 1, 1, (TILES - 1) // UNROLL - 1)

            n_att = [0]

            def att_step(ins):
                ins.then_inc(att_v, 1)
                n_att[0] += 1
                return n_att[0]

            dve.wait_ge(sw_tp, TILES)
            att_step(dve.tensor_copy(s_t, ps[:, 4:6, :]))
            dve.wait_ge(att_t, 1)
            dve.wait_ge(late_in, 16 * 9)
            n = att_step(dve.tensor_copy(norm, ps[:, 0, 0:PAIRS]))
            dve.wait_ge(att_v, n)
            att_step(dve.tensor_scalar(rnorm, norm, EPS_NORM, None, ALU.add))
            n = att_step(dve.tensor_tensor(nb, bfx_bc, norm.unsqueeze(2).broadcast_to([P, PAIRS, D]), ALU.mult))
            dve.wait_ge(att_v, n)
            n = att_step(dve.reciprocal(rnorm, rnorm))
            dve.wait_ge(att_t, 2)
            tp = ps[:, 1, :].rearrange("p (j c) -> p j c", j=PAIRS)
            for hh in range(2):
                rows = slice(hh * G, (hh + 1) * G)
                n = att_step(dve.tensor_tensor(tok[rows], tp[rows, :, hh * D:(hh + 1) * D], nb[rows], ALU.add))
            dve.wait_ge(att_v, n)
            att_step(dve.tensor_tensor(tok, tok, rnorm.unsqueeze(2).broadcast_to([P, PAIRS, D]), ALU.mult))
            dve.wait_ge(att_t, 3)
            att_step(dve.tensor_copy(tok_t[0:D, :], ps[0:D, 2, :]))
            dve.wait_ge(att_clear, 2)
            dve.wait_ge(att_t, 4)
            att_step(dve.tensor_copy(k_t[0:D, :], ps[0:D, 1, :]))
            vp = ps[:, 3, :].rearrange("p (j n) -> p j n", j=PAIRS)
            for hh in range(2):
                rows = slice(hh * D, (hh + 1) * D)
                n_v = att_step(dve.tensor_copy(v_blk[rows, :, hh * G:(hh + 1) * G], vp[rows, :, hh * G:(hh + 1) * G]))
            dve.wait_ge(att_t, 5)
            at3 = att[0:G, :].rearrange("p (h g) -> p h g", h=H)
            sp3 = ps[0:G, 2, :].rearrange("p (h g) -> p h g", h=H)
            dve.tensor_reduce(att_mx[0:G, :], sp3, AX.X, ALU.max).then_inc(biased, 1)
            dve.wait_ge(biased, TILES + 1)
            att_step(dve.tensor_tensor(at3, sp3, att_mx[0:G, :].unsqueeze(2).broadcast_to([G, H, G]), ALU.subtract))
            dve.wait_ge(att_t, 6)
            att_step(dve.tensor_copy(vw, ps[:, 4:6, :].rearrange("p b (j f) -> p (b j) f", f=F)))
            dve.wait_ge(att_a, 2)
            n = att_step(dve.tensor_reduce(att_sm[0:G, :], at3, AX.X, ALU.add))
            dve.wait_ge(att_v, n)
            n = att_step(dve.reciprocal(att_rc[0:G, :], att_sm[0:G, :]))
            dve.wait_ge(att_v, n)
            att_step(dve.tensor_tensor(at3, at3, att_rc[0:G, :].unsqueeze(2).broadcast_to([G, H, G]), ALU.mult))
            dve.wait_ge(att_t, 7)
            ap = ps[:, 6, 0:PAIRS * G].rearrange("p (j g) -> p j g", j=PAIRS)
            for hh in range(2):
                rows = slice(hh * G, (hh + 1) * G)
                att_step(dve.tensor_copy(a_blk[rows, :, hh * G:(hh + 1) * G], ap[rows]))
            dve.wait_ge(att_t, 8)
            att_step(dve.tensor_copy(m_blk, ps[:, 4:6, :].rearrange("p b (j f) -> p (b j) f", f=F)))

            def finish(t, s, i):
                dve.wait_ge(y_psum, t + 1)
                dve.wait_ge(xo_ready, t + 1)
                if past(t, UNROLL):
                    dve.wait_ge(y_out[s // 2], i * 16)
                dve.tensor_tensor(o_sb[:, s, :], ps[:, s, 0:F], xo[:, s, :], ALU.add).then_inc(y_ready, 1)

            run_steps(dve, finish, TILES, 1, MLP_CHUNKS - 1)

        @block.tensor
        def _(pe):
            mm = nc.tensor.matmul
            tr = nc.tensor.transpose
            pe.wait_ge(consts, 7)
            pe.wait_ge(prep_v, 7)
            for k in range(ROWS_PER_PART):
                for t in range(GTILES):
                    src = rel_g[:, t, :].rearrange("p (e k) -> p k e", k=ROWS_PER_PART)[:, k, :]
                    last = tr(ps[:, 6 + k, t * P:(t + 1) * P], src, ident[:, :])
            last.then_inc(prep_t, 1)
            pe.wait_ge(prep_v, 9)
            for t in range(GTILES):
                tr(ps[0:1, 5, t * P:(t + 1) * P], base_col[:, t:t + 1], ident[:, :])
            tr(ps[0:1, 4, 0:P], far_one[:, 0:1], ident[:, :]).then_inc(prep_t, 1)
            pe.wait_ge(prep_v, 19)
            pe.wait_ge(mlp_in, 16 * 3)

            def chunk(c, s, i):
                pe.wait_ge(hot_ready, c * 2 + 2)
                if before(c, FULL_CHUNKS):
                    pe.wait_ge(edge_in[s], i * 16 + 16)
                else:
                    pe.wait_ge(edge_in[s], i * 16 + 32)
                pe.wait_ge(groups_added, c * CHUNK_GROUPS + (CREDIT - (UNROLL - 1) * CHUNK_GROUPS))
                groups = CHUNK_GROUPS if before(c, FULL_CHUNKS) else TAIL_GROUPS
                for g in range(groups):
                    parts = P if before(c, FULL_CHUNKS) or g < groups - 1 else LAST_PARTS
                    if g == WHOLE:
                        pe.wait_ge(low_ready, c + 1)
                    for h in range(KF):
                        cols = slice(h * P, (h + 1) * P)
                        terms = []
                        if g < WHOLE:
                            for k in range(ROWS_PER_PART):
                                terms.append((ring[0:parts, s, g, k, cols],
                                              hot_f[0:parts, s % 2, g * ROWS_PER_PART + k, :]))
                        else:
                            for k in range(ROWS_PER_PART):
                                n = (g - WHOLE) * ROWS_PER_PART + k
                                for v in (upper(ring[0:parts, s, g, k, cols]), upper(rest[0:parts, s % 2, n, cols]),
                                          low[0:parts, s % 2, n, cols]):
                                    terms.append((v, hot_b[0:parts, s % 2, n, :]))
                        for n, (v, hot) in enumerate(terms):
                            last = mm(ps[:, s, g * P + h * WINDOW:g * P + (h + 1) * WINDOW], lhsT=v, rhs=hot,
                                      start=(n == 0), stop=(n == len(terms) - 1))
                last.then_inc(sums_ready, 1)
                if past(c, UNROLL):
                    if s == 1:
                        ln_transposes(i - 1, 2)
                    if s >= 2:
                        first_layer_x(i - 1, 2, s - 2)

            def ln_transposes(i, n):
                pe.wait_ge(xn1_ready, i * 2 + n)
                for a in range(n):
                    for k in range(KF):
                        last = tr(ps[:, 4, k * 256 + a * P:k * 256 + (a + 1) * P], xn[:, a, k * P:(k + 1) * P],
                                  ident[:, :])
                last.then_inc(ln_tp, 1)

            def first_layer_x(i, n, m):
                if m == 0:
                    pe.wait_ge(ln_t_ready, i + 1)
                else:
                    pe.wait_ge(h1x_ready, i * 2 + 1)
                for k in range(KF):
                    last = mm(ps[:, 5, m * 256:m * 256 + n * P], lhsT=w1a_sb[:, k, m * P:(m + 1) * P],
                              rhs=ln_t[:, k, 0:n * P], start=(k == 0), stop=(k == KF - 1))
                last.then_inc(h1x_psum, 1)

            run_steps(pe, chunk, CHUNKS, 1, EDGE_TRIPS - 1)
            first_layer_x(EDGE_TRIPS - 1, 2, 0)
            first_layer_x(EDGE_TRIPS - 1, 2, 1)
            ln_transposes(EDGE_TRIPS, 1)
            for m in range(KF):
                first_layer_x(EDGE_TRIPS, 1, m)

            pe.wait_ge(edges_done, 1)
            far = pe.value_load(far_i[0:1, 0:1], min_val=0, max_val=1)

            def far_group(g, parts):
                pe.wait_ge(gen_e_in, g * 16 + 16)
                for w in range(WIDES):
                    pe.wait_ge(gen_hot, g * (2 * WIDES) + (2 * w + 2))
                    for h in range(KF):
                        for k in range(ROWS_PER_PART):
                            last = mm(ps[:, h, 0:WIDE], lhsT=ring[0:parts, 0, 0, k, h * P:(h + 1) * P],
                                      rhs=g_hot[0:parts, k, 0:WIDE], start=(k == 0), stop=(k == ROWS_PER_PART - 1))
                    last.then_inc(gen_sums, 1)

            with pe.If(far > 0):
                with pe.Fori(0, GROUPS - 1) as g:
                    far_group(g, P)
                far_group(GROUPS - 1, LAST_PARTS)
            pe.wait_ge(edges_done, 2)

            def layer1(i, cols):
                for m in range(KF):
                    for k in range(KF):
                        last = mm(ps[:, m, 0:cols], lhsT=w1b_sb[:, k, m * P:(m + 1) * P],
                                  rhs=agg[:, k, bass.ds(i * 4 * P, cols)], start=(k == 0), stop=(k == KF - 1))
                last.then_inc(l1_psum, 1)

            def layer2(i, cols):
                pe.wait_ge(h1_ready, i + 1)
                for m in range(KF):
                    for k in range(KF):
                        last = mm(ps[:, 2 + m, 0:cols], lhsT=w2_sb[:, k, m * P:(m + 1) * P],
                                  rhs=h1_t[:, k, 0:cols], start=(k == 0), stop=(k == KF - 1))
                last.then_inc(l2_psum, 1)

            def layer3(i, n):
                pe.wait_ge(h2_ready, i * 2 + 2)
                if past(i, 1):
                    pe.wait_ge(x2_ready, i)
                for a in range(n):
                    for k in range(KF):
                        last = mm(ps[:, 4 + a // 2, (a % 2) * F:(a % 2 + 1) * F],
                                  lhsT=h2_t[:, k, a * P:(a + 1) * P], rhs=w3_sb[:, k, :],
                                  start=(k == 0), stop=(k == KF - 1))
                last.then_inc(l3_psum, 1)

            pe.wait_ge(w1b_in, 16)
            layer1(0, 4 * P)
            pe.wait_ge(w23_in, 32)
            layer2(0, 4 * P)
            layer1(1, 4 * P)
            layer3(0, 4)
            pe.wait_ge(fold_in, 16 * 6)
            for k in range(KF):
                for j in range(PAIRS):
                    last = tr(ps[:, 6 + k, j * P:(j + 1) * P], wx[:, k, j * P:(j + 1) * P], ident[:, :])
            last.then_inc(fold_t, 1)
            with pe.Fori(1, MLP_CHUNKS - 1) as i:
                layer2(i, 4 * P)
                layer1(i + 1, 4 * P)
                layer3(i, 4)
            pe.wait_ge(fold_v, 5)
            for j in range(PAIRS):
                for k in range(KF):
                    last = mm(ps[:, 6 + k, j * P:(j + 1) * P], lhsT=wx_t[:, k, j, :], rhs=blk_s, start=True, stop=True)
            last.then_inc(fold_t, 1)
            layer2(MLP_CHUNKS - 1, 4 * P)
            layer1(MLP_CHUNKS, P)
            pe.wait_ge(fold_v, 7)
            for j in range(PAIRS):
                last = mm(ps[:, 6, j * P:(j + 1) * P], lhsT=bx_rep[:, j, :], rhs=blk_s, start=True, stop=True)
            last.then_inc(fold_t, 1)
            layer3(MLP_CHUNKS - 1, 4)
            layer2(MLP_CHUNKS, P)
            layer3(MLP_CHUNKS, 1)

            def tp_rows(t, s):
                pe.wait_ge(xn2_ready, t + 1)
                for k in range(KF):
                    last = tr(ps[:, 2 + s % 2, k * P:(k + 1) * P], xn[:, s, k * P:(k + 1) * P], ident[:, :])
                last.then_inc(tp_ready, 1)

            def soft_step(t, s, i):
                r = (s - 3) % UNROLL
                if past(t, 3):
                    pe.wait_ge(sw_ready, t - 2)
                    for k in range(KF):
                        last = mm(ps[:, 4 + k, :], lhsT=xn[:, r, k * P:(k + 1) * P], rhs=soft[:, r, :],
                                  start=isinstance(t, int) and t == 3, stop=isinstance(t, int) and t == TILES + 2)
                    last.then_inc(xn_used, 1)
                if before(t, TILES):
                    pe.wait_ge(xn_t_ready, t + 1)
                    if past(t, 2):
                        pe.wait_ge(biased, t - 1)
                    for k in range(KF):
                        last = mm(ps[:, s % 2, :], lhsT=xn_t[:, s % 2, k, :], rhs=wc[:, k, :],
                                  start=(k == 0), stop=(k == KF - 1))
                    last.then_inc(logits_ready, 1)
                if past(t, 3):
                    if past(t, 5):
                        pe.wait_ge(sw_t_ready, t - 4)
                    for j in range(PAIRS):
                        last = tr(ps[:, 6 + (s - 3) % 2, j * P:(j + 1) * P], soft[:, r, j * P:(j + 1) * P], ident[:, :])
                    last.then_inc(sw_tp, 1)
                if before(t, TILES - 1):
                    tp_rows(t + 1, (s + 1) % UNROLL)

            pe.wait_ge(fold_v, 9)
            tp_rows(0, 0)
            run_steps(pe, soft_step, TILES + 3, 2, (TILES - 1) // UNROLL - 2)

            pe.wait_ge(sw_summed, TILES + 1)
            for j in range(PAIRS):
                last = mm(ps[:, 0, j:j + 1], lhsT=sw_sum[:, j * P:(j + 1) * P], rhs=ones[:, 0:1], start=True, stop=True)
            last.then_inc(att_t, 1)
            pe.wait_ge(att_v, 1)
            pe.wait_ge(late_in, 16 * 9)
            for j in range(PAIRS):
                for k in range(KF):
                    last = mm(ps[:, 1, j * P:(j + 1) * P], lhsT=s_t[:, k, j * P:(j + 1) * P],
                              rhs=wfx_sb[:, k, j * P:(j + 1) * P], start=(k == 0), stop=(k == KF - 1))
            last.then_inc(att_t, 1)
            pe.wait_ge(att_v, 8)
            for j in range(PAIRS):
                last = tr(ps[0:D, 2, j * P:(j + 1) * P], tok[:, j, :], ident[:, :])
            last.then_inc(att_t, 1)
            pe.wait_ge(att_v, 9)
            mm(ps[0:D, 0, :], lhsT=wq_sb[0:D, :], rhs=tok_t[0:D, :], start=True, stop=True)
            mm(ps[0:D, 1, :], lhsT=wk_sb[0:D, :], rhs=tok_t[0:D, :], start=True, stop=True)
            mm(ps[:, 3, :], lhsT=wv2_sb[0:D, :], rhs=tok_t[0:D, :], start=True, stop=True).then_inc(att_t, 1)
            pe.wait_ge(att_a, 1)
            pe.wait_ge(att_v, 10)
            for h in range(H):
                last = mm(ps[0:G, 2, h * G:(h + 1) * G], lhsT=q_t[0:D, h * G:(h + 1) * G],
                          rhs=k_t[0:D, h * G:(h + 1) * G], start=True, stop=True)
            last.then_inc(att_t, 1)
            pe.wait_ge(att_v, 12)
            for j in range(PAIRS):
                last = mm(ps[:, 4 + j // 2, (j % 2) * F:(j % 2 + 1) * F], lhsT=v_blk[:, j, :], rhs=wout_sb[:, j, :],
                          start=True, stop=True)
            last.then_inc(att_t, 1)
            pe.wait_ge(att_v, 17)
            for j in range(PAIRS):
                last = tr(ps[:, 6, j * G:(j + 1) * G], att[0:G, j * P:(j + 1) * P], ident[0:G, 0:G])
            last.then_inc(att_t, 1)
            pe.wait_ge(att_v, 19)
            for j in range(PAIRS):
                last = mm(ps[:, 4 + j // 2, (j % 2) * F:(j % 2 + 1) * F], lhsT=a_blk[:, j, :], rhs=vw[:, j, :],
                          start=True, stop=True)
            last.then_inc(att_t, 1)
            pe.wait_ge(att_v, 20)

            def project(t, s, i):
                pe.wait_ge(staged, t + 1)
                if past(t, UNROLL):
                    pe.wait_ge(y_ready, t - UNROLL + 1)
                for j in range(PAIRS):
                    last = mm(ps[:, s, 0:F], lhsT=stage[:, s, j * P:(j + 1) * P], rhs=m_blk[:, j, :],
                              start=(j == 0), stop=(j == PAIRS - 1))
                last.then_inc(y_psum, 1)

            run_steps(pe, project, TILES, 1, MLP_CHUNKS - 1)


_INS = ['x', 'dst', 'edge_attr_256', 'L0_gnn_W1', 'L0_gnn_b1', 'L0_gnn_W2', 'L0_gnn_b2', 'L0_gnn_W3', 'L0_gnn_b3',
        'L0_ffn_W_fx', 'L0_ffn_b_fx', 'L0_ffn_W_x', 'L0_ffn_b_x', 'L0_ffn_W_slice', 'L0_ffn_b_slice',
        'L0_ffn_W_q', 'L0_ffn_W_k', 'L0_ffn_W_v', 'L0_ffn_W_out', 'L0_ffn_b_out', 'L0_ffn_temperature']


def kernel(**inputs):
    import numpy as np
    import concourse.bacc as bacc
    from concourse.bass_utils import run_bass_kernel_spmd as run

    nc = bacc.Bacc("TRN2", target_bir_lowering=False, num_devices=1)
    arrays = {f"{n}_in": np.ascontiguousarray(inputs[n]) for n in _INS}
    args = [nc.dram_tensor(n, a.shape, mybir.dt.from_np(a.dtype), kind="ExternalInput").ap()
            for n, a in arrays.items()]
    out = nc.dram_tensor("result", inputs['x'].shape, F32, kind="ExternalOutput").ap()
    build(nc, *args, out)
    return run(nc, [arrays], core_ids=[0]).results[0]["result"]
```

```python
from contextlib import ExitStack

import concourse.bass as bass
from concourse import mybir

F32 = mybir.dt.float32
BF16 = mybir.dt.bfloat16
I32 = mybir.dt.int32
ALU = mybir.AluOpType
ACT = mybir.ActivationFunctionType
AX = mybir.AxisListType

P = 128
UNROLL = 4
WINDOW = 64
ROWS_PER_PART = 2
GROUP = P * ROWS_PER_PART
CHUNK_GROUPS = 4
SPLIT = 2
WHOLE = CHUNK_GROUPS - SPLIT
EPS_LN = 1e-5
EPS_NORM = 1e-5
CREDIT = 16


def past(t, n):
    return not isinstance(t, int) or t >= n


def before(t, n):
    return not isinstance(t, int) or t < n


def run_steps(eng, step, total, peel_front, loop_trips):
    first = peel_front * UNROLL
    for t in range(first):
        step(t, t % UNROLL, t // UNROLL)
    with eng.Fori(peel_front, peel_front + loop_trips) as i:
        for s in range(UNROLL):
            step(i * UNROLL + s, s, i)
    for t in range((peel_front + loop_trips) * UNROLL, total):
        step(t, t % UNROLL, t // UNROLL)


def build(nc, x, dst, edges, w1, b1, w2, b2, w3, b3, w_fx, b_fx, w_x, b_x, w_slice, b_slice,
          w_q, w_k, w_v, w_out, b_out, temperature, out):
    N, F = x.shape
    E = edges.shape[0]
    KF = F // P
    H = temperature.shape[1]
    D, G = w_slice.shape
    S = H * G
    PAIRS = S // P
    TILES = -(-N // P)
    NPAD = TILES * P
    LAST_ROWS = N - (TILES - 1) * P

    GROUPS = -(-E // GROUP)
    LAST_EDGES = E - (GROUPS - 1) * GROUP
    LAST_PARTS = LAST_EDGES // ROWS_PER_PART
    CHUNKS = -(-GROUPS // CHUNK_GROUPS)
    CHUNK_EDGES = CHUNK_GROUPS * GROUP
    FULL_CHUNKS = E // CHUNK_EDGES
    TAIL_GROUPS = GROUPS - FULL_CHUNKS * CHUNK_GROUPS
    EDGE_TRIPS = FULL_CHUNKS // UNROLL
    GTILES = -(-GROUPS // P)
    FULL_GTILES = GROUPS // P
    WIDE = 488
    WIDES = -(-(N + WINDOW) // WIDE)
    AGG = WIDE * WIDES
    CLEAR_V = AGG * 3 // 4
    SCALE = float(D) ** -0.5
    assert F == KF * P and P == 2 * G and D == G and S == 512 and AGG >= N + WINDOW
    assert LAST_EDGES % ROWS_PER_PART == 0 and 2 * EDGE_TRIPS == TILES - 1
    MLP_CHUNKS = (TILES - 1) // 4

    with ExitStack() as ctx:
        def sb(name, shape, dt=F32):
            return ctx.enter_context(nc.sbuf_tensor(name, shape, dt))

        def sem(name):
            return ctx.enter_context(nc.semaphore(name))

        x_sb = sb("x_sb", [P, TILES, F])
        big = sb("big", [P, KF * AGG + KF * NPAD])
        agg = big[:, 0:KF * AGG].rearrange("p (h n) -> p h n", h=KF)
        h1x = big[:, KF * AGG:].rearrange("p (h n) -> p h n", h=KF)
        sw_t = big[:, 0:PAIRS * NPAD].rearrange("p (j n) -> p j n", j=PAIRS)
        tmp = big[:, KF * AGG:]
        dst_f = tmp[:, 0:1024].rearrange("p (t e) -> p t e", t=GTILES)
        rel_g = tmp[:, 1024:2048].rearrange("p (t e) -> p t e", t=GTILES)
        dst_i = tmp[:, 5000:6024].bitcast(I32).rearrange("p (t e) -> p t e", t=GTILES)

        ring_mem = sb("ring_mem", [P, UNROLL * CHUNK_GROUPS * ROWS_PER_PART * F])
        ring = ring_mem[:, :].rearrange("p (s g k f) -> p s g k f", s=UNROLL, g=CHUNK_GROUPS, k=ROWS_PER_PART)

        def part(start, size):
            return ring_mem[:, start:start + size]

        h1_t = part(0, 1024).rearrange("p (m n) -> p m n", m=KF)
        h2_t = part(1024, 1024).rearrange("p (m n) -> p m n", m=KF)
        wfx_sb = part(2048, 1024).rearrange("p (k n) -> p k n", k=KF)
        wout_sb = part(3072, 1024).rearrange("p (j n) -> p j n", j=PAIRS)
        bout_bc = part(4096, 256)
        bfx_bc = part(4352, 256).rearrange("p (j c) -> p j c", j=PAIRS)
        wq_sb = part(4608, 64)
        wk_sb = part(4672, 64)
        wv2_sb = part(4736, 128)
        sw_sum = part(4864, 512)
        soft = part(5376, 2048).rearrange("p (b n) -> p b n", b=UNROLL)
        xn_t = part(7424, 512).rearrange("p (b k n) -> p b k n", b=2, k=KF)
        b3_bc = sw_sum[:, 0:F]
        s_t = part(0, 1024).rearrange("p (k n) -> p k n", k=KF)
        tok = part(1024, 256).rearrange("p (j c) -> p j c", j=PAIRS)
        nb = part(1280, 256).rearrange("p (j c) -> p j c", j=PAIRS)
        norm = part(7936, 4)
        rnorm = part(7940, 4)
        att_mx = part(7944, 8)
        att_sm = part(7952, 8)
        att_rc = part(7960, 4)
        tok_t = part(1536, 512)
        q_t = part(5376, 512)
        k_t = part(5888, 512)
        v_blk = part(6400, 512).rearrange("p (j n) -> p j n", j=PAIRS)
        att = part(6912, 512)
        a_blk = part(7424, 512).rearrange("p (j n) -> p j n", j=PAIRS)
        stage = soft
        o_sb = h1_t.rearrange("p m n -> p (m n)").rearrange("p (b f) -> p b f", b=UNROLL)

        SPL = SPLIT * ROWS_PER_PART
        HOT = WHOLE * ROWS_PER_PART
        hot_f = sb("hot_f", [P, 2, HOT, WINDOW])
        hot_b = sb("hot_b", [P, 2, SPL, WINDOW], BF16)
        split_mem = sb("split_mem", [P, 3072])
        rest = split_mem[:, 0:2048].rearrange("p (b k f) -> p b k f", b=2, k=SPL)
        low = split_mem[:, 2048:3072].bitcast(BF16).rearrange("p (b k f) -> p b k f", b=2, k=SPL)
        wc = split_mem[:, 0:1024].rearrange("p (k n) -> p k n", k=KF)
        c_bc = split_mem[:, 1024:1536]
        w1b_sb = split_mem[:, 1536:2048].rearrange("p (k n) -> p k n", k=KF)
        m_blk = split_mem[:, 2048:3072].rearrange("p (j n) -> p j n", j=PAIRS)

        w2_sb = part(5376, 512).rearrange("p (k n) -> p k n", k=KF)
        w3_sb = part(5888, 512).rearrange("p (k n) -> p k n", k=KF)
        xn = sb("xn", [P, UNROLL, F])
        xo = xn
        vw = xn[:, :, :]
        ln_t = sb("ln_t", [P, KF, 2 * P])
        w1a_sb = sb("w1a_sb", [P, KF, F])
        wx = xn[:, :, :].rearrange("p b f -> p (b f)").rearrange("p (k n) -> p k n", k=KF)
        wx_t = part(6400, 1024).rearrange("p (k j n) -> p k j n", k=KF, j=PAIRS)
        bx_rep = part(7424, 512).rearrange("p (j n) -> p j n", j=PAIRS)
        fold_mem = ln_t[:, :, :].rearrange("p k n -> p (k n)")
        blk_s = fold_mem[:, 0:128]
        bx_col = fold_mem[:, 128:132]
        bsl_bc = fold_mem[:, 132:196]
        temp_bc = fold_mem[:, 196:204]
        inv_temp = fold_mem[:, 204:212]
        ident = sb("ident", [P, P])
        ones = sb("ones", [P, 1])
        iota_w = sb("iota_w", [P, WINDOW])
        rel = sb("rel", [P, CHUNKS * CHUNK_GROUPS, ROWS_PER_PART])
        base_i = xn[:, 2:4, :].rearrange("p b f -> p (b f)").bitcast(I32)
        base_col = sb("base_col", [P, GTILES])
        far_col = sb("far_col", [P, GTILES])
        far_one = sb("far_one", [P, 1])
        far_i = sb("far_i", [1, 2], I32)
        b1_sb = sb("b1_sb", [P, KF])
        b2_sb = sb("b2_sb", [P, KF])
        half = sb("half", [P, UNROLL])
        row_no = sb("row_no", [P, 1])
        row_ok = sb("row_ok", [P, 1])
        bn6 = sb("bn6", [P, UNROLL, 6])
        mv1 = sb("mv1", [P, 2, 2])
        var_e = sb("var_e", [P, UNROLL])
        rstd1 = sb("rstd1", [P, 2])
        shift1 = sb("shift1", [P, 2])
        minus = sb("minus", [P, 2])
        mv4 = sb("mv4", [P, UNROLL, 2])
        eps = sb("eps", [P, UNROLL])
        mean2 = sb("mean2", [P, TILES])
        rstd2 = sb("rstd2", [P, TILES])
        carrier = sb("carrier", [P, 1])
        mx = sb("mx", [P, UNROLL, H])
        sm = sb("sm", [P, UNROLL, H])
        rc = sb("rc", [P, UNROLL, H])
        g_iota = part(2048, 512)
        g_hot = part(2560, 1024).rearrange("p (k n) -> p k n", k=ROWS_PER_PART)
        g_dst = part(3600, 2).bitcast(I32)
        g_abs = part(3604, 2)
        g_cov = part(3608, 2)
        g_win = part(3612, 2)

        ps = ctx.enter_context(nc.psum_tensor("ps", [P, 8, 512], F32))

        dst_in = sem("dst_in")
        edge_in = [sem(f"edge_in{s}") for s in range(UNROLL)]
        x_in = sem("x_in")
        x_tail_in = sem("x_tail_in")
        fold_in = sem("fold_in")
        mlp_in = sem("mlp_in")
        w1b_in = sem("w1b_in")
        w23_in = sem("w23_in")
        b3_in = sem("b3_in")
        late_in = sem("late_in")
        dst_clear = sem("dst_clear")
        consts = sem("consts")
        x_clear = sem("x_clear")
        blk_clear = sem("blk_clear")
        agg_clear = sem("agg_clear")
        prep_v = sem("prep_v")
        prep_t = sem("prep_t")
        rest_ready = sem("rest_ready")
        low_ready = sem("low_ready")
        hot_ready = sem("hot_ready")
        sums_ready = sem("sums_ready")
        groups_added = sem("groups_added")
        bn_done = sem("bn_done")
        mv1_ready = sem("mv1_ready")
        var1_ready = sem("var1_ready")
        pow1_ready = sem("pow1_ready")
        rstd1_ready = sem("rstd1_ready")
        xn1_ready = sem("xn1_ready")
        ln_tp = sem("ln_tp")
        ln_t_ready = sem("ln_t_ready")
        h1x_psum = sem("h1x_psum")
        h1x_ready = sem("h1x_ready")
        edges_done = sem("edges_done")
        gen_e_in = sem("gen_e_in")
        gen_d_in = sem("gen_d_in")
        gen_v = sem("gen_v")
        gen_hot = sem("gen_hot")
        gen_sums = sem("gen_sums")
        gen_group = sem("gen_group")
        xb3_ready = sem("xb3_ready")
        l1_psum = sem("l1_psum")
        h1_sum = sem("h1_sum")
        h1_ready = sem("h1_ready")
        l2_psum = sem("l2_psum")
        h2_ready = sem("h2_ready")
        l3_psum = sem("l3_psum")
        x2_ready = sem("x2_ready")
        bn2_done = sem("bn2_done")
        mv2_ready = sem("mv2_ready")
        mean2_ready = sem("mean2_ready")
        var2_ready = sem("var2_ready")
        rstd2_ready = sem("rstd2_ready")
        fold_v = sem("fold_v")
        fold_t = sem("fold_t")
        xn2_ready = sem("xn2_ready")
        tp_ready = sem("tp_ready")
        xn_t_ready = sem("xn_t_ready")
        logits_ready = sem("logits_ready")
        biased = sem("biased")
        max_ready = sem("max_ready")
        shifted = sem("shifted")
        exp_ready = sem("exp_ready")
        total_ready = sem("total_ready")
        recip_ready = sem("recip_ready")
        sw_ready = sem("sw_ready")
        xn_used = sem("xn_used")
        sw_tp = sem("sw_tp")
        sw_t_ready = sem("sw_t_ready")
        sw_summed = sem("sw_summed")
        att_v = sem("att_v")
        att_a = sem("att_a")
        att_t = sem("att_t")
        att_p = sem("att_p")
        att_clear = sem("att_clear")
        staged = sem("staged")
        xo_ready = sem("xo_ready")
        y_psum = sem("y_psum")
        y_ready = sem("y_ready")
        y_out = [sem(f"y_out{q}") for q in range(2)]

        block = ctx.enter_context(nc.Block())

        def upper(v):
            return v.bitcast(BF16)[:, 1::2]

        def tiles_of(t0, n):
            return x_sb[:, bass.ds(t0, n), :]

        @block.sync
        def _(sp):
            full = FULL_GTILES * P * GROUP
            sp.dma_start(dst_i[:, 0:FULL_GTILES, :],
                         dst[0:full].rearrange("(t p e) -> p t e", p=P, e=GROUP)).then_inc(dst_in, 16)
            sp.wait_ge(dst_clear, 1)
            whole = GROUPS - 1 - FULL_GTILES * P
            sp.dma_start(dst_i[0:whole, FULL_GTILES, :],
                         dst[full:full + whole * GROUP].rearrange("(p e) -> p e", e=GROUP)).then_inc(dst_in, 16)
            row = dst.rearrange("(a e) -> a e", a=1)
            sp.dma_start(dst_i[whole:whole + 1, FULL_GTILES, 0:LAST_EDGES],
                         row[:, E - LAST_EDGES:E]).then_inc(dst_in, 16)
            sp.dma_start(dst_i[whole:whole + 1, FULL_GTILES, LAST_EDGES:GROUP],
                         row[:, E - (GROUP - LAST_EDGES):E]).then_inc(dst_in, 16)

            def chunk(c, s, i):
                if past(c, UNROLL):
                    sp.wait_ge(sums_ready, c - UNROLL + 1)
                if before(c, FULL_CHUNKS):
                    sp.dma_start(ring[:, s].rearrange("p g k f -> p g (k f)"),
                                 edges[bass.ds(c * CHUNK_EDGES, CHUNK_EDGES), :].rearrange(
                                     "(g p k) f -> p g (k f)", p=P, k=ROWS_PER_PART)).then_inc(edge_in[s], 16)
                else:
                    e0 = FULL_CHUNKS * CHUNK_EDGES
                    e1 = (GROUPS - 1) * GROUP
                    sp.dma_start(ring[:, s, 0:TAIL_GROUPS - 1].rearrange("p g k f -> p g (k f)"),
                                 edges[e0:e1, :].rearrange("(g p k) f -> p g (k f)", p=P,
                                                           k=ROWS_PER_PART)).then_inc(edge_in[s], 16)
                    sp.dma_start(ring[0:LAST_PARTS, s, TAIL_GROUPS - 1].rearrange("p k f -> p (k f)"),
                                 edges[e1:E, :].rearrange("(p k) f -> p (k f)",
                                                          k=ROWS_PER_PART)).then_inc(edge_in[s], 16)
                if isinstance(c, int) and c == 3:
                    sp.wait_ge(x_clear, 1)
                    sp.dma_start(x_sb[0:LAST_ROWS, TILES - 1, :], x[(TILES - 1) * P:N, :]).then_inc(x_tail_in, 16)
                if s == 0 and before(c, FULL_CHUNKS - 1):
                    if past(c, UNROLL):
                        sp.wait_ge(x_in, i * 16)
                    sp.dma_start(tiles_of(i * 2, 2),
                                 x[bass.ds(i * (2 * P), 2 * P), :].rearrange("(t p) f -> p t f", p=P)
                                 ).then_inc(x_in, 16)

            run_steps(sp, chunk, CHUNKS, 1, EDGE_TRIPS - 1)
            sp.wait_ge(sums_ready, (FULL_CHUNKS // UNROLL) * UNROLL)
            sp.dma_start(w2_sb, w2.rearrange("(k p) n -> p k n", p=P)).then_inc(w23_in, 16)
            sp.dma_start(w3_sb, w3.rearrange("(k p) n -> p k n", p=P)).then_inc(w23_in, 16)
            sp.dma_start(w1b_sb, w1[F:2 * F, :].rearrange("(k p) n -> p k n", p=P)).then_inc(w1b_in, 16)

            sp.wait_ge(edges_done, 1)
            far = sp.value_load(far_i[0:1, 0:1], min_val=0, max_val=1)

            def reload(g, parts):
                sp.wait_ge(gen_group, g + 1)
                rows = bass.ds(g * GROUP, parts * ROWS_PER_PART)
                sp.dma_start(ring[0:parts, 0, 0].rearrange("p k f -> p (k f)"),
                             edges[rows, :].rearrange("(p k) f -> p (k f)", k=ROWS_PER_PART)).then_inc(gen_e_in, 16)
                sp.dma_start(g_dst[0:parts, :],
                             dst[rows].rearrange("(p k) -> p k", k=ROWS_PER_PART)).then_inc(gen_d_in, 16)

            with sp.If(far > 0):
                with sp.Fori(0, GROUPS - 1) as g:
                    reload(g, P)
                reload(GROUPS - 1, LAST_PARTS)

            sp.wait_ge(edges_done, 2)
            sp.dma_start(b3_bc, b3.rearrange("(a n) -> a n", a=1).broadcast_to([P, F])).then_inc(b3_in, 16)
            sp.wait_ge(h1x_ready, 2 * (EDGE_TRIPS + 1))
            sp.dma_start(wx, w_x.rearrange("(k p) n -> p k n", p=P)).then_inc(fold_in, 16)
            sp.dma_start(bx_col, b_x.rearrange("(j p) -> p j", p=P), allow_slow_non_contiguous=True).then_inc(fold_in, 16)
            sp.dma_start(bsl_bc, b_slice.rearrange("(a g) -> a g", a=1).broadcast_to([P, G])).then_inc(fold_in, 16)
            sp.dma_start(temp_bc, temperature.rearrange("a h b c -> a (h b c)").broadcast_to([P, H])
                         ).then_inc(fold_in, 16)
            sp.wait_ge(blk_clear, 1)
            for hh in range(2):
                sp.dma_start(blk_s[hh * D:(hh + 1) * D, hh * G:(hh + 1) * G], w_slice).then_inc(fold_in, 16)
            sp.dma_start(wfx_sb, w_fx.rearrange("(k p) n -> p k n", p=P)).then_inc(late_in, 16)
            sp.dma_start(wout_sb, w_out.rearrange("(j p) n -> p j n", p=P)).then_inc(late_in, 16)
            sp.dma_start(bout_bc, b_out.rearrange("(a n) -> a n", a=1).broadcast_to([P, F])).then_inc(late_in, 16)
            bfx = b_fx.rearrange("(j h c) -> h j c", h=2, c=D)
            for hh in range(2):
                sp.dma_start(bfx_bc[hh * G:(hh + 1) * G], bfx[hh:hh + 1].broadcast_to([G, PAIRS, D])
                             ).then_inc(late_in, 16)
                sp.dma_start(wv2_sb[0:D, hh * D:(hh + 1) * D], w_v).then_inc(late_in, 16)
            sp.dma_start(wq_sb[0:D, :], w_q).then_inc(late_in, 16)
            sp.dma_start(wk_sb[0:D, :], w_k).then_inc(late_in, 16)

            def store(t, s, i):
                if s % 2 == 1:
                    sp.wait_ge(y_ready, t + 1)
                    sp.dma_start(out[bass.ds((t - 1) * P, 2 * P), :].rearrange("(t p) f -> p t f", p=P),
                                 o_sb[:, s - 1:s + 1, :]).then_inc(y_out[s // 2], 16)
                elif isinstance(t, int) and t == TILES - 1:
                    sp.wait_ge(y_ready, TILES)
                    sp.dma_start(out[t * P:N, :], o_sb[0:LAST_ROWS, s, :]).then_inc(y_out[0], 16)

            run_steps(sp, store, TILES, 0, MLP_CHUNKS)
            sp.wait_ge(y_out[0], 16 * (MLP_CHUNKS + 1))
            sp.wait_ge(y_out[1], 16 * MLP_CHUNKS)

        @block.gpsimd
        def _(pool):
            pool.memset(dst_i[:, FULL_GTILES, :], 0).then_inc(dst_clear, 1)
            pool.memset(ident[:, :], 0.0).then_inc(consts, 1)
            pool.wait_ge(consts, 1)
            pool.affine_select(out=ident[:, :], in_=ident[:, :], compare_op=ALU.not_equal, fill=1.0, base=0,
                               pattern=[[-1, P]], channel_multiplier=1).then_inc(consts, 1)
            pool.iota(iota_w[:, :], [[1, WINDOW]], base=0, channel_multiplier=0,
                      allow_small_or_imprecise_dtypes=True).then_inc(consts, 1)
            pool.memset(minus[:, :], -1.0)
            pool.memset(half[:, :], -0.5).then_inc(consts, 1)
            pool.memset(eps[:, :], EPS_LN).then_inc(consts, 1)
            pool.memset(ones[:, :], 1.0).then_inc(consts, 1)
            pool.iota(row_no[:, :], [[0, 1]], base=0, channel_multiplier=1,
                      allow_small_or_imprecise_dtypes=True).then_inc(consts, 1)
            pool.memset(agg[:, 1, :], 0.0).then_inc(agg_clear, 1)
            pool.memset(x_sb[:, TILES - 1, :], 0.0).then_inc(x_clear, 1)
            pool.memset(agg[:, 0, CLEAR_V:], 0.0).then_inc(agg_clear, 1)
            pool.wait_ge(consts, 7)

            def rstd(mv, dest, n, ready, tiles_ready, step_sem, done, count):
                pool.wait_ge(ready, tiles_ready)
                pool.tensor_tensor(var_e[:, 0:n], mv, eps[:, 0:n], ALU.add).then_inc(step_sem, 1)
                pool.wait_ge(step_sem, count)
                pool.tensor_tensor(dest, var_e[:, 0:n], half[:, 0:n], ALU.pow).then_inc(done, 1)

            def ln_pair(i, n):
                pool.wait_ge(mv1_ready, i * 2 + n)
                if past(i, 1):
                    pool.wait_ge(xn1_ready, i * 2)
                pool.tensor_tensor(var_e[:, 0:n], mv1[:, 0:n, 1], eps[:, 0:n], ALU.add)
                pool.tensor_tensor(shift1[:, 0:n], mv1[:, 0:n, 0], minus[:, 0:n], ALU.mult).then_inc(var1_ready, 1)
                pool.wait_ge(var1_ready, i + 1)
                pool.tensor_tensor(rstd1[:, 0:n], var_e[:, 0:n], half[:, 0:n], ALU.pow).then_inc(pow1_ready, 1)
                pool.wait_ge(pow1_ready, i + 1)
                pool.tensor_tensor(shift1[:, 0:n], shift1[:, 0:n], rstd1[:, 0:n], ALU.mult).then_inc(rstd1_ready, 1)

            def low_part(c, b, parts, rows):
                pool.wait_ge(rest_ready, c + 1)
                if past(c, 2):
                    pool.wait_ge(sums_ready, c - 1)
                v = rest[0:parts, b, 0:rows, :].rearrange("p k f -> p (k f)")
                pool.tensor_tensor(low[0:parts, b, 0:rows, :].rearrange("p k f -> p (k f)"), v, upper(v),
                                   ALU.subtract).then_inc(low_ready, 1)

            def chunk(c, s, i):
                if before(c, FULL_CHUNKS - 2):
                    low_part(c + 2, s % 2, P, SPL)
                elif c == FULL_CHUNKS - 2:
                    low_part(c + 2, s % 2, LAST_PARTS, (TAIL_GROUPS - WHOLE) * ROWS_PER_PART)
                if s == 1 and before(c, FULL_CHUNKS - 1):
                    ln_pair(i, 2)
                if isinstance(c, int) and c == FULL_CHUNKS - 2:
                    ln_pair(EDGE_TRIPS, 1)

            low_part(0, 0, P, SPL)
            low_part(1, 1, P, SPL)
            run_steps(pool, chunk, CHUNKS, 1, EDGE_TRIPS - 2)

            pool.wait_ge(edges_done, 2)
            pool.wait_ge(b3_in, 16)

            def add_b3(i, n):
                pool.tensor_tensor(tiles_of(i * 4, n), tiles_of(i * 4, n),
                                   b3_bc.unsqueeze(1).broadcast_to([P, n, F]), ALU.add).then_inc(xb3_ready, 1)

            def rstd_chunk(i, n):
                rstd(mv4[:, 0:n, 1], rstd2[:, bass.ds(i * 4, n)], n, mv2_ready, i * 4 + n, var2_ready,
                     rstd2_ready, i + 1)

            add_b3(0, 4)
            pool.wait_ge(h1x_ready, 2 * (EDGE_TRIPS + 1))
            pool.memset(blk_s, 0.0).then_inc(blk_clear, 1)
            add_b3(1, 4)
            rstd_chunk(0, 4)
            with pool.Fori(1, MLP_CHUNKS - 1) as i:
                add_b3(i + 1, 4)
                pool.wait_ge(rstd2_ready, i)
                rstd_chunk(i, 4)
            add_b3(MLP_CHUNKS, 1)
            pool.wait_ge(rstd2_ready, MLP_CHUNKS - 1)
            rstd_chunk(MLP_CHUNKS - 1, 4)

            pool.wait_ge(xb3_ready, MLP_CHUNKS + 1)
            pool.memset(sw_sum, 0.0).then_inc(sw_summed, 1)

            def soft_step(t, s, i):
                if before(t, TILES):
                    pool.wait_ge(max_ready, t + 1)
                    v = soft[:, s, :].rearrange("p (h g) -> p h g", h=H)
                    pool.tensor_tensor(v, v, mx[:, s, :].unsqueeze(2).broadcast_to([P, H, G]),
                                       ALU.subtract).then_inc(shifted, 1)
                if isinstance(t, int) and t == 0:
                    pool.wait_ge(rstd2_ready, MLP_CHUNKS)
                    rstd_chunk(MLP_CHUNKS, 1)
                if past(t, 1) and before(t, TILES + 1):
                    pool.wait_ge(sw_ready, t)
                    pool.wait_ge(sw_summed, t)
                    pool.tensor_tensor(sw_sum, sw_sum, soft[:, (s - 1) % UNROLL, :], ALU.add).then_inc(sw_summed, 1)

            run_steps(pool, soft_step, TILES + 1, 1, (TILES - 1) // UNROLL - 1)

            pool.wait_ge(sw_tp, TILES)
            pool.wait_ge(sw_summed, TILES + 1)
            pool.memset(v_blk, 0.0).then_inc(att_clear, 1)
            pool.memset(a_blk, 0.0).then_inc(att_clear, 1)

            pool.wait_ge(late_in, 16 * 9)
            pool.wait_ge(att_t, 8)

            def residual(t, s, i):
                if past(t, UNROLL):
                    pool.wait_ge(y_ready, t - UNROLL + 1)
                pool.tensor_tensor(xo[:, s, :], x_sb[:, bass.ds(t, 1), :].rearrange("p a f -> p (a f)"),
                                   bout_bc, ALU.add).then_inc(xo_ready, 1)

            run_steps(pool, residual, TILES, 1, MLP_CHUNKS - 1)

        @block.scalar
        def _(act):
            act.dma_start(w1a_sb[:, :, :], w1[0:F, :].rearrange("(k p) n -> p k n", p=P)).then_inc(mlp_in, 16)
            act.dma_start(b1_sb[:, :], b1.rearrange("(m p) -> p m", p=P), allow_slow_non_contiguous=True).then_inc(mlp_in, 16)
            act.dma_start(b2_sb[:, :], b2.rearrange("(m p) -> p m", p=P), allow_slow_non_contiguous=True).then_inc(mlp_in, 16)
            act.wait_ge(mlp_in, 16 * 3)

            def norm_rows(i, n):
                act.wait_ge(rstd1_ready, i + 1)
                for a in range(n):
                    act.activation(xn[:, a, :], x_sb[:, bass.ds(i * 2 + a, 1), :].rearrange("p a f -> p (a f)"),
                                   ACT.Identity, bias=shift1[:, a:a + 1], scale=rstd1[:, a:a + 1]).then_inc(xn1_ready, 1)

            def copy_ln_t(i, n, bank):
                act.wait_ge(ln_tp, i + 1)
                act.activation(ln_t[:, :, 0:n * P], ps[:, bank, :].rearrange("p (k c) -> p k c", k=KF)[:, :, 0:n * P],
                               ACT.Copy).then_inc(ln_t_ready, 1)

            def copy_h1x(i, n, banks):
                for m in range(KF):
                    act.wait_ge(h1x_psum, i * 2 + (m + 1))
                    act.activation(h1x[:, m, bass.ds(i * 2 * P, n * P)], ps[:, banks[m], m * 256:m * 256 + n * P],
                                   ACT.Identity, bias=b1_sb[:, m:m + 1]).then_inc(h1x_ready, 1)

            with act.Fori(0, EDGE_TRIPS - 1) as i:
                norm_rows(i, 2)
                copy_ln_t(i, 2, 4)
                copy_h1x(i, 2, (5, 5))
            norm_rows(EDGE_TRIPS - 1, 2)
            copy_ln_t(EDGE_TRIPS - 1, 2, 4)
            norm_rows(EDGE_TRIPS, 1)
            copy_h1x(EDGE_TRIPS - 1, 2, (5, 6))
            copy_ln_t(EDGE_TRIPS, 1, 7)
            copy_h1x(EDGE_TRIPS, 1, (5, 6))

            def relus(i, cols, halves):
                act.wait_ge(h1_sum, i + 1)
                act.activation(h1_t[:, :, 0:cols], h1_t[:, :, 0:cols], ACT.Relu).then_inc(h1_ready, 1)
                act.wait_ge(l2_psum, i + 1)
                for m in range(KF):
                    act.activation(h2_t[:, m, 0:cols], halves[m], ACT.Relu,
                                   bias=b2_sb[:, m:m + 1]).then_inc(h2_ready, 1)

            with act.Fori(0, MLP_CHUNKS) as i:
                relus(i, 4 * P, [ps[:, 2 + m, :] for m in range(KF)])

            def copy_xn_t(t, b):
                act.wait_ge(tp_ready, t + 1)
                act.activation(xn_t[:, b], ps[:, 2 + b, 0:2 * P].rearrange("p (k n) -> p k n", k=KF),
                               ACT.Copy).then_inc(xn_t_ready, 1)

            def soft_step(t, s, i):
                if past(t, 3):
                    act.wait_ge(sw_tp, t - 2)
                    act.activation(sw_t[:, :, bass.ds((t - 3) * P, P)],
                                   ps[:, 6 + (s - 3) % 2, :].rearrange("p (j n) -> p j n", j=PAIRS),
                                   ACT.Copy).then_inc(sw_t_ready, 1)
                if before(t, TILES - 1):
                    if past(t, 1):
                        act.wait_ge(logits_ready, t)
                    copy_xn_t(t + 1, (s + 1) % 2)
                if before(t, TILES):
                    act.wait_ge(shifted, t + 1)
                    act.activation(soft[:, s, :], soft[:, s, :], ACT.Exp).then_inc(exp_ready, 1)

            copy_xn_t(0, 0)
            relus(MLP_CHUNKS, P, [ps[:, 3, m * P:(m + 1) * P] for m in range(KF)])
            run_steps(act, soft_step, TILES + 3, 2, (TILES - 1) // UNROLL - 2)

            act.wait_ge(sw_tp, TILES)
            act.activation(s_t[:, 1, :], ps[:, 5, :], ACT.Copy).then_inc(att_a, 1)
            act.wait_ge(att_clear, 2)
            act.wait_ge(att_p, 1)
            act.activation(q_t[0:D, :], ps[0:D, 0, :], ACT.Copy, scale=SCALE).then_inc(att_a, 1)
            act.wait_ge(att_v, 13)
            act.activation(att[0:G, :], att[0:G, :], ACT.Exp).then_inc(att_a, 1)
            act.wait_ge(att_t, 5)
            act.activation(vw, ps[:, 4:6, :].rearrange("p b (j f) -> p (b j) f", f=F), ACT.Copy).then_inc(att_a, 1)
            act.wait_ge(att_t, 6)
            act.activation(a_blk[G:2 * G, :, G:2 * G], ps[G:2 * G, 6, 0:PAIRS * G].rearrange("p (j g) -> p j g", j=PAIRS),
                           ACT.Copy).then_inc(att_a, 1)

            def stage_step(t, s, i):
                if not past(t, UNROLL):
                    return
                if past(t, 2 * UNROLL):
                    act.wait_ge(y_psum, t - UNROLL + 1)
                act.activation(stage[:, s, :].rearrange("p (j n) -> p j n", j=PAIRS),
                               sw_t[:, :, bass.ds(t * P, P)], ACT.Copy).then_inc(staged, 1)

            act.wait_ge(att_t, 8)
            run_steps(act, stage_step, TILES, 2, MLP_CHUNKS - 2)

        @block.vector
        def _(dve):
            done = [0]

            def then(ins):
                ins.then_inc(prep_v, 1)
                done[0] += 1
                return done[0]

            def one_hot(dest, c, first, n, done):
                where = rel[:, bass.ds(c * CHUNK_GROUPS + first, n), :].rearrange("p g k -> p (g k)")
                shape = [P, n * ROWS_PER_PART, WINDOW]
                dve.tensor_tensor(dest, iota_w[:, :].unsqueeze(1).broadcast_to(shape),
                                  where.unsqueeze(2).broadcast_to(shape), ALU.is_equal).then_inc(done, 1)

            def hot_whole(c, b):
                one_hot(hot_f[:, b], c, 0, WHOLE, hot_ready)

            def hot_parts(c, b):
                one_hot(hot_b[:, b], c, WHOLE, SPLIT, hot_ready)

            def split_rest(c, s, i, parts, rows, loads):
                dve.wait_ge(edge_in[s], i * 16 + loads * 16)
                v = ring[0:parts, s, WHOLE:, :, :].rearrange("p g k f -> p (g k f)")[:, 0:rows * F]
                dve.tensor_tensor(rest[0:parts, s % 2, 0:rows, :].rearrange("p k f -> p (k f)"), v, upper(v),
                                  ALU.subtract).then_inc(rest_ready, 1)

            dve.memset(agg[:, 0, 0:CLEAR_V], 0.0).then_inc(agg_clear, 1)
            dve.wait_ge(dst_in, 16 * 4)
            dve.wait_ge(prep_v, then(dve.tensor_copy(dst_f, dst_i)))
            dve.wait_ge(prep_v, then(dve.tensor_reduce(base_col[:, :], dst_f, AX.X, ALU.min)))
            dve.wait_ge(prep_v, then(dve.tensor_scalar(base_col[:, :], base_col[:, :], 0.0, float(N), ALU.max, ALU.min)))
            for t in range(GTILES):
                n = then(dve.tensor_scalar(rel_g[:, t, :], dst_f[:, t, :], base_col[:, t:t + 1], None, ALU.subtract))
            split_rest(0, 0, 0, P, SPL, 1)
            dve.wait_ge(prep_v, n)
            dve.wait_ge(prep_v, then(dve.tensor_reduce(far_col[:, :], rel_g, AX.X, ALU.max)))
            then(dve.tensor_reduce(far_one[:, :], far_col[:, :], AX.X, ALU.max))
            dve.wait_ge(agg_clear, 3)
            dve.wait_ge(consts, 7)
            dve.tensor_scalar(row_ok[:, :], row_no[:, :], float(LAST_ROWS), None, ALU.is_lt).then_inc(groups_added, CREDIT)
            dve.wait_ge(prep_t, 1)
            for k in range(ROWS_PER_PART):
                for t in range(GTILES):
                    n = min(P, CHUNKS * CHUNK_GROUPS - t * P)
                    in_table = then(dve.tensor_copy(rel[:, t * P:t * P + n, k], ps[:, 6 + k, t * P:t * P + n]))
            dve.wait_ge(prep_v, in_table)
            hot_whole(0, 0)
            hot_parts(0, 0)
            split_rest(1, 1, 0, P, SPL, 1)
            hot_whole(1, 1)
            hot_parts(1, 1)
            dve.wait_ge(prep_t, 2)
            then(dve.tensor_copy(base_i[0:1, :], ps[0:1, 5, :]))
            dve.wait_ge(prep_v, then(dve.tensor_reduce(far_col[0:1, 0:1], ps[0:1, 4, 0:P], AX.X, ALU.max)))
            table = then(dve.tensor_scalar(far_i[0:1, 0:1], far_col[0:1, 0:1], float(WINDOW), None, ALU.is_ge))
            dve.wait_ge(prep_v, table)
            base_regs = [dve.alloc_register(f"base{n}") for n in range(UNROLL * CHUNK_GROUPS)]
            base_of = [None] * len(base_regs)

            def norm_stats(i, a):
                dve.bn_stats(bn6[:, a, :], x_sb[:, bass.ds(i * 2 + a, 1), :].rearrange("p a f -> p (a f)")
                             ).then_inc(bn_done, 1)

            def norm_sums(i, n):
                dve.wait_ge(bn_done, i * 2 + n)
                dve.tensor_copy(carrier[:, :], bn6[:, 0, 0:1])
                for a in range(n):
                    dve.bn_aggr(mv1[:, a, :], bn6[:, a, :]).then_inc(mv1_ready, 1)

            def prepare(c, s, i, step):
                if step == 0 and before(c, FULL_CHUNKS - 2):
                    split_rest(c + 2, (s + 2) % UNROLL, i if s < 2 else i + 1, P, SPL, 1)
                elif step == 0 and c == FULL_CHUNKS - 2:
                    split_rest(c + 2, (s + 2) % UNROLL, (c + 2) // UNROLL, LAST_PARTS,
                               (TAIL_GROUPS - WHOLE) * ROWS_PER_PART, 2)
                if step == 1 and before(c, CHUNKS - 2):
                    hot_whole(c + 2, s % 2)
                if step == 2 and before(c, CHUNKS - 2):
                    hot_parts(c + 2, s % 2)

            def chunk(c, s, i):
                dve.wait_ge(sums_ready, c + 1)
                if s == 0:
                    if before(c, FULL_CHUNKS - 1):
                        prepare(c, s, i, 0)
                    dve.load(base_regs, base_i[0:1, bass.ds(i * (UNROLL * CHUNK_GROUPS), UNROLL * CHUNK_GROUPS)])
                    for n, r in enumerate(base_regs):
                        base_of[n] = dve.snap(r, min_val=0, max_val=N)
                for g in range(CHUNK_GROUPS if before(c, FULL_CHUNKS) else TAIL_GROUPS):
                    dve.wait_ge(groups_added, c * CHUNK_GROUPS + (CREDIT + g))
                    win = agg[:, :, bass.ds(base_of[s * CHUNK_GROUPS + g], WINDOW)]
                    dve.tensor_tensor(win, win, ps[:, s, g * P:(g + 1) * P].rearrange("p (h n) -> p h n", h=KF),
                                      ALU.add).then_inc(groups_added, 1)
                    if before(c, FULL_CHUNKS - 1):
                        prepare(c, s, i, g + 1 if s == 0 else g)
                if before(c, FULL_CHUNKS - 1):
                    if s == 0:
                        dve.wait_ge(x_in, i * 16 + 16)
                    if s < 2:
                        norm_stats(i, s)
                    if s == 1:
                        norm_sums(i, 2)
                if isinstance(c, int) and c == FULL_CHUNKS - 2:
                    dve.wait_ge(x_tail_in, 16)
                    norm_stats(EDGE_TRIPS, 0)
                    dve.wait_ge(rstd1_ready, EDGE_TRIPS)
                    norm_sums(EDGE_TRIPS, 1)

            run_steps(dve, chunk, CHUNKS, 0, EDGE_TRIPS - 1)
            dve.wait_ge(groups_added, CREDIT + GROUPS)
            dve.drain().then_inc(edges_done, 1)

            far = dve.value_load(far_i[0:1, 0:1], min_val=0, max_val=1)
            with dve.If(far > 0):
                for n in range(512 // WINDOW):
                    dve.tensor_scalar(g_iota[:, n * WINDOW:(n + 1) * WINDOW], iota_w[:, :], float(n * WINDOW), None,
                                      ALU.add).then_inc(gen_v, 1)
                dve.wait_ge(gen_v, 8)
                dve.drain().then_inc(gen_group, 1)
                PER_GROUP = 3 + WIDES

                def far_group(g, parts):
                    step = g * PER_GROUP + 8
                    dve.wait_ge(gen_d_in, g * 16 + 16)
                    dve.tensor_copy(g_abs[0:parts, :], g_dst[0:parts, :]).then_inc(gen_v, 1)
                    dve.tensor_scalar(g_cov[0:parts, :], rel[0:parts, bass.ds(g, 1), :].rearrange("p g k -> p (g k)"),
                                      float(WINDOW), float(4 * AGG), ALU.is_lt, ALU.mult).then_inc(gen_v, 1)
                    dve.wait_ge(gen_v, step + 2)
                    dve.tensor_tensor(g_abs[0:parts, :], g_abs[0:parts, :], g_cov[0:parts, :], ALU.add).then_inc(gen_v, 1)
                    for w in range(WIDES):
                        dve.wait_ge(gen_v, step + (3 + w))
                        dve.tensor_scalar(g_win[0:parts, :], g_abs[0:parts, :], float(w * WIDE), None,
                                          ALU.subtract).then_inc(gen_v, 1)
                        dve.wait_ge(gen_v, step + (4 + w))
                        for k in range(ROWS_PER_PART):
                            dve.tensor_scalar(g_hot[0:parts, k, :], g_iota[0:parts, :], g_win[0:parts, k:k + 1], None,
                                              ALU.is_equal).then_inc(gen_hot, 1)
                        dve.wait_ge(gen_sums, g * WIDES + (w + 1))
                        view = agg[:, :, w * WIDE:(w + 1) * WIDE]
                        last = dve.tensor_tensor(view, view, ps[:, 0:2, 0:WIDE], ALU.add)
                        last.then_inc(groups_added, 1)
                        dve.wait_ge(groups_added, g * WIDES + (CREDIT + GROUPS + w + 1))
                    dve.memset(g_cov, 0.0).then_inc(gen_group, 1)

                with dve.Fori(0, GROUPS - 1) as g:
                    far_group(g, P)
                far_group(GROUPS - 1, LAST_PARTS)
            dve.drain().then_inc(edges_done, 1)

            def add_h1(i, cols):
                dve.wait_ge(l1_psum, i + 1)
                dve.tensor_tensor(h1_t[:, :, 0:cols], ps[:, 0:2, 0:cols], h1x[:, :, bass.ds(i * 4 * P, cols)],
                                  ALU.add).then_inc(h1_sum, 1)

            def residual(i, n):
                if past(i, 1):
                    dve.wait_ge(var2_ready, i)
                dve.wait_ge(xb3_ready, i + 1)
                dve.wait_ge(l3_psum, i + 1)
                rows = tiles_of(i * 4, n)
                dve.tensor_tensor(rows, rows, ps[:, 4:6, :].rearrange("p b (t f) -> p (b t) f", f=F)[:, 0:n, :],
                                  ALU.add).then_inc(x2_ready, 1)
                dve.wait_ge(consts, 7)
                dve.wait_ge(x2_ready, i + 1)
                for a in range(n):
                    dve.bn_stats(bn6[:, a, :], x_sb[:, bass.ds(i * 4 + a, 1), :].rearrange("p a f -> p (a f)")
                                 ).then_inc(bn2_done, 1)
                dve.wait_ge(bn2_done, i * 4 + n)
                dve.tensor_copy(carrier[:, :], bn6[:, 0, 0:1])
                for a in range(n):
                    dve.bn_aggr(mv4[:, a, :], bn6[:, a, :]).then_inc(mv2_ready, 1)
                dve.wait_ge(mv2_ready, i * 4 + n)
                dve.tensor_copy(mean2[:, bass.ds(i * 4, n)], mv4[:, 0:n, 0]).then_inc(mean2_ready, 1)

            def heads(v):
                return v.rearrange("p (h g) -> p h g", h=H)

            folded = [0]

            def fold_step(ins):
                ins.then_inc(fold_v, 1)
                folded[0] += 1
                return folded[0]

            dve.wait_ge(h1x_ready, 2 * EDGE_TRIPS)
            add_h1(0, 4 * P)
            add_h1(1, 4 * P)
            residual(0, 4)
            dve.wait_ge(fold_in, 16 * 6)
            dve.wait_ge(fold_v, fold_step(dve.tensor_scalar(inv_temp, temp_bc, 0.1, 5.0, ALU.max, ALU.min)))
            fold_step(dve.reciprocal(inv_temp, inv_temp))
            fold_step(dve.tensor_copy(bx_rep, bx_col.unsqueeze(2).broadcast_to([P, PAIRS, P])))
            dve.wait_ge(fold_t, 1)
            for k in range(KF):
                fold_step(dve.tensor_copy(wx_t[:, k].rearrange("p j n -> p (j n)"), ps[:, 6 + k, :]))
            add_h1(2, 4 * P)
            residual(1, 4)
            inv_all = inv_temp.unsqueeze(2).broadcast_to([P, H, G])
            dve.wait_ge(fold_t, 2)
            for k in range(KF):
                fold_step(dve.tensor_tensor(heads(wc[:, k, :]), heads(ps[:, 6 + k, :]), inv_all, ALU.mult))
            add_h1(3, 4 * P)
            residual(2, 4)
            dve.wait_ge(fold_t, 3)
            dve.wait_ge(fold_v, fold_step(dve.tensor_tensor(heads(c_bc), heads(ps[:, 6, :]),
                                                            bsl_bc.unsqueeze(1).broadcast_to([P, H, G]), ALU.add)))
            fold_step(dve.tensor_tensor(heads(c_bc), heads(c_bc), inv_all, ALU.mult))
            with dve.Fori(3, MLP_CHUNKS - 1) as i:
                add_h1(i + 1, 4 * P)
                residual(i, 4)
            dve.wait_ge(h1x_ready, 2 * (EDGE_TRIPS + 1))
            add_h1(MLP_CHUNKS, P)

            def normalise(t, s):
                if past(t, UNROLL):
                    dve.wait_ge(xn_used, t - UNROLL + 1)
                dve.tensor_scalar(xn[:, s, :], x_sb[:, bass.ds(t, 1), :].rearrange("p a f -> p (a f)"),
                                  mean2[:, bass.ds(t, 1)], rstd2[:, bass.ds(t, 1)], ALU.subtract, ALU.mult
                                  ).then_inc(xn2_ready, 1)

            def soft_step(t, s, i):
                if isinstance(t, int) and t == 1:
                    residual(MLP_CHUNKS, 1)
                if isinstance(t, int) and t == 3:
                    dve.wait_ge(rstd2_ready, MLP_CHUNKS + 1)
                if past(t, 1) and before(t, TILES - 1):
                    normalise(t + 1, (s + 1) % UNROLL)
                if before(t, TILES):
                    dve.wait_ge(logits_ready, t + 1)
                    if past(t, UNROLL):
                        dve.wait_ge(sw_tp, t - UNROLL + 1)
                        dve.wait_ge(sw_summed, t - UNROLL + 2)
                    dve.tensor_tensor(soft[:, s, :], ps[:, s % 2, :], c_bc, ALU.add).then_inc(biased, 1)
                    dve.wait_ge(biased, t + 1)
                    dve.tensor_reduce(mx[:, s, :], heads(soft[:, s, :]), AX.X, ALU.max).then_inc(max_ready, 1)
                if past(t, 1):
                    r = (s - 1) % UNROLL
                    dve.wait_ge(exp_ready, t)
                    dve.tensor_reduce(sm[:, r, :], heads(soft[:, r, :]), AX.X, ALU.add).then_inc(total_ready, 1)
                    dve.wait_ge(total_ready, t)
                    dve.reciprocal(rc[:, r, :], sm[:, r, :]).then_inc(recip_ready, 1)
                    dve.wait_ge(recip_ready, t)
                    if isinstance(t, int) and t == TILES:
                        dve.tensor_scalar(rc[:, r, :], rc[:, r, :], row_ok[:, 0:1], None, ALU.mult).then_inc(recip_ready, 1)
                        dve.wait_ge(recip_ready, t + 1)
                    dve.tensor_tensor(heads(soft[:, r, :]), heads(soft[:, r, :]),
                                      rc[:, r, :].unsqueeze(2).broadcast_to([P, H, G]), ALU.mult).then_inc(sw_ready, 1)

            dve.wait_ge(rstd2_ready, MLP_CHUNKS - 1)
            dve.wait_ge(fold_t, 3)
            normalise(0, 0)
            normalise(1, 1)
            residual(MLP_CHUNKS - 1, 4)
            dve.wait_ge(fold_v, 9)
            run_steps(dve, soft_step, TILES + 1, 1, (TILES - 1) // UNROLL - 1)

            n_att = [0]

            def att_step(ins):
                ins.then_inc(att_v, 1)
                n_att[0] += 1
                return n_att[0]

            dve.wait_ge(sw_tp, TILES)
            att_step(dve.tensor_copy(s_t[:, 0, :], ps[:, 4, :]))
            dve.wait_ge(att_t, 1)
            dve.wait_ge(late_in, 16 * 9)
            n = att_step(dve.tensor_copy(norm, ps[:, 0, 0:PAIRS]))
            dve.wait_ge(att_v, n)
            att_step(dve.tensor_scalar(rnorm, norm, EPS_NORM, None, ALU.add))
            n = att_step(dve.tensor_tensor(nb, bfx_bc, norm.unsqueeze(2).broadcast_to([P, PAIRS, D]), ALU.mult))
            dve.wait_ge(att_v, n)
            n = att_step(dve.reciprocal(rnorm, rnorm))
            dve.wait_ge(att_t, 2)
            tp = ps[:, 1, :].rearrange("p (j c) -> p j c", j=PAIRS)
            for hh in range(2):
                rows = slice(hh * G, (hh + 1) * G)
                n = att_step(dve.tensor_tensor(tok[rows], tp[rows, :, hh * D:(hh + 1) * D], nb[rows], ALU.add))
            dve.wait_ge(att_v, n)
            att_step(dve.tensor_tensor(tok, tok, rnorm.unsqueeze(2).broadcast_to([P, PAIRS, D]), ALU.mult))
            dve.wait_ge(att_t, 3)
            att_step(dve.tensor_copy(tok_t[0:D, :], ps[0:D, 2, :]))
            dve.wait_ge(att_clear, 2)
            dve.wait_ge(att_p, 2)
            att_step(dve.tensor_copy(k_t[0:D, :], ps[0:D, 1, :]))
            dve.wait_ge(att_p, 3)
            vp = ps[:, 3, :].rearrange("p (j n) -> p j n", j=PAIRS)
            for hh in range(2):
                rows = slice(hh * D, (hh + 1) * D)
                n_v = att_step(dve.tensor_copy(v_blk[rows, :, hh * G:(hh + 1) * G], vp[rows, :, hh * G:(hh + 1) * G]))
            dve.wait_ge(att_t, 4)
            at3 = att[0:G, :].rearrange("p (h g) -> p h g", h=H)
            sp3 = ps[0:G, 2, :].rearrange("p (h g) -> p h g", h=H)
            dve.tensor_reduce(att_mx[0:G, :], sp3, AX.X, ALU.max).then_inc(biased, 1)
            dve.wait_ge(biased, TILES + 1)
            att_step(dve.tensor_tensor(at3, sp3, att_mx[0:G, :].unsqueeze(2).broadcast_to([G, H, G]), ALU.subtract))
            dve.wait_ge(att_a, 3)
            n = att_step(dve.tensor_reduce(att_sm[0:G, :], at3, AX.X, ALU.add))
            dve.wait_ge(att_v, n)
            for hh in range(2):
                att_step(dve.reciprocal(att_rc[hh * G:(hh + 1) * G, :],
                                        att_sm[0:G, :].rearrange("p (j h) -> p h j", h=2)[:, hh, :]))
            dve.wait_ge(att_t, 6)
            att_step(dve.tensor_copy(a_blk[0:G, :, 0:G],
                                     ps[0:G, 6, 0:PAIRS * G].rearrange("p (j g) -> p j g", j=PAIRS)))
            for b in range(2):
                dve.wait_ge(att_t, 7 + b)
                if b == 0:
                    dve.wait_ge(att_v, 16)
                att_step(dve.tensor_tensor(m_blk[:, 2 * b:2 * b + 2, :], ps[:, 4 + b, :].rearrange("p (j f) -> p j f", f=F),
                                           att_rc[:, 2 * b:2 * b + 2].unsqueeze(2).broadcast_to([P, 2, F]), ALU.mult))

            def finish(t, s, i):
                dve.wait_ge(y_psum, t + 1)
                dve.wait_ge(xo_ready, t + 1)
                if past(t, UNROLL):
                    dve.wait_ge(y_out[s // 2], i * 16)
                dve.tensor_tensor(o_sb[:, s, :], ps[:, s, 0:F], xo[:, s, :], ALU.add).then_inc(y_ready, 1)

            run_steps(dve, finish, TILES, 1, MLP_CHUNKS - 1)

        @block.tensor
        def _(pe):
            mm = nc.tensor.matmul
            tr = nc.tensor.transpose
            pe.wait_ge(consts, 7)

            def keep_busy(times, blocks, bank):
                for _ in range(times):
                    mm(ps[:, bank, 0:blocks * P].rearrange("p (a n) -> p a n", n=P), lhsT=ident[:, :],
                       rhs=ident[:, :].unsqueeze(1).broadcast_to([P, blocks, P]), start=True, stop=True)

            keep_busy(7, 4, 3)
            pe.wait_ge(prep_v, 7)
            for k in range(ROWS_PER_PART):
                for t in range(GTILES):
                    src = rel_g[:, t, :].rearrange("p (e k) -> p k e", k=ROWS_PER_PART)[:, k, :]
                    last = tr(ps[:, 6 + k, t * P:(t + 1) * P], src, ident[:, :])
            last.then_inc(prep_t, 1)
            pe.wait_ge(prep_v, 9)
            for t in range(GTILES):
                tr(ps[0:1, 5, t * P:(t + 1) * P], base_col[:, t:t + 1], ident[:, :])
            tr(ps[0:1, 4, 0:P], far_one[:, 0:1], ident[:, :]).then_inc(prep_t, 1)
            keep_busy(2, 4, 3)

            def chunk(c, s, i):
                pe.wait_ge(hot_ready, c * 2 + 2)
                if before(c, FULL_CHUNKS):
                    pe.wait_ge(edge_in[s], i * 16 + 16)
                else:
                    pe.wait_ge(edge_in[s], i * 16 + 32)
                pe.wait_ge(groups_added, c * CHUNK_GROUPS + (CREDIT - (UNROLL - 1) * CHUNK_GROUPS))
                groups = CHUNK_GROUPS if before(c, FULL_CHUNKS) else TAIL_GROUPS
                for g in range(groups):
                    parts = P if before(c, FULL_CHUNKS) or g < groups - 1 else LAST_PARTS
                    if g == WHOLE:
                        pe.wait_ge(low_ready, c + 1)
                    for h in range(KF):
                        cols = slice(h * P, (h + 1) * P)
                        terms = []
                        if g < WHOLE:
                            for k in range(ROWS_PER_PART):
                                terms.append((ring[0:parts, s, g, k, cols],
                                              hot_f[0:parts, s % 2, g * ROWS_PER_PART + k, :]))
                        else:
                            for k in range(ROWS_PER_PART):
                                n = (g - WHOLE) * ROWS_PER_PART + k
                                for v in (upper(ring[0:parts, s, g, k, cols]), upper(rest[0:parts, s % 2, n, cols]),
                                          low[0:parts, s % 2, n, cols]):
                                    terms.append((v, hot_b[0:parts, s % 2, n, :]))
                        for n, (v, hot) in enumerate(terms):
                            last = mm(ps[:, s, g * P + h * WINDOW:g * P + (h + 1) * WINDOW], lhsT=v, rhs=hot,
                                      start=(n == 0), stop=(n == len(terms) - 1))
                last.then_inc(sums_ready, 1)
                if past(c, UNROLL):
                    if isinstance(c, int) and c == UNROLL:
                        pe.wait_ge(prep_v, 19)
                        pe.wait_ge(mlp_in, 16 * 3)
                    if s == 1:
                        ln_transposes(i - 1, 2)
                    if s >= 2:
                        first_layer_x(i - 1, 2, s - 2)

            def ln_transposes(i, n, bank=4):
                pe.wait_ge(xn1_ready, i * 2 + n)
                for a in range(n):
                    for k in range(KF):
                        last = tr(ps[:, bank, k * 256 + a * P:k * 256 + (a + 1) * P], xn[:, a, k * P:(k + 1) * P],
                                  ident[:, :])
                last.then_inc(ln_tp, 1)

            def first_layer_x(i, n, m, bank=5):
                if m == 0:
                    pe.wait_ge(ln_t_ready, i + 1)
                elif bank == 5:
                    pe.wait_ge(h1x_ready, i * 2 + 1)
                for k in range(KF):
                    last = mm(ps[:, bank, m * 256:m * 256 + n * P], lhsT=w1a_sb[:, k, m * P:(m + 1) * P],
                              rhs=ln_t[:, k, 0:n * P], start=(k == 0), stop=(k == KF - 1))
                last.then_inc(h1x_psum, 1)

            run_steps(pe, chunk, CHUNKS, 1, EDGE_TRIPS - 1)
            first_layer_x(EDGE_TRIPS - 1, 2, 0)
            first_layer_x(EDGE_TRIPS - 1, 2, 1, bank=6)
            ln_transposes(EDGE_TRIPS, 1, bank=7)

            pe.wait_ge(edges_done, 1)
            far = pe.value_load(far_i[0:1, 0:1], min_val=0, max_val=1)

            def far_group(g, parts):
                pe.wait_ge(gen_e_in, g * 16 + 16)
                for w in range(WIDES):
                    pe.wait_ge(gen_hot, g * (2 * WIDES) + (2 * w + 2))
                    for h in range(KF):
                        for k in range(ROWS_PER_PART):
                            last = mm(ps[:, h, 0:WIDE], lhsT=ring[0:parts, 0, 0, k, h * P:(h + 1) * P],
                                      rhs=g_hot[0:parts, k, 0:WIDE], start=(k == 0), stop=(k == ROWS_PER_PART - 1))
                    last.then_inc(gen_sums, 1)

            with pe.If(far > 0):
                with pe.Fori(0, GROUPS - 1) as g:
                    far_group(g, P)
                far_group(GROUPS - 1, LAST_PARTS)
            pe.wait_ge(edges_done, 2)

            def layer1(i, cols):
                for m in range(KF):
                    for k in range(KF):
                        last = mm(ps[:, m, 0:cols], lhsT=w1b_sb[:, k, m * P:(m + 1) * P],
                                  rhs=agg[:, k, bass.ds(i * 4 * P, cols)], start=(k == 0), stop=(k == KF - 1))
                last.then_inc(l1_psum, 1)

            def layer2(i, cols, halves):
                pe.wait_ge(h1_ready, i + 1)
                for m in range(KF):
                    for k in range(KF):
                        last = mm(halves[m], lhsT=w2_sb[:, k, m * P:(m + 1) * P],
                                  rhs=h1_t[:, k, 0:cols], start=(k == 0), stop=(k == KF - 1))
                last.then_inc(l2_psum, 1)

            def layer3(i, n):
                pe.wait_ge(h2_ready, i * 2 + 2)
                if past(i, 1):
                    pe.wait_ge(x2_ready, i)
                for a in range(n):
                    for k in range(KF):
                        last = mm(ps[:, 4 + a // 2, (a % 2) * F:(a % 2 + 1) * F],
                                  lhsT=h2_t[:, k, a * P:(a + 1) * P], rhs=w3_sb[:, k, :],
                                  start=(k == 0), stop=(k == KF - 1))
                last.then_inc(l3_psum, 1)

            l2_banks = [ps[:, 2 + m, :] for m in range(KF)]
            pe.wait_ge(w1b_in, 16)
            layer1(0, 4 * P)
            for m in range(KF):
                first_layer_x(EDGE_TRIPS, 1, m, bank=5 + m)
            pe.wait_ge(w23_in, 32)
            layer2(0, 4 * P, l2_banks)
            layer1(1, 4 * P)
            layer3(0, 4)
            pe.wait_ge(fold_in, 16 * 6)
            for k in range(KF):
                for j in range(PAIRS):
                    last = tr(ps[:, 6 + k, j * P:(j + 1) * P], wx[:, k, j * P:(j + 1) * P], ident[:, :])
            last.then_inc(fold_t, 1)
            layer2(1, 4 * P, l2_banks)
            layer1(2, 4 * P)
            layer3(1, 4)
            pe.wait_ge(fold_v, 5)
            for j in range(PAIRS):
                for k in range(KF):
                    last = mm(ps[:, 6 + k, j * P:(j + 1) * P], lhsT=wx_t[:, k, j, :], rhs=blk_s, start=True, stop=True)
            last.then_inc(fold_t, 1)
            layer2(2, 4 * P, l2_banks)
            layer1(3, 4 * P)
            layer3(2, 4)
            pe.wait_ge(fold_v, 7)
            for j in range(PAIRS):
                last = mm(ps[:, 6, j * P:(j + 1) * P], lhsT=bx_rep[:, j, :], rhs=blk_s, start=True, stop=True)
            last.then_inc(fold_t, 1)
            with pe.Fori(3, MLP_CHUNKS - 1) as i:
                layer2(i, 4 * P, l2_banks)
                layer1(i + 1, 4 * P)
                layer3(i, 4)
            layer2(MLP_CHUNKS - 1, 4 * P, l2_banks)
            layer1(MLP_CHUNKS, P)
            layer3(MLP_CHUNKS - 1, 4)

            def tp_rows(t, s):
                pe.wait_ge(xn2_ready, t + 1)
                for k in range(KF):
                    last = tr(ps[:, 2 + s % 2, k * P:(k + 1) * P], xn[:, s, k * P:(k + 1) * P], ident[:, :])
                last.then_inc(tp_ready, 1)

            def soft_step(t, s, i):
                r = (s - 3) % UNROLL
                if past(t, 3):
                    pe.wait_ge(sw_ready, t - 2)
                    for k in range(KF):
                        last = mm(ps[:, 4 + k, :], lhsT=xn[:, r, k * P:(k + 1) * P], rhs=soft[:, r, :],
                                  start=isinstance(t, int) and t == 3, stop=isinstance(t, int) and t == TILES + 2)
                    last.then_inc(xn_used, 1)
                if before(t, TILES):
                    pe.wait_ge(xn_t_ready, t + 1)
                    if past(t, 2):
                        pe.wait_ge(biased, t - 1)
                    for k in range(KF):
                        last = mm(ps[:, s % 2, :], lhsT=xn_t[:, s % 2, k, :], rhs=wc[:, k, :],
                                  start=(k == 0), stop=(k == KF - 1))
                    last.then_inc(logits_ready, 1)
                if isinstance(t, int) and t == 0:
                    layer3(MLP_CHUNKS, 1)
                if past(t, 3):
                    if past(t, 5):
                        pe.wait_ge(sw_t_ready, t - 4)
                    for j in range(PAIRS):
                        last = tr(ps[:, 6 + (s - 3) % 2, j * P:(j + 1) * P], soft[:, r, j * P:(j + 1) * P], ident[:, :])
                    last.then_inc(sw_tp, 1)
                if before(t, TILES - 1):
                    tp_rows(t + 1, (s + 1) % UNROLL)

            tp_rows(0, 0)
            layer2(MLP_CHUNKS, P, [ps[:, 3, m * P:(m + 1) * P] for m in range(KF)])
            pe.wait_ge(fold_v, 9)
            run_steps(pe, soft_step, TILES + 3, 2, (TILES - 1) // UNROLL - 2)

            pe.wait_ge(sw_summed, TILES + 1)
            for j in range(PAIRS):
                last = mm(ps[:, 0, j:j + 1], lhsT=sw_sum[:, j * P:(j + 1) * P], rhs=ones[:, 0:1], start=True, stop=True)
            last.then_inc(att_t, 1)
            pe.wait_ge(att_v, 1)
            pe.wait_ge(att_a, 1)
            pe.wait_ge(late_in, 16 * 9)
            for j in range(PAIRS):
                for k in range(KF):
                    last = mm(ps[:, 1, j * P:(j + 1) * P], lhsT=s_t[:, k, j * P:(j + 1) * P],
                              rhs=wfx_sb[:, k, j * P:(j + 1) * P], start=(k == 0), stop=(k == KF - 1))
            last.then_inc(att_t, 1)
            pe.wait_ge(att_v, 8)
            for j in range(PAIRS):
                last = tr(ps[0:D, 2, j * P:(j + 1) * P], tok[:, j, :], ident[:, :])
            last.then_inc(att_t, 1)
            keep_busy(2, 2, 7)
            pe.wait_ge(att_v, 9)
            mm(ps[0:D, 0, :], lhsT=wq_sb[0:D, :], rhs=tok_t[0:D, :], start=True, stop=True).then_inc(att_p, 1)
            mm(ps[0:D, 1, :], lhsT=wk_sb[0:D, :], rhs=tok_t[0:D, :], start=True, stop=True).then_inc(att_p, 1)
            mm(ps[:, 3, :], lhsT=wv2_sb[0:D, :], rhs=tok_t[0:D, :], start=True, stop=True).then_inc(att_p, 1)
            pe.wait_ge(att_a, 2)
            pe.wait_ge(att_v, 10)
            for h in range(H):
                last = mm(ps[0:G, 2, h * G:(h + 1) * G], lhsT=q_t[0:D, h * G:(h + 1) * G],
                          rhs=k_t[0:D, h * G:(h + 1) * G], start=True, stop=True)
            last.then_inc(att_t, 1)
            pe.wait_ge(att_v, 12)
            for j in range(PAIRS):
                last = mm(ps[:, 4 + j // 2, (j % 2) * F:(j % 2 + 1) * F], lhsT=v_blk[:, j, :], rhs=wout_sb[:, j, :],
                          start=True, stop=True)
            last.then_inc(att_t, 1)
            keep_busy(2, 2, 7)
            pe.wait_ge(att_a, 3)
            for j in range(PAIRS):
                last = tr(ps[:, 6, j * G:(j + 1) * G], att[0:G, j * P:(j + 1) * P], ident[0:G, 0:G])
            last.then_inc(att_t, 1)
            keep_busy(1, 2, 7)
            pe.wait_ge(att_a, 5)
            pe.wait_ge(att_v, 17)
            for j in range(PAIRS):
                last = mm(ps[:, 4 + j // 2, (j % 2) * F:(j % 2 + 1) * F], lhsT=a_blk[:, j, :], rhs=vw[:, j, :],
                          start=True, stop=True)
                if j % 2 == 1:
                    last.then_inc(att_t, 1)

            def project(t, s, i):
                if past(t, UNROLL):
                    pe.wait_ge(staged, t - UNROLL + 1)
                    pe.wait_ge(y_ready, t - UNROLL + 1)
                for j in range(PAIRS):
                    if isinstance(t, int) and t == 0 and j % 2 == 0:
                        pe.wait_ge(att_v, 18 + j // 2)
                    rows = stage[:, s, j * P:(j + 1) * P] if past(t, UNROLL) else sw_t[:, j, t * P:(t + 1) * P]
                    last = mm(ps[:, s, 0:F], lhsT=rows, rhs=m_blk[:, j, :],
                              start=(j == 0), stop=(j == PAIRS - 1))
                last.then_inc(y_psum, 1)

            run_steps(pe, project, TILES, 1, MLP_CHUNKS - 1)


_INS = ['x', 'dst', 'edge_attr_256', 'L0_gnn_W1', 'L0_gnn_b1', 'L0_gnn_W2', 'L0_gnn_b2', 'L0_gnn_W3', 'L0_gnn_b3',
        'L0_ffn_W_fx', 'L0_ffn_b_fx', 'L0_ffn_W_x', 'L0_ffn_b_x', 'L0_ffn_W_slice', 'L0_ffn_b_slice',
        'L0_ffn_W_q', 'L0_ffn_W_k', 'L0_ffn_W_v', 'L0_ffn_W_out', 'L0_ffn_b_out', 'L0_ffn_temperature']


def kernel(**inputs):
    import numpy as np
    import concourse.bacc as bacc
    from concourse.bass_utils import run_bass_kernel_spmd as run

    nc = bacc.Bacc("TRN2", target_bir_lowering=False, num_devices=1)
    arrays = {f"{n}_in": np.ascontiguousarray(inputs[n]) for n in _INS}
    args = [nc.dram_tensor(n, a.shape, mybir.dt.from_np(a.dtype), kind="ExternalInput").ap()
            for n, a in arrays.items()]
    out = nc.dram_tensor("result", inputs['x'].shape, F32, kind="ExternalOutput").ap()
    build(nc, *args, out)
    return run(nc, [arrays], core_ids=[0]).results[0]["result"]
```
